# Optimizing a Trainium2 kernel written in Bass

```python
import numpy as np
import jax
import jax.numpy as jnp

def _softmax(x, axis=-1):
    return jax.nn.softmax(x, axis=axis)

def _gelu(x):
    return jax.nn.gelu(x, approximate=True)

def _silu(x):
    return jax.nn.silu(x)

def _sigmoid(x):
    return jax.nn.sigmoid(x)

def _layernorm(x, axis=-1, eps=1e-05):
    m = jnp.mean(x, axis=axis, keepdims=True)
    v = jnp.var(x, axis=axis, keepdims=True)
    return (x - m) / jnp.sqrt(v + eps)

def _scatter_add(tgt, idx, src, axis=0):
    return tgt.at[idx].add(src)

def _segment_sum(src, seg, n):
    return jax.ops.segment_sum(src, seg, n)
kernel_name = 'mk_macaron_d1_jaxref_r8_e3c20d'

def setup_inputs(seed: int=0):
    np.random.seed(seed)
    _w = jnp.asarray

    def _L0_attn_setup():
        import jax, jax.numpy as jnp
        import numpy as np

        def _rotate_every_two(x):
            x1 = x[..., ::2]
            x2 = x[..., 1::2]
            return jnp.stack((-x2, x1), axis=-1).reshape(x.shape)
        key = jax.random.key(seed)
        ks = jax.random.split(key, 6)
        B, S, D = (2, 256, 128)
        w = lambda k, shape: jax.random.normal(k, shape, dtype=jnp.float32) * 0.02
        return {'x': jax.random.normal(ks[0], (B, S, D), dtype=jnp.float32), 'Wq': w(ks[1], (D, D)), 'bq': jnp.zeros((D,), jnp.float32), 'Wk': w(ks[2], (D, D)), 'bk': jnp.zeros((D,), jnp.float32), 'Wv': w(ks[3], (D, 2 * D)), 'bv': jnp.zeros((2 * D,), jnp.float32), 'Wg': w(ks[4], (D, 2 * D)), 'bg': jnp.zeros((2 * D,), jnp.float32), 'Wo': w(ks[5], (2 * D, D)), 'bo': jnp.zeros((D,), jnp.float32)}
    _L0_attn_in = _L0_attn_setup()

    def _L0_ffn_setup():
        import jax, jax.numpy as jnp
        import numpy as np
        D_MODEL = 128
        D_FF = 512
        N_EXPERTS = 8
        TOP_K = 2

        def _ffn(x, w1, b1, w2, b2):
            h = jax.nn.gelu(x @ w1.T + b1)
            return h @ w2.T + b2
        key = jax.random.key(seed)
        ks = jax.random.split(key, 12)
        s = 0.02
        x = jax.random.normal(ks[0], (4, 256, D_MODEL), dtype=jnp.float32)
        shared_w1 = jax.random.normal(ks[1], (D_FF, D_MODEL), dtype=jnp.float32) * s
        shared_b1 = jnp.zeros((D_FF,), dtype=jnp.float32)
        shared_w2 = jax.random.normal(ks[2], (D_MODEL, D_FF), dtype=jnp.float32) * s
        shared_b2 = jnp.zeros((D_MODEL,), dtype=jnp.float32)
        router_w = jax.random.normal(ks[3], (N_EXPERTS, D_MODEL), dtype=jnp.float32) * s
        router_b = jnp.zeros((N_EXPERTS,), dtype=jnp.float32)
        spec_w1 = jax.random.normal(ks[4], (N_EXPERTS, D_FF, D_MODEL), dtype=jnp.float32) * s
        spec_b1 = jnp.zeros((N_EXPERTS, D_FF), dtype=jnp.float32)
        spec_w2 = jax.random.normal(ks[5], (N_EXPERTS, D_MODEL, D_FF), dtype=jnp.float32) * s
        spec_b2 = jnp.zeros((N_EXPERTS, D_MODEL), dtype=jnp.float32)
        return dict(x=x, shared_w1=shared_w1, shared_b1=shared_b1, shared_w2=shared_w2, shared_b2=shared_b2, router_w=router_w, router_b=router_b, spec_w1=spec_w1, spec_b1=spec_b1, spec_w2=spec_w2, spec_b2=spec_b2)
    _L0_ffn_in = _L0_ffn_setup()
    _d = {'L0_attn_x': _L0_attn_in['x'], 'L0_attn_Wq': _L0_attn_in['Wq'], 'L0_attn_bq': _L0_attn_in['bq'], 'L0_attn_Wk': _L0_attn_in['Wk'], 'L0_attn_bk': _L0_attn_in['bk'], 'L0_attn_Wv': _L0_attn_in['Wv'], 'L0_attn_bv': _L0_attn_in['bv'], 'L0_attn_Wg': _L0_attn_in['Wg'], 'L0_attn_bg': _L0_attn_in['bg'], 'L0_attn_Wo': _L0_attn_in['Wo'], 'L0_attn_bo': _L0_attn_in['bo'], 'L0_ffn_shared_w1': _L0_ffn_in['shared_w1'], 'L0_ffn_shared_b1': _L0_ffn_in['shared_b1'], 'L0_ffn_shared_w2': _L0_ffn_in['shared_w2'], 'L0_ffn_shared_b2': _L0_ffn_in['shared_b2'], 'L0_ffn_router_w': _L0_ffn_in['router_w'], 'L0_ffn_router_b': _L0_ffn_in['router_b'], 'L0_ffn_spec_w1': _L0_ffn_in['spec_w1'], 'L0_ffn_spec_b1': _L0_ffn_in['spec_b1'], 'L0_ffn_spec_w2': _L0_ffn_in['spec_w2'], 'L0_ffn_spec_b2': _L0_ffn_in['spec_b2']}
    _x0 = _d['L0_attn_x']
    _d['L0_attn_x'] = jax.random.normal(jax.random.fold_in(jax.random.key(seed), 1), (16, 256, 128), dtype=_x0.dtype)
    del _x0
    return _d

def reference(L0_attn_x, L0_attn_Wq, L0_attn_bq, L0_attn_Wk, L0_attn_bk, L0_attn_Wv, L0_attn_bv, L0_attn_Wg, L0_attn_bg, L0_attn_Wo, L0_attn_bo, L0_ffn_shared_w1, L0_ffn_shared_b1, L0_ffn_shared_w2, L0_ffn_shared_b2, L0_ffn_router_w, L0_ffn_router_b, L0_ffn_spec_w1, L0_ffn_spec_b1, L0_ffn_spec_w2, L0_ffn_spec_b2):

    def _L0_attn_ref(x, Wq, bq, Wk, bk, Wv, bv, Wg, bg, Wo, bo):
        import jax, jax.numpy as jnp
        import numpy as np

        def _rotate_every_two(x):
            x1 = x[..., ::2]
            x2 = x[..., 1::2]
            return jnp.stack((-x2, x1), axis=-1).reshape(x.shape)
        B, S, D = x.shape
        H = 16
        key_dim = D // H
        head_dim = 2 * D // H
        scaling = key_dim ** (-0.5)
        angle = 1.0 / 10000.0 ** jnp.linspace(0.0, 1.0, key_dim // 2)
        angle = jnp.repeat(angle, 2).astype(jnp.float32)
        decay = jnp.log(1.0 - 2.0 ** (-5.0 - jnp.arange(H, dtype=jnp.float32)))
        idx = jnp.arange(S, dtype=jnp.float32)
        sin = jnp.sin(idx[:, None] * angle[None, :])
        cos = jnp.cos(idx[:, None] * angle[None, :])
        diff = idx[:, None] - idx[None, :]
        mask = jnp.where(diff >= 0, jnp.exp(decay[:, None, None] * diff), 0.0)
        mask = mask / jnp.sqrt(mask.sum(-1, keepdims=True))
        q = (x @ Wq + bq).reshape(B, S, H, key_dim).transpose(0, 2, 1, 3)
        k = ((x @ Wk + bk) * scaling).reshape(B, S, H, key_dim).transpose(0, 2, 1, 3)
        v = x @ Wv + bv
        g = x @ Wg + bg
        qr = q * cos + _rotate_every_two(q) * sin
        kr = k * cos + _rotate_every_two(k) * sin
        vr = v.reshape(B, S, H, head_dim).transpose(0, 2, 1, 3)
        qk = jnp.einsum('bhsd,bhtd->bhst', qr, kr) * mask
        denom = jnp.clip(jnp.abs(jax.lax.stop_gradient(qk).sum(-1, keepdims=True)), 1.0, None)
        qk = qk / denom
        out = jnp.einsum('bhst,bhtd->bhsd', qk, vr).transpose(0, 2, 1, 3)
        mu = out.mean(-1, keepdims=True)
        var = ((out - mu) ** 2).mean(-1, keepdims=True)
        out = (out - mu) / jnp.sqrt(var + 1e-05)
        out = out.reshape(B, S, H * head_dim)
        out = jax.nn.silu(g) * out
        return out @ Wo + bo

    def _L0_ffn_ref(x, shared_w1, shared_b1, shared_w2, shared_b2, router_w, router_b, spec_w1, spec_b1, spec_w2, spec_b2):
        import jax, jax.numpy as jnp
        import numpy as np
        D_MODEL = 128
        D_FF = 512
        N_EXPERTS = 8
        TOP_K = 2

        def _ffn(x, w1, b1, w2, b2):
            h = jax.nn.gelu(x @ w1.T + b1)
            return h @ w2.T + b2
        B, T, D = x.shape
        xf = x.reshape(-1, D)
        U = xf.shape[0]
        logits = xf @ router_w.T + router_b
        routing = jax.nn.softmax(logits, axis=-1)
        sel_w, sel_idx = jax.lax.top_k(routing, TOP_K)
        sel_w = sel_w / sel_w.sum(axis=-1, keepdims=True)
        comb = jnp.zeros_like(routing).at[jnp.arange(U)[:, None], sel_idx].set(sel_w)
        shared_out = _ffn(xf, shared_w1, shared_b1, shared_w2, shared_b2)

        def body(acc, params):
            w1, b1, w2, b2, we = params
            return (acc + we[:, None] * _ffn(xf, w1, b1, w2, b2), None)
        acc0 = jnp.zeros_like(shared_out)
        acc, _ = jax.lax.scan(body, acc0, (spec_w1, spec_b1, spec_w2, spec_b2, comb.T))
        return (shared_out + acc).reshape(B, T, D)
    x = L0_attn_x
    x = x + 0.5 * _L0_ffn_ref(_layernorm(x, axis=-1), L0_ffn_shared_w1, L0_ffn_shared_b1, L0_ffn_shared_w2, L0_ffn_shared_b2, L0_ffn_router_w, L0_ffn_router_b, L0_ffn_spec_w1, L0_ffn_spec_b1, L0_ffn_spec_w2, L0_ffn_spec_b2)
    x = x + _L0_attn_ref(_layernorm(x, axis=-1), L0_attn_Wq, L0_attn_bq, L0_attn_Wk, L0_attn_bk, L0_attn_Wv, L0_attn_bv, L0_attn_Wg, L0_attn_bg, L0_attn_Wo, L0_attn_bo)
    x = x + 0.5 * _L0_ffn_ref(_layernorm(x, axis=-1), L0_ffn_shared_w1, L0_ffn_shared_b1, L0_ffn_shared_w2, L0_ffn_shared_b2, L0_ffn_router_w, L0_ffn_router_b, L0_ffn_spec_w1, L0_ffn_spec_b1, L0_ffn_spec_w2, L0_ffn_spec_b2)
    return x

_drawn_inputs = setup_inputs


def setup_inputs(seed=0):
    import zlib

    import numpy as np

    out = dict(_drawn_inputs(seed))
    spreads = {'L0_attn_bq': (0.0, 0.445),
     'L0_attn_bk': (0.0, 0.297),
     'L0_attn_bv': (0.0, 0.301),
     'L0_attn_bg': (0.0, 0.496),
     'L0_attn_bo': (0.0, 0.1),
     'L0_ffn_shared_b1': (0.0, 0.339),
     'L0_ffn_shared_b2': (0.0, 0.1),
     'L0_ffn_router_b': (0.0, 0.1),
     'L0_ffn_spec_b1': (0.0, 0.449),
     'L0_ffn_spec_b2': (0.0, 0.1)}
    factors = {}
    for name, (base, spread) in spreads.items():
        noise = np.random.default_rng([zlib.crc32(name.encode()), seed]).standard_normal(out[name].shape)
        drawn = base * np.exp(spread * noise) if base else spread * noise
        out[name] = jnp.asarray(drawn.astype(out[name].dtype))
    for name, factor in factors.items():
        out[name] = (out[name] * factor).astype(out[name].dtype)
    return out
```

```python
from contextlib import ExitStack

import concourse.bass as bass
from concourse import mybir

F32, F32R, I32 = mybir.dt.float32, mybir.dt.float32r, mybir.dt.int32
ALU, ACT, AX = mybir.AluOpType, mybir.ActivationFunctionType, mybir.AxisListType

P = 128
BATCH, SEQ, D = 16, 256, 128
TOKENS = BATCH * SEQ
TILES = TOKENS // P
FF, EXPERTS, TOP = 512, 8, 2
CHUNKS = FF // P
UNIT = 512
UT = UNIT // P
SHARED_UNITS = TOKENS // UNIT
ROUTED_UNITS = (TOP * TOKENS + EXPERTS * (UNIT - 1)) // UNIT
UNITS = SHARED_UNITS + ROUTED_UNITS
ROW = D + 2
DST_ROWS = TOKENS + UNIT
W_COLS = 2 * FF + CHUNKS + 1
HEADS, KD, VD = 16, 8, 16
V1 = VD + 1
EPS = 1e-5
C_ID, C_REV, C_STEP, C_UNIT, C_HEAD = 0, TILES, TILES + EXPERTS, TILES + 2 * EXPERTS, TILES + 2 * EXPERTS + 32
C_COLS = C_HEAD + 4


def wait_past(eng, sem, value):
    if not isinstance(value, int) or value > 0:
        eng.wait_ge(sem, value)


def release(nc, sems):
    nc.clear_and_free_semaphores(sems)
    nc.all_engine_barrier()


class Chain:

    def __init__(self, eng, sem):
        self.eng, self.sem, self.count = eng, sem, 0

    def then(self, instruction):
        self.count += 1
        instruction.then_inc(self.sem, 1)
        self.eng.wait_ge(self.sem, self.count)


def three_passes(pe, out, w_hi, w_lo, x_hi, x_lo, start=True, stop=True):
    pe.matmul(out, w_hi, x_hi, start=start, stop=False)
    pe.matmul(out, w_hi, x_lo, start=False, stop=False)
    return pe.matmul(out, w_lo, x_hi, start=False, stop=stop)


def layernorm_stats(dve, act_sqrt, chain, x, m):
    with dve.Fori(0, TILES // 4) as block:
        for j in range(4):
            last = dve.bn_stats(m["stats"][:, bass.ds(block * 4 + j, 1), :].rearrange("p t s -> p (t s)"),
                                x[:, bass.ds(block * 4 + j, 1), :].rearrange("p t d -> p (t d)"))
        last.then_inc(m["stats_done"], 1)
    dve.wait_ge(m["stats_done"], TILES // 4)
    even_mean, even_cv, odd_mean, odd_cv = (m["stats"][:, :, k] for k in (1, 2, 4, 5))
    dve.tensor_tensor(m["diff"][:, :], even_mean, odd_mean, ALU.subtract)
    dve.tensor_tensor(m["mean"][:, :], even_mean, odd_mean, ALU.add)
    chain.then(dve.tensor_tensor(m["var"][:, :], even_cv, odd_cv, ALU.add))
    chain.then(dve.tensor_tensor(m["diff"][:, :], m["diff"][:, :], m["diff"][:, :], ALU.mult))
    chain.then(dve.scalar_tensor_tensor(out=m["var"][:, :], in0=m["var"][:, :], scalar=4.0 / D, in1=m["diff"][:, :],
                                        op0=ALU.mult, op1=ALU.add))
    dve.tensor_scalar(m["mean"][:, :], m["mean"][:, :], 0.5, None, ALU.mult)
    dve.tensor_scalar(m["var"][:, :], m["var"][:, :], 0.25, EPS, ALU.mult, ALU.add).then_inc(m["var_done"], 1)
    dve.wait_ge(act_sqrt, 1)
    chain.then(dve.reciprocal(m["rstd"][:, :], m["root"][:, :]))
    chain.then(dve.tensor_tensor(m["diff"][:, :], m["rstd"][:, :], m["rstd"][:, :], ALU.mult))
    chain.then(dve.scalar_tensor_tensor(out=m["diff"][:, :], in0=m["diff"][:, :], scalar=-0.5, in1=m["var"][:, :],
                                        op0=ALU.mult, op1=ALU.mult))
    chain.then(dve.scalar_tensor_tensor(out=m["rstd"][:, :], in0=m["diff"][:, :], scalar=1.5, in1=m["rstd"][:, :],
                                        op0=ALU.add, op1=ALU.mult))


def normalise(dve, out, x, tile, m):
    return dve.tensor_scalar(out, x[:, bass.ds(tile, 1), :].rearrange("p t d -> p (t d)"),
                             m["mean"][:, bass.ds(tile, 1)], m["rstd"][:, bass.ds(tile, 1)], ALU.subtract, ALU.mult)


def run_steps(eng, step):
    a, b = 4, SHARED_UNITS - 2
    c = SHARED_UNITS + 4
    d = c + (UNITS - 1 - c) // 2 * 2
    for u in range(a):
        step(u, u)
    with eng.Fori(a // 2, b // 2) as pair:
        for j in range(2):
            step(pair * 2 + j, a + j)
    for u in range(b, c):
        step(u, u)
    with eng.Fori(c // 2, d // 2) as pair:
        for j in range(2):
            step(pair * 2 + j, c + j)
    for u in range(d, UNITS + 2):
        step(u, u)


def moe(nc, t, f, x_rows, dst):
    scattered = t["scattered"][f]
    with ExitStack() as ctx:
        sems = []

        def sem(name):
            sems.append(nc.alloc_semaphore(f"m{f}_{name}"))
            return sems[-1]

        def sb(name, shape, dt=F32):
            return ctx.enter_context(nc.sbuf_tensor(f"m{f}_{name}", shape, dt))

        bank = [ctx.enter_context(nc.psum_tensor(f"m{f}_bank{i}", [P, UNIT], F32)) for i in range(8)]
        up_bank, down_bank, y_bank, x_bank = bank[0:4], bank[4:6], bank[6], bank[7]

        m = dict(stats=sb("stats", [P, TILES, 6]), mean=sb("mean", [P, TILES]), var=sb("var", [P, TILES]),
                            diff=sb("diff", [P, TILES]), root=sb("root", [P, TILES]), rstd=sb("rstd", [P, TILES]),
                            stats_done=sem("stats_done"), var_done=sem("var_done"))
        xn = [sb(f"xn{p}", [P, UT, D]) for p in range(2)]
        x_t = [sb(f"x_t{p}", [P, UNIT]) for p in range(2)]
        x_t_all = sb("x_t_all", [P, SHARED_UNITS, UNIT])
        rows_out = sb("rows_out", [P, TILES, ROW])
        logits = sb("logits", [P, TILES, EXPERTS])
        prob = sb("prob", [P, TILES, EXPERTS])
        rest = sb("rest", [P, TILES, EXPERTS])
        score = sb("score", [P, TILES, EXPERTS])
        chosen = [sb(f"chosen{k}", [P, TILES, EXPERTS]) for k in range(TOP)]
        both = sb("both", [P, TILES, EXPERTS], F32R)
        best = sb("best", [P, TILES])
        top = [sb(f"top{k}", [P, TILES]) for k in range(TOP)]
        gate = [sb(f"gate{k}", [P, TILES]) for k in range(TOP)]
        totals = sb("totals", [P, TILES, EXPERTS])
        running = sb("running", [P, TILES, EXPERTS])
        units_of = sb("units_of", [P, EXPERTS])
        end_of = sb("end_of", [P, EXPERTS])
        base_of = sb("base_of", [P, EXPERTS])
        over = sb("over", [P, EXPERTS, EXPERTS])
        passed = sb("passed", [P, ROUTED_UNITS, EXPERTS - 1])
        expert_f = sb("expert_f", [P, ROUTED_UNITS])
        expert_of = sb("expert_of", [P, ROUTED_UNITS], I32)
        place_f = [sb(f"place_f{k}", [P, TILES]) for k in range(TOP)]
        place = [sb(f"place{k}", [P, TILES], I32) for k in range(TOP)]
        w_raw = [sb(f"w_raw{p}", [P, W_COLS]) for p in range(2)]
        w_hi = [sb(f"w_hi{p}", [P, 2, FF], F32R) for p in range(2)]
        w_lo = [sb(f"w_lo{p}", [P, 2, FF], F32R) for p in range(2)]
        sh_raw, sh_hi, sh_lo = sb("sh_raw", [P, W_COLS]), sb("sh_hi", [P, 2, FF], F32R), sb("sh_lo", [P, 2, FF], F32R)
        bias_of = sb("bias_of", [P, ROUTED_UNITS, CHUNKS + 1])
        tail_of = sb("tail_of", [P, ROUTED_UNITS, UT, 2])
        rows = [sb(f"rows{p}", [P, UT, ROW]) for p in range(2)]
        x_hi = [sb(f"x_hi{p}", [P, UNIT], F32R) for p in range(2)]
        x_lo = [sb(f"x_lo{p}", [P, UNIT], F32R) for p in range(2)]
        h = sb("h", [P, CHUNKS, UNIT])
        h_hi = sb("h_hi", [P, 2, CHUNKS, UNIT], F32R)
        h_lo = sb("h_lo", [P, 2, CHUNKS, UNIT], F32R)
        y_t = [sb(f"y_t{p}", [P, UNIT]) for p in range(2)]
        y = [sb(f"y{p}", [P, UT, D]) for p in range(2)]
        number = [sb(f"number{p}", [P, UT], I32) for p in range(2)]
        turn = sb("turn", [1, 1 + ROUTED_UNITS])
        router_w = sb("router_w", [P, EXPERTS])
        router_b = sb("router_b", [P, EXPERTS])
        earlier = sb("earlier", [P, P], F32R)
        ones = sb("ones", [P, P], F32R)

        s = {n: sem(n) for n in (
            "params", "casts", "rooted", "chain", "act_chain", "xn_done", "xn_turned", "xt_out", "xt_kept", "logit_done",
            "logit_kept", "row_kept", "shifted", "exped", "both_done", "prefixed", "gates_done", "places_done",
            "experts_done", "id_done", "gate2_done", "scatter0", "scatter1", "sh_loaded", "sh_hi", "sh_split",
            "x_turned", "x_high", "x_split", "w1_high", "w1_split", "w2_high", "w2_split", "up_done", "gelu_done",
            "h_high", "h_split", "down_done", "yt_done", "y_turned", "y_done", "tail_kept", "bias_kept", "y_added", "turn_set")}
        w_loaded = [sem(f"w_loaded{p}") for p in range(2)]
        rows_loaded = [sem(f"rows_loaded{p}") for p in range(2)]
        y_stored = [sem(f"y_stored{p}") for p in range(2)]

        ctx.callback(release, nc, sems)
        block = ctx.enter_context(nc.Block())

        @block.sync
        def _(sp):
            if f == 0:
                for q in range(4):
                    n = TILES // 4
                    sp.dma_start(t["x"][:, q * n:q * n + n, :], x_rows[q * n * P:(q + 1) * n * P, :]
                                 .rearrange("(t p) d -> p t d", p=P)).then_inc(t["x_loaded"], 16)
            sp.dma_start(router_w[:, :], t["router_w"]).then_inc(s["params"], 16)
            sp.dma_start(router_b[:, :], t["router_b"]).then_inc(s["params"], 16)
            sp.dma_start(sh_raw[:, :], t["experts"][EXPERTS]).then_inc(s["sh_loaded"], 16)

            def load_weights(r, p, expert):
                wait_past(sp, s["bias_kept"], r - 1)
                wait_past(sp, s["w2_split"], r - 1)
                sp.dma_start(w_raw[p][:, :], t["experts"][bass.ds(expert, 1), :, :].rearrange("e p c -> (e p) c")
                             ).then_inc(w_loaded[p], 16)

            def load_rows(r, p):
                wait_past(sp, s["tail_kept"], r - 1)
                wait_past(sp, s["x_turned"], r - 1)
                sp.dma_start(rows[p][:, :, :], scattered[bass.ds(r * UNIT, UNIT), :]
                             .rearrange("(t p) c -> p t c", p=P)).then_inc(rows_loaded[p], 16)

            def expert(r):
                return sp.value_load(expert_of[0:1, bass.ds(r, 1)], min_val=0, max_val=EXPERTS - 1)

            sp.wait_ge(s["experts_done"], 1)
            for r in range(2):
                load_weights(r, r % 2, expert(r))

            sp.wait_ge(s["scatter0"], 16 * TILES)
            sp.wait_ge(s["scatter1"], 16 * TILES)
            for r in range(2):
                load_rows(r, r)
            with sp.Fori(1, ROUTED_UNITS // 2) as pair:
                for p in range(2):
                    e = expert(pair * 2 + p)
                    load_weights(pair * 2 + p, p, e)
                    load_rows(pair * 2 + p, p)
            for r in range(ROUTED_UNITS // 2 * 2, ROUTED_UNITS):
                load_weights(r, r % 2, expert(r))
                load_rows(r, r % 2)
            sp.wait_ge(s["y_added"], 16 * UT * ROUTED_UNITS)
            sp.wait_ge(y_stored[0], 16 * (SHARED_UNITS // 2))
            sp.wait_ge(y_stored[1], 16 * (SHARED_UNITS // 2))

        @block.gpsimd
        def _(pool):
            def keep_rows(b, p):
                pool.wait_ge(s["xn_done"], b + 1)
                pool.tensor_copy(rows_out[:, bass.ds(b * UT, UT), 0:D], xn[p][:, :, :]).then_inc(s["row_kept"], 1)

            with pool.Fori(0, SHARED_UNITS // 2) as pair:
                for p in range(2):
                    keep_rows(pair * 2 + p, p)
            pool.wait_ge(s["row_kept"], SHARED_UNITS)
            pool.wait_ge(s["id_done"], 1)
            pool.wait_ge(s["gates_done"], 1)
            pool.wait_ge(s["places_done"], 1)
            pool.wait_ge(t["filled"][f], 16 * (UT + 1))
            for tile in range(TILES):
                pool.indirect_dma_start(scattered, bass.IndirectOffsetOnAxis(ap=place[0][:, tile:tile + 1], axis=0),
                                        rows_out[:, tile, :], None).then_inc(s["scatter0"], 16)
            pool.wait_ge(s["scatter0"], 16 * TILES)
            pool.tensor_copy(rows_out[:, :, D], gate[1][:, :]).then_inc(s["gate2_done"], 1)
            pool.wait_ge(s["gate2_done"], 1)
            for tile in range(TILES):
                pool.indirect_dma_start(scattered, bass.IndirectOffsetOnAxis(ap=place[1][:, tile:tile + 1], axis=0),
                                        rows_out[:, tile, :], None).then_inc(s["scatter1"], 16)

            def add_rows(r, p):
                pool.wait_ge(s["y_done"], r + SHARED_UNITS + 1)
                wait_past(pool, s["y_added"], r * (16 * UT))
                pool.tensor_tensor(turn[:, bass.ds(r + 1, 1)], turn[:, 0:1], turn[:, 0:1], ALU.add)
                for j in range(UT):
                    pool.indirect_dma_start(dst, bass.IndirectOffsetOnAxis(ap=number[p][:, j:j + 1], axis=0),
                                            y[p][:, j, :], None, compute_op=ALU.add).then_inc(s["y_added"], 16)

            pool.wait_ge(y_stored[0], 16 * (SHARED_UNITS // 2))
            pool.wait_ge(y_stored[1], 16 * (SHARED_UNITS // 2))
            pool.memset(turn[:, :], 0.0).then_inc(s["turn_set"], 1)
            pool.wait_ge(s["turn_set"], 1)
            add_rows(0, 0)
            add_rows(1, 1)
            with pool.Fori(1, ROUTED_UNITS // 2) as pair:
                for p in range(2):
                    add_rows(pair * 2 + p, p)
            for r in range(ROUTED_UNITS // 2 * 2, ROUTED_UNITS):
                add_rows(r, r % 2)

        @block.tensor
        def _(pe):
            pe.wait_ge(s["params"], 32)

            def turn_block(b, p):
                pe.wait_ge(s["xn_done"], b + 1)
                wait_past(pe, s["xt_kept"], b - 1)
                for j in range(UT):
                    last = pe.transpose(up_bank[p][:, j * P:(j + 1) * P], xn[p][:, j, :], t["ident"][:, :])
                last.then_inc(s["xn_turned"], 1)

            def route_block(b, p):
                pe.wait_ge(s["xt_out"], b + 1)
                wait_past(pe, s["logit_kept"], b - 1)
                for j in range(UT):
                    last = pe.matmul(up_bank[2 + p][:, j * EXPERTS:(j + 1) * EXPERTS], x_t[p][:, j * P:(j + 1) * P],
                                     router_w[:, :], start=True, stop=True)
                last.then_inc(s["logit_done"], 1)

            turn_block(0, 0)
            turn_block(1, 1)
            route_block(0, 0)
            with pe.Fori(1, SHARED_UNITS // 2) as pair:
                turn_block(pair * 2, 0)
                route_block(pair * 2 - 1, 1)
                turn_block(pair * 2 + 1, 1)
                route_block(pair * 2, 0)
            route_block(SHARED_UNITS - 1, 1)

            pe.wait_ge(s["both_done"], 1)
            flat = both[:, :, :].rearrange("p t e -> p (t e)")
            pe.matmul(down_bank[0][:, 0:TILES * EXPERTS], earlier[:, :], flat, start=True, stop=True)
            pe.matmul(down_bank[1][:, 0:TILES * EXPERTS], ones[:, :], flat, start=True, stop=True
                      ).then_inc(s["prefixed"], 1)

            def step(u, like):
                p, q = like % 2, (like + 1) % 2
                up, down, turn = like < UNITS, 1 <= like <= UNITS, 2 <= like
                hi, lo = (sh_hi, sh_lo) if like < SHARED_UNITS else (w_hi[p], w_lo[p])
                hi1, lo1 = (sh_hi, sh_lo) if like - 1 < SHARED_UNITS else (w_hi[q], w_lo[q])
                for c in range(CHUNKS):
                    cols = slice(c * P, (c + 1) * P)
                    if up:
                        if c == 0:
                            pe.wait_ge(s["x_split"], u + 1)
                            if like < SHARED_UNITS:
                                pe.wait_ge(s["sh_split"], 1)
                            else:
                                pe.wait_ge(s["w1_split"], u - SHARED_UNITS + 1)
                        if like == 0:
                            pe.wait_ge(s["logit_kept"], SHARED_UNITS)
                        wait_past(pe, s["gelu_done"], (u - 1) * CHUNKS + c + 1)
                        three_passes(pe, up_bank[c][:, :], hi[:, 0, cols], lo[:, 0, cols], x_hi[p][:, :], x_lo[p][:, :]
                                     ).then_inc(s["up_done"], 1)
                    if down:
                        if c == 0:
                            if like - 1 >= SHARED_UNITS:
                                pe.wait_ge(s["w2_split"], u - SHARED_UNITS)
                            wait_past(pe, s["yt_done"], u - 2)
                            if like - 1 < 2:
                                pe.wait_ge(s["places_done"], 1)
                        pe.wait_ge(s["h_split"], (u - 1) * CHUNKS + c + 1)
                        last = three_passes(pe, down_bank[q][:, :], hi1[:, 1, cols], lo1[:, 1, cols],
                                            h_hi[:, q, c, :], h_lo[:, q, c, :], start=c == 0, stop=c == CHUNKS - 1)
                        if c == CHUNKS - 1:
                            last.then_inc(s["down_done"], 1)
                    if c == 0 and SHARED_UNITS <= like + 1 < UNITS:
                        r = u + 1 - SHARED_UNITS
                        pe.wait_ge(rows_loaded[q], (r - q) * 8 + 16)
                        pe.wait_ge(s["x_split"], u + 1)
                        for j in range(UT):
                            last = pe.transpose(x_bank[:, j * P:(j + 1) * P], rows[q][:, j, 0:D], t["ident"][:, :])
                        last.then_inc(s["x_turned"], 1)
                    if c == 1 and turn:
                        pe.wait_ge(s["yt_done"], u - 1)
                        wait_past(pe, s["y_done"], u - 2)
                        for j in range(UT):
                            last = pe.transpose(y_bank[:, j * P:(j + 1) * P], y_t[p][:, j * P:(j + 1) * P], t["ident"][:, :])
                        last.then_inc(s["y_turned"], 1)

            run_steps(pe, step)

        @block.scalar
        def _(act):
            act.wait_ge(m["var_done"], 1)
            act.activation(m["root"][:, :], m["var"][:, :], ACT.Sqrt).then_inc(s["rooted"], 1)

            def evacuate(b, p):
                act.wait_ge(s["xn_turned"], b + 1)
                wait_past(act, s["logit_done"], b - 1)
                act.copy(x_t[p][:, :], up_bank[p][:, :]).then_inc(s["xt_out"], 1)
                act.copy(x_t_all[:, bass.ds(b, 1), :].rearrange("p b n -> p (b n)"), up_bank[p][:, :]
                         ).then_inc(s["xt_kept"], 1)

            evacuate(0, 0)
            evacuate(1, 1)
            with act.Fori(1, SHARED_UNITS // 2) as pair:
                for p in range(2):
                    evacuate(pair * 2 + p, p)
            act.wait_ge(s["sh_loaded"], 16)
            act.copy(sh_hi[:, :, :].rearrange("p a c -> p (a c)"), sh_raw[:, 0:2 * FF]).then_inc(s["sh_hi"], 1)
            act.wait_ge(s["shifted"], 1)
            act.activation(prob[:, :, :], logits[:, :, :], ACT.Exp).then_inc(s["exped"], 1)

            def high_x(u, like):
                p = like % 2
                if like < SHARED_UNITS:
                    act.wait_ge(s["xt_kept"], SHARED_UNITS)
                    source = x_t_all[:, bass.ds(u, 1), :].rearrange("p b n -> p (b n)")
                else:
                    act.wait_ge(s["x_turned"], u - SHARED_UNITS + 1)
                    source = x_bank[:, :]
                wait_past(act, s["up_done"], (u - 1) * CHUNKS)
                act.copy(x_hi[p][:, :], source).then_inc(s["x_high"], 1)

            def high_w(which, u, like, done):
                p, r = like % 2, u - SHARED_UNITS
                act.wait_ge(w_loaded[p], (r - p) * 8 + 16)
                if which == 0:
                    wait_past(act, s["up_done"], (u - 1) * CHUNKS)
                else:
                    wait_past(act, s["down_done"], u - 1)
                act.copy(w_hi[p][:, which, :], w_raw[p][:, which * FF:(which + 1) * FF]).then_inc(done, 1)

            high_x(0, 0)

            def step(u, like):
                p = like % 2
                if like >= 2:
                    act.wait_ge(s["down_done"], u - 1)
                    wait_past(act, s["y_turned"], u - 2)
                    if like - 2 < SHARED_UNITS:
                        bias = sh_raw[:, 2 * FF + CHUNKS:]
                    else:
                        act.wait_ge(s["bias_kept"], u - 2 - SHARED_UNITS + 1)
                        bias = bias_of[:, bass.ds(u - 2 - SHARED_UNITS, 1), CHUNKS:].rearrange("p u c -> p (u c)")
                    act.activation(y_t[p][:, :], down_bank[p][:, :], ACT.Identity, bias=bias).then_inc(s["yt_done"], 1)
                for c in range(CHUNKS):
                    if like < UNITS:
                        act.wait_ge(s["up_done"], u * CHUNKS + c + 1)
                        wait_past(act, s["h_split"], (u - 1) * CHUNKS + c + 1)
                        if like < SHARED_UNITS:
                            bias = sh_raw[:, 2 * FF + c:2 * FF + c + 1]
                        else:
                            if c == 0:
                                act.wait_ge(s["bias_kept"], u - SHARED_UNITS + 1)
                            bias = bias_of[:, bass.ds(u - SHARED_UNITS, 1), c:c + 1].rearrange("p u c -> p (u c)")
                        act.activation(h[:, c, :], up_bank[c][:, :], ACT.Gelu_apprx_tanh, bias=bias
                                       ).then_inc(s["gelu_done"], 1)
                    if c == 0 and SHARED_UNITS <= like + 1 < UNITS:
                        high_w(0, u + 1, like + 1, s["w1_high"])
                    if c == 1 and like + 1 < UNITS:
                        high_x(u + 1, like + 1)
                    if c == 2 and SHARED_UNITS <= like < UNITS:
                        high_w(1, u, like, s["w2_high"])
                    if c == 3 and 2 <= like < SHARED_UNITS + 2:
                        act.wait_ge(s["y_done"], u - 1)
                        act.dma_start(dst[bass.ds((u - 2) * UNIT, UNIT), :].rearrange("(t p) d -> p t d", p=P),
                                      y[p][:, :, :]).then_inc(y_stored[p], 16)

            run_steps(act, step)

        @block.vector
        def _(dve):
            chain = Chain(dve, s["chain"])
            dve.wait_ge(t["tables_loaded"], 16 * t["n_tables"])
            dve.tensor_copy(earlier[:, :], t["earlier"][:, :])
            dve.tensor_scalar(ones[:, :], t["earlier"][:, :], 0.0, 1.0, ALU.mult, ALU.add).then_inc(s["casts"], 1)
            dve.wait_ge(t["x_loaded"], 64)
            layernorm_stats(dve, s["rooted"], chain, t["x"], m)

            def normalise_block(b, p):
                wait_past(dve, s["xn_turned"], b - 1)
                wait_past(dve, s["row_kept"], b - 1)
                for j in range(UT):
                    last = normalise(dve, xn[p][:, j, :], t["x"], b * UT + j, m)
                last.then_inc(s["xn_done"], 1)

            def keep_logits(b, p):
                dve.wait_ge(s["logit_done"], b + 1)
                dve.tensor_tensor(logits[:, bass.ds(b * UT, UT), :],
                                  up_bank[2 + p][:, 0:UT * EXPERTS].rearrange("p (t e) -> p t e", e=EXPERTS),
                                  router_b[:, :].unsqueeze(1).to_broadcast([P, UT, EXPERTS]), ALU.add
                                  ).then_inc(s["logit_kept"], 1)

            dve.wait_ge(s["params"], 32)
            normalise_block(0, 0)
            normalise_block(1, 1)
            keep_logits(0, 0)
            with dve.Fori(1, SHARED_UNITS // 2) as pair:
                normalise_block(pair * 2, 0)
                keep_logits(pair * 2 - 1, 1)
                normalise_block(pair * 2 + 1, 1)
                keep_logits(pair * 2, 0)
            keep_logits(SHARED_UNITS - 1, 1)
            dve.wait_ge(s["logit_kept"], SHARED_UNITS)

            def per_expert(column):
                return column[:, :].unsqueeze(2).to_broadcast([P, TILES, EXPERTS])

            def per_token(row):
                return row.unsqueeze(1).to_broadcast([P, TILES, EXPERTS])

            chain.then(dve.tensor_reduce(best[:, :], logits[:, :, :], AX.X, ALU.max))
            dve.tensor_tensor(logits[:, :, :], logits[:, :, :], per_expert(best), ALU.subtract).then_inc(s["shifted"], 1)
            dve.wait_ge(s["exped"], 1)
            chain.then(dve.tensor_reduce(best[:, :], prob[:, :, :], AX.X, ALU.add))
            chain.then(dve.reciprocal(best[:, :], best[:, :]))
            chain.then(dve.tensor_tensor(prob[:, :, :], prob[:, :, :], per_expert(best), ALU.mult))
            rev = t["const"][:, C_REV:C_REV + EXPERTS]
            left = prob
            for k in range(TOP):
                chain.then(dve.tensor_reduce(top[k][:, :], left[:, :, :], AX.X, ALU.max))
                chain.then(dve.tensor_tensor(score[:, :, :], left[:, :, :], per_expert(top[k]), ALU.is_equal))
                chain.then(dve.tensor_tensor(score[:, :, :], score[:, :, :], per_token(rev), ALU.mult))
                chain.then(dve.tensor_reduce(best[:, :], score[:, :, :], AX.X, ALU.max))
                chain.then(dve.tensor_tensor(chosen[k][:, :, :], score[:, :, :], per_expert(best), ALU.is_equal))
                if k == 0:
                    chain.then(dve.scalar_tensor_tensor(out=rest[:, :, :], in0=chosen[0][:, :, :], scalar=-2.0,
                                                        in1=prob[:, :, :], op0=ALU.mult, op1=ALU.add))
                    left = rest
            dve.wait_ge(s["casts"], 1)
            dve.tensor_tensor(both[:, :, :], chosen[0][:, :, :], chosen[1][:, :, :], ALU.add).then_inc(s["both_done"], 1)
            chain.then(dve.tensor_tensor(best[:, :], top[0][:, :], top[1][:, :], ALU.add))
            chain.then(dve.reciprocal(best[:, :], best[:, :]))
            for k in range(TOP):
                chain.then(dve.scalar_tensor_tensor(out=gate[k][:, :], in0=top[k][:, :], scalar=0.5, in1=best[:, :],
                                                    op0=ALU.mult, op1=ALU.mult))
            dve.tensor_copy(rows_out[:, :, D + 1], t["const"][:, C_ID:C_ID + TILES]).then_inc(s["id_done"], 1)
            dve.tensor_copy(rows_out[:, :, D], gate[0][:, :]).then_inc(s["gates_done"], 1)
            dve.wait_ge(s["prefixed"], 1)
            chain.then(dve.tensor_copy(totals[:, :, :].rearrange("p t e -> p (t e)"), down_bank[1][:, 0:TILES * EXPERTS]))
            for e in range(EXPERTS):
                last = dve.tensor_tensor_scan(running[:, :, e], t["ones"][:, 0:TILES], totals[:, :, e], 0.0,
                                              ALU.mult, ALU.add)
            chain.then(last)
            steps = t["const"][:, C_STEP:C_STEP + EXPERTS]
            chain.then(dve.tensor_tensor(over[:, :, :],
                                         running[:, TILES - 1, :].unsqueeze(2).to_broadcast([P, EXPERTS, EXPERTS]),
                                         steps.unsqueeze(1).to_broadcast([P, EXPERTS, EXPERTS]), ALU.is_gt))
            chain.then(dve.tensor_reduce(units_of[:, :], over[:, :, :], AX.X, ALU.add))
            chain.then(dve.tensor_tensor_scan(end_of[:, :], t["ones"][:, 0:EXPERTS], units_of[:, :], 0.0, ALU.mult, ALU.add))
            chain.then(dve.tensor_tensor(base_of[:, :], end_of[:, :], units_of[:, :], ALU.subtract))
            chain.then(dve.tensor_scalar(base_of[:, :], base_of[:, :], float(UNIT), None, ALU.mult))
            chain.then(dve.tensor_tensor(
                passed[:, :, :], end_of[:, 0:EXPERTS - 1].unsqueeze(1).to_broadcast([P, ROUTED_UNITS, EXPERTS - 1]),
                t["const"][:, C_UNIT:C_UNIT + ROUTED_UNITS].unsqueeze(2).to_broadcast([P, ROUTED_UNITS, EXPERTS - 1]),
                ALU.is_le))
            chain.then(dve.tensor_reduce(expert_f[:, :], passed[:, :, :], AX.X, ALU.add))
            dve.tensor_copy(expert_of[:, :], expert_f[:, :]).then_inc(s["experts_done"], 1)
            chain.then(dve.tensor_tensor(running[:, :, :], running[:, :, :], totals[:, :, :], ALU.subtract))
            chain.then(dve.tensor_tensor(running[:, :, :], running[:, :, :], per_token(base_of[:, :]), ALU.add))
            chain.then(dve.tensor_tensor(running[:, :, :], running[:, :, :],
                                         down_bank[0][:, 0:TILES * EXPERTS].rearrange("p (t e) -> p t e", e=EXPERTS),
                                         ALU.add))
            for k in range(TOP):
                chain.then(dve.tensor_tensor(score[:, :, :], running[:, :, :], chosen[k][:, :, :], ALU.mult))
                chain.then(dve.tensor_reduce(place_f[k][:, :], score[:, :, :], AX.X, ALU.add))
                last = dve.tensor_copy(place[k][:, :], place_f[k][:, :])
            last.then_inc(s["places_done"], 1)

            dve.wait_ge(s["sh_hi"], 1)
            dve.tensor_tensor(sh_lo[:, :, :].rearrange("p a c -> p (a c)"), sh_raw[:, 0:2 * FF],
                              sh_hi[:, :, :].rearrange("p a c -> p (a c)").bitcast(F32), ALU.subtract).then_inc(s["sh_split"], 1)

            def low_x(u, like):
                p = like % 2
                dve.wait_ge(s["x_high"], u + 1)
                source = (x_t_all[:, bass.ds(u, 1), :].rearrange("p b n -> p (b n)") if like < SHARED_UNITS
                          else x_bank[:, :])
                dve.tensor_tensor(x_lo[p][:, :], source, x_hi[p][:, :].bitcast(F32), ALU.subtract).then_inc(s["x_split"], 1)
                if like >= SHARED_UNITS:
                    r = u - SHARED_UNITS
                    dve.wait_ge(rows_loaded[p], (r - p) * 8 + 16)
                    dve.tensor_scalar(tail_of[:, bass.ds(r, 1), :, :].rearrange("p u t c -> p (u t) c"),
                                      rows[p][:, :, D:ROW], 1.0, None, ALU.mult).then_inc(s["tail_kept"], 1)

            def low_w(which, u, like, high, done):
                p, r = like % 2, u - SHARED_UNITS
                dve.wait_ge(high, r + 1)
                if which == 0:
                    dve.tensor_scalar(bias_of[:, bass.ds(r, 1), :].rearrange("p u c -> p (u c)"),
                                      w_raw[p][:, 2 * FF:], 1.0, None, ALU.mult).then_inc(s["bias_kept"], 1)
                dve.tensor_tensor(w_lo[p][:, which, :], w_raw[p][:, which * FF:(which + 1) * FF],
                                  w_hi[p][:, which, :].bitcast(F32), ALU.subtract).then_inc(done, 1)

            low_x(0, 0)

            def step(u, like):
                p = like % 2
                for c in range(CHUNKS):
                    if like < UNITS:
                        n = u * CHUNKS + c + 1
                        dve.wait_ge(s["gelu_done"], n)
                        wait_past(dve, s["down_done"], u - 1)
                        dve.tensor_copy(h_hi[:, p, c, :], h[:, c, :]).then_inc(s["h_high"], 1)
                        dve.wait_ge(s["h_high"], n)
                        dve.tensor_tensor(h_lo[:, p, c, :], h[:, c, :], h_hi[:, p, c, :].bitcast(F32), ALU.subtract
                                          ).then_inc(s["h_split"], 1)
                    if c == 0 and SHARED_UNITS <= like + 1 < UNITS:
                        low_w(0, u + 1, like + 1, s["w1_high"], s["w1_split"])
                    if c == 1 and like + 1 < UNITS:
                        low_x(u + 1, like + 1)
                    if c == 2 and SHARED_UNITS <= like < UNITS:
                        low_w(1, u, like, s["w2_high"], s["w2_split"])
                    if c == 2 and like >= 2:
                        v, kind = u - 2, like - 2
                        dve.wait_ge(s["y_turned"], v + 1)
                        if kind < SHARED_UNITS + 2:
                            dve.wait_ge(y_stored[p], (v - p) * 8)
                        else:
                            dve.wait_ge(s["y_added"], (v - SHARED_UNITS - 1) * (16 * UT))
                        if kind < SHARED_UNITS:
                            dve.scalar_tensor_tensor(
                                out=y[p][:, :, :].rearrange("p t d -> p (t d)"), in0=y_bank[:, :], scalar=0.5,
                                in1=t["x"][:, bass.ds(v * UT, UT), :].rearrange("p t d -> p (t d)"),
                                op0=ALU.mult, op1=ALU.add).then_inc(s["y_done"], 1)
                        else:
                            r = v - SHARED_UNITS
                            dve.wait_ge(s["tail_kept"], r + 1)
                            dve.tensor_scalar(number[p][:, :], tail_of[:, bass.ds(r, 1), :, 1].rearrange("p u t -> p (u t)"),
                                              1.0, None, ALU.mult)
                            for j in range(UT):
                                last = dve.tensor_scalar(y[p][:, j, :], y_bank[:, j * P:(j + 1) * P],
                                                         tail_of[:, bass.ds(r, 1), j, 0:1].rearrange("p u c -> p (u c)"),
                                                         None, ALU.mult)
                            last.then_inc(s["y_done"], 1)

            run_steps(dve, step)


def run_batches(eng, step):
    for b in range(4):
        step(b, b)
    with eng.Fori(2, BATCH // 2 - 1) as pair:
        for j in range(2):
            step(pair * 2 + j, 4 + j)
    for b in range(BATCH - 2, BATCH + 2):
        step(b, b)


def own_columns(values, c):
    return values[:, c, :, :, :].rearrange("p h j v -> p h (j v)").rearrange("p h (k v) -> p h k v", v=VD)[:, :, 0:4:3, :]


def retention(nc, t, src):
    with ExitStack() as ctx:
        sems = []

        def sem(name):
            sems.append(nc.alloc_semaphore(f"r_{name}"))
            return sems[-1]

        def sb(name, shape, dt=F32):
            return ctx.enter_context(nc.sbuf_tensor(f"r_{name}", shape, dt))

        def psum(name, shape):
            return ctx.enter_context(nc.psum_tensor(f"r_{name}", shape, F32))

        CH = SEQ // P
        GROUPS = HEADS // 4
        W = 4 * D
        score_bank = [psum(f"score{i}", [P, 4, P]) for i in range(2)]
        turn_bank = psum("turn", [P, 512])
        qk_bank, heads_bank = psum("qk", [P, 512]), psum("heads", [P, CH, 2 * D])
        v_bank = psum("v", [P, 2, 2 * D])
        out_bank = [psum(f"out{c}", [P, 2, P]) for c in range(CH)]

        m = dict(stats=sb("stats", [P, TILES, 6]), mean=sb("mean", [P, TILES]), var=sb("var", [P, TILES]),
                            diff=sb("diff", [P, TILES]), root=sb("root", [P, TILES]), rstd=sb("rstd", [P, TILES]),
                            stats_done=sem("stats_done"), var_done=sem("var_done"))
        qk_raw, qk_hi, qk_lo = sb("qk_raw", [P, W]), sb("qk_hi", [P, W], F32R), sb("qk_lo", [P, W], F32R)
        vg_raw, vg_hi, vg_lo = sb("vg_raw", [P, W]), sb("vg_hi", [P, W], F32R), sb("vg_lo", [P, W], F32R)
        o_raw, o_hi, o_lo = sb("o_raw", [P, 2 * D]), sb("o_hi", [P, 2 * D], F32R), sb("o_lo", [P, 2 * D], F32R)
        vg_bias, o_bias, qk_bias = sb("vg_bias", [P, W]), sb("o_bias", [P, D]), sb("qk_bias", [P, 4])
        turns = sb("turns", [P, 4, SEQ])
        mask = sb("mask", [P, HEADS, P])
        q_decay, k_decay, own_head = sb("q_decay", [P, P]), sb("k_decay", [P, P]), sb("own_head", [P, HEADS, VD])
        decays, head_of = sb("decays", [P, SEQ]), sb("head_of", [P, HEADS])

        xn = [sb(f"xn{p}", [P, CH, D]) for p in range(2)]
        x_hi, x_lo = sb("x_hi", [P, SEQ], F32R), sb("x_lo", [P, SEQ], F32R)
        q_part, q_turn = sb("q_part", [P, SEQ]), sb("q_turn", [P, SEQ])
        k_part, k_turn = sb("k_part", [P, SEQ]), sb("k_turn", [P, SEQ])
        q_all = sb("q_all", [P, SEQ])
        keys = [sb(f"keys{p}", [P, SEQ]) for p in range(2)]
        spread = [sb(f"spread{p}", [P, 4, SEQ]) for p in range(2)]
        q_dec = [sb(f"q_dec{p}", [P, P]) for p in range(2)]
        values = [sb(f"values{p}", [P, CH, HEADS // 2, 2, 2 * VD]) for p in range(2)]
        key_sums, sum_terms = sb("key_sums", [P, SEQ]), sb("sum_terms", [P, SEQ])
        out_turned = sb("out_turned", [P, CH, 2, P])
        g_raw = [sb(f"g_raw{p}", [P, CH, 2 * D]) for p in range(2)]
        g_act = [sb(f"g_act{p}", [P, CH, 2 * D]) for p in range(2)]
        probs = sb("probs", [P, CH, HEADS, P])
        k_dec, state = sb("k_dec", [P, P]), sb("state", [P, HEADS, VD])
        heads = [sb(f"heads{p}", [P, CH * HEADS, VD]) for p in range(2)]
        squares = sb("squares", [P, CH * HEADS, VD])
        bounded, clipped, square_sum, o_var, power, o_rstd, factor = (
            sb(name, [P, CH * HEADS]) for name in ("bounded", "clipped", "square_sum", "o_var", "power", "o_rstd",
                                                   "factor"))
        inverse, inverse2 = ([sb(f"{name}{p}", [P, CH * HEADS]) for p in range(2)] for name in ("inverse", "inverse2"))
        normed = sb("normed", [P, CH * HEADS, VD])
        gated = sb("gated", [P, CH * HEADS, VD])
        y_hi, y_lo = sb("y_hi", [P, CH * 2 * P], F32R), sb("y_lo", [P, CH * 2 * P], F32R)
        x_plus = [sb(f"x_plus{p}", [P, CH, D]) for p in range(2)]
        value_mean = sb("value_mean", [P, 2, HEADS])

        s = {n: sem(n) for n in (
            "params", "rooted", "chain", "high", "split", "power_set", "zeros_set", "xn_done", "x_turned", "x_high",
            "x_split", "q_done", "k_done", "parts_done", "q_all_done", "keys_done", "spread_done", "q_dec_done",
            "v_done", "v_kept", "g_kept", "g_done", "scored", "masked", "k_turned", "k_dec_done", "state_done",
            "state_kept", "out0_done", "out_done", "out_kept", "heads_turned",
            "heads_kept", "key_sums_done", "sum_terms_done", "squared", "sum_bounded", "sum_clipped",
            "sum_inverted", "inverse_squared", "squares_summed", "var_scaled", "o_var_done", "rstd_done",
            "factor_done", "normed_done", "gated_done", "y_turned", "y_high", "y_split", "o_done", "x_plus_done",
            "added")}
        x_in = [sem(f"x_in{q}") for q in range(4)]

        ctx.callback(release, nc, sems)
        block = ctx.enter_context(nc.Block())
        a = t["a"]
        loads = ((qk_raw[:, :], a["w_qk"]), (vg_raw[:, :], a["w_vg"]), (o_raw[:, :], a["w_o"]),
                 (vg_bias[:, :], a["b_vg"]), (o_bias[:, :], a["b_o"]), (qk_bias[:, :], a["b_qk"]),
                 (turns[:, :, :], a["turns"]), (q_decay[:, :], a["q_decay"]), (k_decay[:, :], a["k_decay"]),
                 (own_head[:, :, :], a["own_head"]), (mask[:, :, :], a["mask"]),
                 (decays[:, :], a["decays"]), (head_of[:, :], a["head_of"]))
        n_params = 16 * len(loads)

        @block.sync
        def _(sp):
            n = TILES // 4
            for q in range(4):
                sp.dma_start(t["x"][:, q * n:q * n + n, :], src[q * n * P:(q + 1) * n * P, :]
                             .rearrange("(t p) d -> p t d", p=P)).then_inc(x_in[q], 16)
            for to, what in loads:
                sp.dma_start(to, what).then_inc(s["params"], 16)

        @block.gpsimd
        def _(pool):
            pool.memset(power[:, :], -0.5).then_inc(s["power_set"], 1)
            for p in range(2):
                last = pool.memset(values[p][:, :, :, :, :], 0.0)
            last.then_inc(s["zeros_set"], 1)
            pool.wait_ge(s["params"], n_params)
            pool.wait_ge(s["power_set"], 1)

            def step(b, like):
                p = like % 2
                if 2 <= like:
                    pool.wait_ge(s["o_var_done"], b - 1)
                    pool.tensor_tensor(o_rstd[:, :], o_var[:, :], power[:, :], ALU.pow).then_inc(s["rstd_done"], 1)
                    pool.wait_ge(s["rstd_done"], b - 1)
                    wait_past(pool, s["normed_done"], b - 2)
                    pool.tensor_tensor(factor[:, :], o_rstd[:, :], inverse[p][:, :], ALU.mult).then_inc(s["factor_done"], 1)
                    wait_past(pool, s["added"], b - 3)
                    pool.tensor_tensor(x_plus[p][:, :, :], t["x"][:, bass.ds((b - 2) * CH, CH), :],
                                       o_bias[:, :].unsqueeze(1).to_broadcast([P, CH, D]), ALU.add
                                       ).then_inc(s["x_plus_done"], 1)
                if like < BATCH:
                    pool.wait_ge(s["parts_done"], 2 * b + 2)
                    wait_past(pool, s["spread_done"], b)
                    wait_past(pool, s["q_dec_done"], b)
                    pool.tensor_tensor(q_all[:, :], q_part[:, :], q_turn[:, :], ALU.add).then_inc(s["q_all_done"], 1)
                    wait_past(pool, s["out_done"], b - 1)
                    pool.tensor_tensor(keys[p][:, :], k_part[:, :], k_turn[:, :], ALU.add).then_inc(s["keys_done"], 1)
                    pool.wait_ge(s["q_all_done"], b + 1)
                    pool.tensor_tensor(q_dec[p][:, :], q_all[:, P:SEQ], q_decay[:, :], ALU.mult
                                       ).then_inc(s["q_dec_done"], 1)
                    pool.wait_ge(s["key_sums_done"], b + 1)
                    wait_past(pool, s["k_turned"], b)
                    pool.tensor_tensor(sum_terms[:, :], q_all[:, :], key_sums[:, :], ALU.mult
                                       ).then_inc(s["sum_terms_done"], 1)

            run_batches(pool, step)

        @block.tensor
        def _(pe):
            pe.wait_ge(s["split"], 3)

            def turn_x(b, p):
                pe.wait_ge(s["xn_done"], b + 1)
                for c in range(CH):
                    last = pe.transpose(turn_bank[:, c * P:c * P + P], xn[p][:, c, :], t["ident"][:, :])
                last.then_inc(s["x_turned"], 1)

            turn_x(0, 0)

            def score(c, g, b, q):
                n = (b - 1) * (CH * GROUPS) + c * GROUPS + g
                wait_past(pe, s["masked"], n - 1)
                rows, cols = slice(32 * g, 32 * g + 32), slice(c * P, c * P + P)
                pe.matmul(score_bank[g % 2][:, :, :], keys[q][rows, cols], spread[q][rows, :, cols],
                          start=True, stop=True).then_inc(s["scored"], 1)

            def outputs(c, first, b, q):
                pe.wait_ge(s["masked"], (b - 1) * (CH * GROUPS) + c * GROUPS + first // 4 + 1)
                if c == 1 and first % 8 == 0:
                    pe.matmul(out_bank[1][:, first // 8, :], state[:, first:first + 8, :].rearrange("p h v -> p (h v)"),
                              q_dec[q][:, :], start=True, stop=False, skip_group_check=True)
                for h in range(first, first + 4):
                    quad, half = h // 2 % 4 * 32, h // 8
                    last = pe.matmul(out_bank[c][quad:quad + 32, half, :], values[q][:, c, h // 2, h % 2, :],
                                     probs[:, c, h, :], start=c == 0 and h % 2 == 0, stop=h % 2 == 1,
                                     skip_group_check=True)
                return last

            def turn_heads(c, b):
                pe.wait_ge(s["out_kept"], (b - 1) * CH + c + 1)
                wait_past(pe, s["heads_kept"], (b - 1) * CH + c)
                for half in range(2):
                    last = pe.transpose(heads_bank[:, c, half * P:half * P + P], out_turned[:, c, half, :],
                                        t["ident"][:, :])
                last.then_inc(s["heads_turned"], 1)

            def step(b, like):
                p, q = like % 2, (like + 1) % 2
                new, mid, old, ahead = like < BATCH, 1 <= like <= BATCH, 2 <= like, like + 1 < BATCH
                if mid:
                    pe.wait_ge(s["keys_done"], b)
                    if new:
                        pe.wait_ge(s["x_split"], b + 1)
                    pe.wait_ge(s["sum_terms_done"], b)
                    pe.transpose(turn_bank[:, 0:P], keys[q][:, 0:P], t["ident"][:, :])
                    for c in range(CH):
                        last = pe.matmul(turn_bank[:, P + c * HEADS:P + (c + 1) * HEADS], sum_terms[:, c * P:(c + 1) * P],
                                         head_of[:, :], start=True, stop=True)
                    last.then_inc(s["k_turned"], 1)
                    pe.wait_ge(s["spread_done"], b)
                    score(0, 0, b, q)
                    score(0, 1, b, q)
                if new:
                    pe.wait_ge(s["x_split"], b + 1)
                    wait_past(pe, s["parts_done"], 2 * b)
                    for k in range(2):
                        cols = slice(k * D, (k + 1) * D)
                        last = three_passes(pe, qk_bank[:, k * SEQ:(k + 1) * SEQ], qk_hi[:, cols], qk_lo[:, cols], x_hi[:, :], x_lo[:, :])
                    last.then_inc(s["q_done"], 1)
                if mid:
                    score(0, 2, b, q)
                    score(0, 3, b, q)
                    outputs(0, 0, b, q)
                    pe.wait_ge(s["k_dec_done"], b)
                    pe.wait_ge(s["v_kept"], CH * b)
                    if new:
                        pe.wait_ge(s["parts_done"], 2 * b + 1)
                    else:
                        pe.wait_ge(s["parts_done"], 2 * b)
                    pe.matmul(qk_bank[:, 0:HEADS * VD], k_dec[:, :], own_columns(values[q], 0),
                              start=True, stop=True).then_inc(s["state_done"], 1)
                    score(1, 0, b, q)
                if new:
                    pe.wait_ge(s["parts_done"], 2 * b + 1)
                    wait_past(pe, s["state_kept"], b)
                    for k in range(2):
                        cols = slice((2 + k) * D, (3 + k) * D)
                        last = three_passes(pe, qk_bank[:, k * SEQ:(k + 1) * SEQ], qk_hi[:, cols], qk_lo[:, cols], x_hi[:, :], x_lo[:, :])
                    last.then_inc(s["k_done"], 1)
                if mid:
                    outputs(0, 4, b, q)
                    score(1, 1, b, q)
                    outputs(0, 8, b, q)

                def values_and_gates(c):
                    wait_past(pe, s["g_kept"], CH * b + c)
                    if c == 0:
                        wait_past(pe, s["added"], b - 2)
                    cols = slice(c * P, c * P + P)
                    three_passes(pe, v_bank[:, :, :].rearrange("p c n -> p (c n)"), x_hi[:, cols], x_lo[:, cols],
                                 vg_hi[:, :], vg_lo[:, :]).then_inc(s["v_done"], 1)

                if new:
                    values_and_gates(0)
                if mid:
                    score(1, 2, b, q)
                    outputs(0, 12, b, q).then_inc(s["out0_done"], 1)
                    score(1, 3, b, q)
                if new:
                    values_and_gates(1)
                if mid:
                    turn_heads(0, b)
                if old:
                    pe.wait_ge(s["gated_done"], b - 1)
                    if mid:
                        pe.wait_ge(s["sum_clipped"], b)
                    for k in range(CH * 2):
                        last = pe.transpose(turn_bank[:, k * P:k * P + P],
                                            gated[:, :, :].rearrange("p h v -> p (h v)")[:, k * P:k * P + P],
                                            t["ident"][:, :])
                    last.then_inc(s["y_turned"], 1)
                if mid:
                    pe.wait_ge(s["state_kept"], b)
                    pe.wait_ge(s["q_dec_done"], b)
                    outputs(1, 0, b, q)
                if mid:
                    outputs(1, 4, b, q)
                    outputs(1, 8, b, q)
                if ahead:
                    if old:
                        pe.wait_ge(s["y_split"], b - 1)
                    elif mid:
                        pe.wait_ge(s["sum_clipped"], b)
                    else:
                        pe.wait_ge(s["x_split"], b + 1)
                    turn_x(b + 1, q)
                if mid:
                    outputs(1, 12, b, q).then_inc(s["out_done"], 1)
                if old:
                    pe.wait_ge(s["y_split"], b - 1)
                    if new:
                        pe.wait_ge(s["g_kept"], CH * (b + 1))
                    wait_past(pe, s["added"], b - 2)
                    for c in range(CH):
                        for half in range(2):
                            k = c * 2 + half
                            cols, w = slice(k * P, k * P + P), slice(half * D, half * D + D)
                            last = three_passes(pe, v_bank[:, 0, c * D:(c + 1) * D], y_hi[:, cols], y_lo[:, cols],
                                                o_hi[:, w], o_lo[:, w], start=half == 0, stop=half == 1)
                    last.then_inc(s["o_done"], 1)
                if mid:
                    turn_heads(1, b)

            run_batches(pe, step)

        @block.scalar
        def _(act):
            act.wait_ge(m["var_done"], 1)
            act.activation(m["root"][:, :], m["var"][:, :], ACT.Sqrt).then_inc(s["rooted"], 1)
            act.wait_ge(s["params"], n_params)
            act.copy(qk_hi[:, :], qk_raw[:, :]).then_inc(s["high"], 1)
            act.copy(o_hi[:, :], o_raw[:, :]).then_inc(s["high"], 1)

            def high_x(b):
                act.wait_ge(s["x_turned"], b + 1)
                wait_past(act, s["v_done"], CH * b)
                act.copy(x_hi[:, :], turn_bank[:, 0:SEQ]).then_inc(s["x_high"], 1)

            high_x(0)

            def keep_out(c, b):
                act.wait_ge(s["out_done" if c else "out0_done"], b)
                wait_past(act, s["heads_turned"], (b - 2) * CH + c + 1)
                act.copy(out_turned[:, c, :, :], out_bank[c][:, :, :]).then_inc(s["out_kept"], 1)

            def keep_heads(c, b, p):
                act.wait_ge(s["heads_turned"], (b - 1) * CH + c + 1)
                if c == 0:
                    wait_past(act, s["normed_done"], b - 2)
                act.copy(heads[p][:, c * HEADS:(c + 1) * HEADS, :].rearrange("p h v -> p (h v)"), heads_bank[:, c, :]
                         ).then_inc(s["heads_kept"], 1)

            def step(b, like):
                p, q = like % 2, (like + 1) % 2
                if 2 <= like:
                    keep_heads(1, b - 1, p)
                    act.wait_ge(s["heads_kept"], CH * (b - 1))
                    wait_past(act, s["squares_summed"], b - 2)
                    act.activation(squares[:, :, :], heads[p][:, :, :], ACT.Square).then_inc(s["squared"], 1)
                if 1 <= like <= BATCH:
                    keep_out(0, b)
                    keep_heads(0, b, q)
                if like >= 2:
                    act.wait_ge(s["y_turned"], b - 1)
                    wait_past(act, s["o_done"], b - 2)
                    act.copy(y_hi[:, :], turn_bank[:, :]).then_inc(s["y_high"], 1)
                if like < BATCH:
                    act.wait_ge(s["q_all_done"], b + 1)
                    wait_past(act, s["scored"], (b - 1) * (CH * GROUPS))
                    for j in range(4):
                        last = act.mul(spread[p][:, j, :], q_all[:, :], t["const"][:, C_HEAD + j:C_HEAD + j + 1])
                    last.then_inc(s["spread_done"], 1)
                if like + 1 < BATCH:
                    high_x(b + 1)
                if like < BATCH:
                    act.wait_ge(s["g_kept"], CH * (b + 1))
                    wait_past(act, s["gated_done"], b - 1)
                    act.activation(g_act[p][:, :, :], g_raw[p][:, :, :], ACT.Silu).then_inc(s["g_done"], 1)
                if 1 <= like <= BATCH:
                    keep_out(1, b)

            run_batches(act, step)

        @block.vector
        def _(dve):
            chain = Chain(dve, s["chain"])
            for q in range(4):
                dve.wait_ge(x_in[q], 16)
            layernorm_stats(dve, s["rooted"], chain, t["x"], m)
            dve.wait_ge(s["params"], n_params)
            per_head = [v[:, 0:2 * D].rearrange("p (h v) -> p h v", v=VD) for v in (vg_raw, vg_bias)]
            for k, part in enumerate(per_head):
                last = dve.tensor_reduce(value_mean[:, k, :], part, AX.X, ALU.add)
            chain.then(last)
            for k, part in enumerate(per_head):
                last = dve.scalar_tensor_tensor(out=part, in0=value_mean[:, k, :].unsqueeze(2).to_broadcast([P, HEADS, VD]),
                                                scalar=-1.0 / VD, in1=part, op0=ALU.mult, op1=ALU.add)
            chain.then(last)
            chain.then(dve.tensor_copy(vg_hi[:, :], vg_raw[:, :]))
            dve.wait_ge(s["high"], 2)
            for hi, lo, raw in ((qk_hi, qk_lo, qk_raw), (vg_hi, vg_lo, vg_raw), (o_hi, o_lo, o_raw)):
                dve.tensor_tensor(lo[:, :], raw[:, :], hi[:, :].bitcast(F32), ALU.subtract).then_inc(s["split"], 1)

            def normalise_batch(b, p):
                wait_past(dve, s["x_turned"], b - 1)
                for c in range(CH):
                    last = normalise(dve, xn[p][:, c, :], t["x"], b * CH + c, m)
                last.then_inc(s["xn_done"], 1)

            def low_x(b):
                dve.wait_ge(s["x_high"], b + 1)
                dve.tensor_tensor(x_lo[:, :], turn_bank[:, 0:SEQ], x_hi[:, :].bitcast(F32), ALU.subtract
                                  ).then_inc(s["x_split"], 1)

            dve.wait_ge(s["zeros_set"], 1)
            normalise_batch(0, 0)
            normalise_batch(1, 1)
            low_x(0)

            def masks(c, g, b):
                n = (b - 1) * (CH * GROUPS) + c * GROUPS + g
                dve.wait_ge(s["scored"], n + 1)
                if g == 0:
                    wait_past(dve, s["out_done" if c else "out0_done"], b - 1)
                dve.tensor_tensor(probs[:, c, 4 * g:4 * g + 4, :], score_bank[g % 2][:, :, :],
                                  mask[:, 4 * g:4 * g + 4, :], ALU.mult).then_inc(s["masked"], 1)

            def turned(b, first, done, parts):
                dve.wait_ge(done, b + 1)
                for k, to in enumerate(parts):
                    w = first + k
                    last = dve.scalar_tensor_tensor(out=to[:, :], in0=qk_bank[:, k * SEQ:(k + 1) * SEQ],
                                                    scalar=qk_bias[:, w:w + 1], in1=turns[:, w, :],
                                                    op0=ALU.add, op1=ALU.mult)
                last.then_inc(s["parts_done"], 1)

            def keep_values(c, b, p):
                if c == 0:
                    wait_past(dve, s["out_done"], b - 1)
                    wait_past(dve, s["g_done"], b - 1)
                dve.wait_ge(s["v_done"], CH * b + c + 1)
                dve.tensor_tensor(own_columns(values[p], c),
                                  v_bank[:, 0, :].rearrange("p (h j v) -> p h j v", j=2, v=VD),
                                  vg_bias[:, 0:2 * D].rearrange("p (h j v) -> p h j v", j=2, v=VD), ALU.add
                                  ).then_inc(s["v_kept"], 1)
                dve.tensor_tensor(g_raw[p][:, c, :], v_bank[:, 1, :], vg_bias[:, 2 * D:], ALU.add
                                  ).then_inc(s["g_kept"], 1)

            def step(b, like):
                p, q = like % 2, (like + 1) % 2
                new, mid, old = like < BATCH, 1 <= like <= BATCH, 2 <= like
                if mid:
                    sums = turn_bank[:, P:P + CH * HEADS]
                    dve.wait_ge(s["k_turned"], b)
                    dve.tensor_scalar(bounded[:, :], sums, 1.0, None, ALU.max).then_inc(s["sum_bounded"], 1)
                    wait_past(dve, s["state_done"], b - 1)
                    dve.tensor_tensor(k_dec[:, :], turn_bank[:, 0:P], k_decay[:, :], ALU.mult).then_inc(s["k_dec_done"], 1)
                    dve.wait_ge(s["sum_bounded"], b)
                    dve.scalar_tensor_tensor(out=clipped[:, :], in0=sums, scalar=-1.0, in1=bounded[:, :],
                                             op0=ALU.mult, op1=ALU.max).then_inc(s["sum_clipped"], 1)
                    masks(0, 0, b)
                    dve.wait_ge(s["sum_clipped"], b)
                    wait_past(dve, s["factor_done"], b - 2)
                    dve.reciprocal(inverse[q][:, :], clipped[:, :]).then_inc(s["sum_inverted"], 1)
                if old:
                    dve.wait_ge(s["squared"], b - 1)
                    dve.tensor_reduce(square_sum[:, :], squares[:, :, :], AX.X, ALU.add).then_inc(s["squares_summed"], 1)
                if mid:
                    dve.wait_ge(s["sum_inverted"], b)
                    dve.tensor_tensor(inverse2[q][:, :], inverse[q][:, :], inverse[q][:, :], ALU.mult
                                      ).then_inc(s["inverse_squared"], 1)
                    masks(0, 1, b)
                if old:
                    dve.wait_ge(s["squares_summed"], b - 1)
                    dve.wait_ge(s["inverse_squared"], b - 1)
                    dve.scalar_tensor_tensor(out=square_sum[:, :], in0=square_sum[:, :], scalar=1.0 / VD,
                                             in1=inverse2[p][:, :], op0=ALU.mult, op1=ALU.mult).then_inc(s["var_scaled"], 1)
                    dve.wait_ge(s["var_scaled"], b - 1)
                    wait_past(dve, s["rstd_done"], b - 2)
                    dve.tensor_scalar(o_var[:, :], square_sum[:, :], EPS, None, ALU.add).then_inc(s["o_var_done"], 1)
                if new:
                    wait_past(dve, s["q_all_done"], b)
                    wait_past(dve, s["keys_done"], b)
                    turned(b, 0, s["q_done"], (q_part, q_turn))
                if mid:
                    masks(0, 2, b)
                    masks(0, 3, b)
                    dve.wait_ge(s["state_done"], b)
                    dve.tensor_tensor(state[:, :, :].rearrange("p h v -> p (h v)"),
                                      qk_bank[:, 0:HEADS * VD],
                                      own_head[:, :, :].rearrange("p h v -> p (h v)"), ALU.mult
                                      ).then_inc(s["state_kept"], 1)
                if new:
                    turned(b, 2, s["k_done"], (k_part, k_turn))
                if mid:
                    masks(1, 0, b)
                    masks(1, 1, b)
                if old:
                    dve.wait_ge(s["factor_done"], b - 1)
                    wait_past(dve, s["gated_done"], b - 2)
                    dve.tensor_tensor(normed[:, :, :], heads[p][:, :, :],
                                      factor[:, :].unsqueeze(2).to_broadcast([P, CH * HEADS, VD]), ALU.mult
                                      ).then_inc(s["normed_done"], 1)
                if new:
                    keep_values(0, b, p)
                if mid:
                    masks(1, 2, b)
                if old:
                    dve.wait_ge(s["normed_done"], b - 1)
                    dve.wait_ge(s["g_done"], b - 1)
                    wait_past(dve, s["y_turned"], b - 2)
                    dve.tensor_tensor(gated[:, :, :].rearrange("p h v -> p (h v)"),
                                      normed[:, :, :].rearrange("p h v -> p (h v)"),
                                      g_act[p][:, :, :].rearrange("p c n -> p (c n)"), ALU.mult
                                      ).then_inc(s["gated_done"], 1)
                if mid:
                    masks(1, 3, b)
                if new:
                    keep_values(1, b, p)
                if new:
                    dve.wait_ge(s["keys_done"], b + 1)
                    wait_past(dve, s["sum_terms_done"], b)
                    dve.tensor_tensor_scan(key_sums[:, :], decays[:, :], keys[p][:, :], 0.0, ALU.mult, ALU.add
                                           ).then_inc(s["key_sums_done"], 1)
                if like + 2 < BATCH:
                    normalise_batch(b + 2, p)
                if old:
                    dve.wait_ge(s["y_high"], b - 1)
                    dve.tensor_tensor(y_lo[:, :], turn_bank[:, :], y_hi[:, :].bitcast(F32), ALU.subtract
                                      ).then_inc(s["y_split"], 1)
                if like + 1 < BATCH:
                    low_x(b + 1)
                if old:
                    dve.wait_ge(s["o_done"], b - 1)
                    dve.wait_ge(s["x_plus_done"], b - 1)
                    dve.tensor_tensor(t["x"][:, bass.ds((b - 2) * CH, CH), :], v_bank[:, 0, :].rearrange("p (c d) -> p c d", c=CH),
                                      x_plus[p][:, :, :], ALU.add).then_inc(s["added"], 1)

            run_batches(dve, step)


def program(nc, a, out):
    with ExitStack() as ctx:
        def sb(name, shape, dt=F32):
            return ctx.enter_context(nc.sbuf_tensor(name, shape, dt))

        def sem(name):
            return ctx.enter_context(nc.semaphore(name))

        t = dict(
            x=sb("x", [P, TILES, D]), ident=sb("ident", [P, P]), earlier=sb("earlier", [P, P]),
            ones=sb("ones", [P, 2 * HEADS]), const=sb("const", [P, C_COLS]), n_tables=3,
            x_loaded=sem("x_loaded"), tables_loaded=sem("tables_loaded"),
            filled=[sem(f"filled{f}") for f in range(2)],
            scattered=[nc.dram_tensor(f"scattered{f}", (ROUTED_UNITS * UNIT, ROW), F32, kind="Internal").ap()
                       for f in range(2)],
            experts=a["experts"], router_w=a["router_w"], router_b=a["router_b"], a=a)
        middle = nc.dram_tensor("middle", (DST_ROWS, D), F32, kind="Internal").ap()
        padding = sb("padding", [P, UT, ROW])
        padding_set, ones_set = sem("padding_set"), sem("ones_set")
        with nc.Block() as block:
            @block.sync
            def _(sp):
                sp.dma_start(t["ident"][:, :], a["ident"]).then_inc(t["tables_loaded"], 16)
                sp.dma_start(t["earlier"][:, :], a["earlier"]).then_inc(t["tables_loaded"], 16)
                sp.dma_start(t["const"][:, :], a["const"]).then_inc(t["tables_loaded"], 16)

            @block.vector
            def _(dve):
                dve.memset(padding[:, :, 0:D + 1], 0.0).then_inc(padding_set, 1)
                dve.wait_ge(t["tables_loaded"], 16 * t["n_tables"])
                dve.tensor_scalar(padding[:, :, D + 1], t["const"][:, C_ID:C_ID + UT], float(TOKENS), None, ALU.add
                                  ).then_inc(padding_set, 1)
                dve.memset(t["ones"][:, :], 1.0).then_inc(ones_set, 1)

            @block.gpsimd
            def _(pool):
                pool.wait_ge(padding_set, 2)
                for f in range(2):
                    for j in range(UT):
                        pool.dma_start(t["scattered"][f].rearrange("(n j p) c -> j p n c", p=P, j=UT)[j],
                                       padding[:, j, :].unsqueeze(1).to_broadcast([P, ROUTED_UNITS, ROW])
                                       ).then_inc(t["filled"][f], 16)
                    pool.dma_start([middle, out][f][TOKENS:DST_ROWS, :].rearrange("(j p) d -> p j d", p=P),
                                   padding[:, :, 0:D]).then_inc(t["filled"][f], 16)

        moe(nc, t, 0, a["x"], middle)
        retention(nc, t, middle)
        moe(nc, t, 1, None, out)


def tables():
    import numpy as np

    p = np.arange(P)
    const = np.zeros((P, C_COLS), np.float32)
    const[:, C_ID:C_ID + TILES] = p[:, None] + P * np.arange(TILES)
    const[:, C_REV:C_REV + EXPERTS] = EXPERTS - np.arange(EXPERTS)
    const[:, C_STEP:C_STEP + EXPERTS] = UNIT * np.arange(EXPERTS)
    const[:, C_UNIT:C_UNIT + ROUTED_UNITS] = np.arange(ROUTED_UNITS)
    const[:, C_HEAD:C_HEAD + 4] = (p[:, None] % 32) // KD == np.arange(4)
    head = np.arange(HEADS)
    angle = np.repeat((1.0 / 10000.0 ** np.linspace(0.0, 1.0, KD // 2, dtype=np.float32)).astype(np.float32), 2)
    at = np.arange(SEQ, dtype=np.float32)
    sin, cos = np.sin(at[None, :] * angle[:, None]), np.cos(at[None, :] * angle[:, None])
    sin = sin * np.where(np.arange(KD) % 2 == 0, -1.0, 1.0)[:, None]
    scaling = KD ** -0.5
    decay = np.log(1.0 - 2.0 ** (-5.0 - head))
    apart = np.arange(SEQ)[:, None] - np.arange(SEQ)[None, :]
    full = np.where(apart >= 0, np.exp(decay[:, None, None] * apart), 0.0)
    norm = np.repeat(1.0 / np.sqrt(full.sum(-1)), KD, axis=0)
    turns = np.tile(cos, (HEADS, 1)), np.tile(sin, (HEADS, 1))
    turns = np.stack([turns[0] * norm, turns[1] * norm, turns[0] * scaling, turns[1] * scaling], axis=1)
    mask = full[:, 0:P, 0:P].transpose(2, 0, 1)
    of_row = p // KD
    q_decay = np.exp(decay[of_row][:, None] * p[None, :])
    k_decay = np.exp(decay[of_row][None, :] * (P - p[:, None]))
    head_of = of_row[:, None] == head[None, :]
    out = {"turns": turns, "mask": mask, "q_decay": q_decay, "k_decay": k_decay, "head_of": head_of,
           "own_head": np.repeat(head_of[:, :, None], VD, axis=2),
           "decays": np.broadcast_to(np.exp(decay[of_row])[:, None], (P, SEQ))}
    out = {k: v.astype(np.float32) for k, v in out.items()} | {"ident": np.eye(P, dtype=np.float32), "earlier": (p[:, None] < p[None, :]).astype(np.float32),
           "const": const}
    return out


def kernel(**inputs):
    import numpy as np
    import concourse.bacc as bacc
    from concourse.bass_utils import run_bass_kernel_spmd as run

    i = {k.replace("L0_", ""): np.asarray(v) for k, v in inputs.items()}

    def expert_rows(w1, b1, w2, b2):
        return np.concatenate([w1.T, w2.T.reshape(CHUNKS, P, D).transpose(1, 0, 2).reshape(P, FF),
                               b1.reshape(CHUNKS, P).T, b2[:, None]], axis=1)

    experts = [expert_rows(i["ffn_spec_w1"][e], i["ffn_spec_b1"][e], i["ffn_spec_w2"][e], i["ffn_spec_b2"][e])
               for e in range(EXPERTS)]
    experts.append(expert_rows(i["ffn_shared_w1"], i["ffn_shared_b1"], i["ffn_shared_w2"], i["ffn_shared_b2"]))
    swap = np.arange(D) ^ 1
    arrays = {
        "x": i["attn_x"].reshape(TOKENS, D),
        "experts": np.stack(experts),
        "router_w": i["ffn_router_w"].T,
        "router_b": np.broadcast_to(i["ffn_router_b"], (P, EXPERTS)),
        "w_qk": np.concatenate([i["attn_Wq"], i["attn_Wq"][:, swap], i["attn_Wk"], i["attn_Wk"][:, swap]], axis=1),
        "b_qk": np.stack([i["attn_bq"], i["attn_bq"][swap], i["attn_bk"], i["attn_bk"][swap]], axis=1),
        "w_vg": np.concatenate([i["attn_Wv"], i["attn_Wg"]], axis=1),
        "b_vg": np.broadcast_to(np.concatenate([i["attn_bv"], i["attn_bg"]]), (P, 4 * D)),
        "w_o": i["attn_Wo"].reshape(2, P, D).transpose(1, 0, 2).reshape(P, 2 * D),
        "b_o": np.broadcast_to(i["attn_bo"], (P, D)),
        **tables(),
    }
    nc = bacc.Bacc("TRN2", target_bir_lowering=False, num_devices=1)
    arrays = {f"in_{k}": np.ascontiguousarray(v) for k, v in arrays.items()}
    a = {k[3:]: nc.dram_tensor(k, v.shape, mybir.dt.from_np(v.dtype), kind="ExternalInput").ap()
         for k, v in arrays.items()}
    out = nc.dram_tensor("out", (DST_ROWS, D), F32, kind="ExternalOutput").ap()
    program(nc, a, out)
    result = run(nc, [arrays], core_ids=[0])
    return result.results[0]["out"][:TOKENS].reshape(BATCH, SEQ, D)
```

```python
from contextlib import ExitStack

import concourse.bass as bass
from concourse import mybir

F32, F32R, I32 = mybir.dt.float32, mybir.dt.float32r, mybir.dt.int32
ALU, ACT, AX = mybir.AluOpType, mybir.ActivationFunctionType, mybir.AxisListType

P = 128
BATCH, SEQ, D = 16, 256, 128
TOKENS = BATCH * SEQ
TILES = TOKENS // P
FF, EXPERTS, TOP = 512, 8, 2
CHUNKS = FF // P
UNIT = 512
UT = UNIT // P
SHARED_UNITS = TOKENS // UNIT
ROUTED_UNITS = (TOP * TOKENS + EXPERTS * (UNIT - 1)) // UNIT
UNITS = SHARED_UNITS + ROUTED_UNITS
ROW = D + 2
DST_ROWS = TOKENS + UNIT
W_COLS = 2 * FF + CHUNKS + 1
HEADS, KD, VD = 16, 8, 16
V1 = VD + 1
EPS = 1e-5
C_ID, C_REV, C_STEP, C_UNIT, C_HEAD = 0, TILES, TILES + EXPERTS, TILES + 2 * EXPERTS, TILES + 2 * EXPERTS + 32
C_COLS = C_HEAD + 4


def wait_past(eng, sem, value):
    if not isinstance(value, int) or value > 0:
        eng.wait_ge(sem, value)


def release(nc, sems):
    nc.clear_and_free_semaphores(sems)
    nc.all_engine_barrier()


class Chain:

    def __init__(self, eng, sem):
        self.eng, self.sem, self.count = eng, sem, 0

    def then(self, instruction):
        self.count += 1
        instruction.then_inc(self.sem, 1)
        self.eng.wait_ge(self.sem, self.count)


def three_passes(pe, out, w_hi, w_lo, x_hi, x_lo, start=True, stop=True):
    pe.matmul(out, w_hi, x_hi, start=start, stop=False)
    pe.matmul(out, w_hi, x_lo, start=False, stop=False)
    return pe.matmul(out, w_lo, x_hi, start=False, stop=stop)


def layernorm_stats(dve, act_sqrt, chain, x, m, arrived):
    for tile in range(TILES):
        if arrived and tile % (TILES // 4) == 0:
            dve.wait_ge(arrived[tile // (TILES // 4)], 16)
        last = dve.bn_stats(m["stats"][:, tile, :], x[:, tile, :])
    chain.then(last)
    even_mean, even_cv, odd_mean, odd_cv = (m["stats"][:, :, k] for k in (1, 2, 4, 5))
    dve.tensor_tensor(m["diff"][:, :], even_mean, odd_mean, ALU.subtract)
    dve.tensor_tensor(m["mean"][:, :], even_mean, odd_mean, ALU.add)
    chain.then(dve.tensor_tensor(m["var"][:, :], even_cv, odd_cv, ALU.add))
    chain.then(dve.tensor_tensor(m["diff"][:, :], m["diff"][:, :], m["diff"][:, :], ALU.mult))
    chain.then(dve.scalar_tensor_tensor(out=m["var"][:, :], in0=m["var"][:, :], scalar=4.0 / D, in1=m["diff"][:, :],
                                        op0=ALU.mult, op1=ALU.add))
    dve.tensor_scalar(m["mean"][:, :], m["mean"][:, :], 0.5, None, ALU.mult)
    dve.tensor_scalar(m["var"][:, :], m["var"][:, :], 0.25, EPS, ALU.mult, ALU.add).then_inc(m["var_done"], 1)
    dve.wait_ge(act_sqrt, 1)
    chain.then(dve.reciprocal(m["rstd"][:, :], m["root"][:, :]))
    chain.then(dve.tensor_tensor(m["diff"][:, :], m["rstd"][:, :], m["rstd"][:, :], ALU.mult))
    chain.then(dve.scalar_tensor_tensor(out=m["diff"][:, :], in0=m["diff"][:, :], scalar=-0.5, in1=m["var"][:, :],
                                        op0=ALU.mult, op1=ALU.mult))
    chain.then(dve.scalar_tensor_tensor(out=m["rstd"][:, :], in0=m["diff"][:, :], scalar=1.5, in1=m["rstd"][:, :],
                                        op0=ALU.add, op1=ALU.mult))


def normalise(dve, out, x, tile, m):
    return dve.tensor_scalar(out, x[:, bass.ds(tile, 1), :].rearrange("p t d -> p (t d)"),
                             m["mean"][:, bass.ds(tile, 1)], m["rstd"][:, bass.ds(tile, 1)], ALU.subtract, ALU.mult)


def run_steps(eng, step):
    a, b = 4, SHARED_UNITS - 2
    c = SHARED_UNITS + 4
    d = c + (UNITS - 1 - c) // 2 * 2
    for u in range(a):
        step(u, u)
    with eng.Fori(a // 2, b // 2) as pair:
        for j in range(2):
            step(pair * 2 + j, a + j)
    for u in range(b, c):
        step(u, u)
    with eng.Fori(c // 2, d // 2) as pair:
        for j in range(2):
            step(pair * 2 + j, c + j)
    for u in range(d, UNITS + 2):
        step(u, u)


def moe(nc, t, f, dst):
    scattered = t["scattered"][f]
    with ExitStack() as ctx:
        sems = []

        def sem(name):
            sems.append(nc.alloc_semaphore(f"m{f}_{name}"))
            return sems[-1]

        def sb(name, shape, dt=F32):
            return ctx.enter_context(nc.sbuf_tensor(f"m{f}_{name}", shape, dt))

        bank = [ctx.enter_context(nc.psum_tensor(f"m{f}_bank{i}", [P, UNIT], F32)) for i in range(8)]
        up_bank, down_bank, y_bank, x_bank = bank[0:4], bank[4:6], bank[6], bank[7]

        m = dict(stats=sb("stats", [P, TILES, 6]), mean=sb("mean", [P, TILES]), var=sb("var", [P, TILES]),
                            diff=sb("diff", [P, TILES]), root=sb("root", [P, TILES]), rstd=sb("rstd", [P, TILES]),
                            var_done=sem("var_done"))
        xn = [sb(f"xn{p}", [P, UT, D]) for p in range(2)]
        x_t = [sb(f"x_t{p}", [P, UNIT]) for p in range(2)]
        x_t_all = sb("x_t_all", [P, SHARED_UNITS, UNIT])
        rows_out = sb("rows_out", [P, TILES, ROW])
        logits = sb("logits", [P, TILES, EXPERTS])
        prob = sb("prob", [P, TILES, EXPERTS])
        rest = sb("rest", [P, TILES, EXPERTS])
        score = sb("score", [P, TILES, EXPERTS])
        chosen = [sb(f"chosen{k}", [P, TILES, EXPERTS]) for k in range(TOP)]
        both = sb("both", [P, TILES, EXPERTS], F32R)
        best = sb("best", [P, TILES])
        top = [sb(f"top{k}", [P, TILES]) for k in range(TOP)]
        gate = [sb(f"gate{k}", [P, TILES]) for k in range(TOP)]
        totals = sb("totals", [P, TILES, EXPERTS])
        running = sb("running", [P, TILES, EXPERTS])
        units_of = sb("units_of", [P, EXPERTS])
        end_of = sb("end_of", [P, EXPERTS])
        base_of = sb("base_of", [P, EXPERTS])
        over = sb("over", [P, EXPERTS, EXPERTS])
        passed = sb("passed", [P, ROUTED_UNITS, EXPERTS - 1])
        expert_f = sb("expert_f", [P, ROUTED_UNITS])
        expert_of = sb("expert_of", [P, ROUTED_UNITS], I32)
        place_f = [sb(f"place_f{k}", [P, TILES]) for k in range(TOP)]
        place = [sb(f"place{k}", [P, TILES], I32) for k in range(TOP)]
        w1_raw = [sb(f"w1_raw{p}", [P, W_COLS - FF]) for p in range(2)]
        w2_raw = [sb(f"w2_raw{p}", [P, FF]) for p in range(2)]
        w_hi = [sb(f"w_hi{p}", [P, 2, FF], F32R) for p in range(2)]
        w_lo = [sb(f"w_lo{p}", [P, 2, FF], F32R) for p in range(2)]
        sh_raw, sh_hi, sh_lo = sb("sh_raw", [P, W_COLS]), sb("sh_hi", [P, 2, FF], F32R), sb("sh_lo", [P, 2, FF], F32R)
        bias_of = sb("bias_of", [P, ROUTED_UNITS, CHUNKS + 1])
        tail_of = sb("tail_of", [P, ROUTED_UNITS, UT, 2])
        rows = [sb(f"rows{p}", [P, UT, ROW]) for p in range(2)]
        x_hi = [sb(f"x_hi{p}", [P, UNIT], F32R) for p in range(2)]
        x_lo = [sb(f"x_lo{p}", [P, UNIT], F32R) for p in range(2)]
        h = sb("h", [P, CHUNKS, UNIT])
        h_hi = sb("h_hi", [P, 2, CHUNKS, UNIT], F32R)
        h_lo = sb("h_lo", [P, 2, CHUNKS, UNIT], F32R)
        y_t = [sb(f"y_t{p}", [P, UNIT]) for p in range(2)]
        y = [sb(f"y{p}", [P, UT, D]) for p in range(2)]
        number = [sb(f"number{p}", [P, UT], I32) for p in range(2)]
        turn = sb("turn", [1, 1 + ROUTED_UNITS])
        router_w = sb("router_w", [P, EXPERTS])
        router_b = sb("router_b", [P, EXPERTS])
        earlier = sb("earlier", [P, P], F32R)
        ones = sb("ones", [P, P], F32R)

        s = {n: sem(n) for n in (
            "params", "casts", "rooted", "chain", "act_chain", "xn_done", "xn_turned", "xt_out", "xt_kept", "logit_done",
            "logit_kept", "row_kept", "shifted", "exped", "both_done", "prefixed", "gates_done", "places_done",
            "experts_done", "id_done", "gate2_done", "scatter0", "scatter1", "sh_loaded", "sh_hi", "sh_split",
            "x_turned", "x_high", "x_split", "w1_high", "w1_split", "w2_high", "w2_split", "up_done", "gelu_done",
            "h_high", "h_split", "down_done", "yt_done", "y_turned", "y_done", "tail_kept", "bias_kept", "y_added", "turn_set", "number_done", "filled")}
        w1_loaded = [sem(f"w1_loaded{p}") for p in range(2)]
        w2_loaded = [sem(f"w2_loaded{p}") for p in range(2)]
        rows_loaded = [sem(f"rows_loaded{p}") for p in range(2)]
        y_stored = [sem(f"y_stored{p}") for p in range(2)]

        ctx.callback(release, nc, sems)
        block = ctx.enter_context(nc.Block())

        @block.sync
        def _(sp):
            sp.dma_start(router_w[:, :], t["router_w"]).then_inc(s["params"], 16)
            sp.dma_start(router_b[:, :], t["router_b"]).then_inc(s["params"], 16)
            sp.dma_start(sh_raw[:, :], t["experts"][EXPERTS]).then_inc(s["sh_loaded"], 16)

            for j in range(UT):
                sp.dma_start(scattered.rearrange("(n j p) c -> j p n c", p=P, j=UT)[j],
                             t["padding"][:, j, :].unsqueeze(1).to_broadcast([P, ROUTED_UNITS, ROW])
                             ).then_inc(s["filled"], 16)
            sp.dma_start(dst[TOKENS:DST_ROWS, :].rearrange("(j p) d -> p j d", p=P), t["padding"][:, :, 0:D]
                         ).then_inc(s["filled"], 16)

            def load_w1(r, p):
                e = expert(r)
                wait_past(sp, s["bias_kept"], r - 1)
                wait_past(sp, s["w1_split"], r - 1)
                sp.dma_start(w1_raw[p][:, :], t["experts"][bass.ds(e, 1), :, FF:].rearrange("e p c -> (e p) c")
                             ).then_inc(w1_loaded[p], 16)

            def load_w2(r, p):
                e = expert(r)
                wait_past(sp, s["w2_split"], r - 1)
                sp.dma_start(w2_raw[p][:, :], t["experts"][bass.ds(e, 1), :, 0:FF].rearrange("e p c -> (e p) c")
                             ).then_inc(w2_loaded[p], 16)

            def load_rows(r, p):
                wait_past(sp, s["tail_kept"], r - 1)
                wait_past(sp, s["x_turned"], r - 1)
                sp.dma_start(rows[p][:, :, :], scattered[bass.ds(r * UNIT, UNIT), :]
                             .rearrange("(t p) c -> p t c", p=P)).then_inc(rows_loaded[p], 16)

            def expert(r):
                return sp.value_load(expert_of[0:1, bass.ds(r, 1)], min_val=0, max_val=EXPERTS - 1)

            sp.wait_ge(s["experts_done"], 1)
            for r in range(2):
                load_w1(r, r)
                load_w2(r, r)

            sp.wait_ge(s["scatter0"], 16 * TILES)
            sp.wait_ge(s["scatter1"], 16 * TILES)
            for r in range(2):
                load_rows(r, r)

            def load(r, p):
                load_rows(r, p)
                load_w1(r, p)
                load_w2(r, p)

            with sp.Fori(1, ROUTED_UNITS // 2) as pair:
                for p in range(2):
                    load(pair * 2 + p, p)
            for r in range(ROUTED_UNITS // 2 * 2, ROUTED_UNITS):
                load(r, r % 2)
            sp.wait_ge(s["y_added"], 16 * UT * ROUTED_UNITS)
            sp.wait_ge(y_stored[0], 16 * (SHARED_UNITS // 2))
            sp.wait_ge(y_stored[1], 16 * (SHARED_UNITS // 2))

        @block.gpsimd
        def _(pool):
            def keep_rows(b, p):
                pool.wait_ge(s["xn_done"], b + 1)
                pool.tensor_copy(rows_out[:, bass.ds(b * UT, UT), 0:D], xn[p][:, :, :]).then_inc(s["row_kept"], 1)

            with pool.Fori(0, SHARED_UNITS // 2) as pair:
                for p in range(2):
                    keep_rows(pair * 2 + p, p)
            pool.wait_ge(s["row_kept"], SHARED_UNITS)
            pool.wait_ge(s["id_done"], 1)
            pool.wait_ge(s["gates_done"], 1)
            pool.wait_ge(s["places_done"], 1)
            pool.wait_ge(s["filled"], 16 * (UT + 1))
            for tile in range(TILES):
                pool.indirect_dma_start(scattered, bass.IndirectOffsetOnAxis(ap=place[0][:, tile:tile + 1], axis=0),
                                        rows_out[:, tile, :], None).then_inc(s["scatter0"], 16)
            pool.wait_ge(s["scatter0"], 16 * TILES)
            pool.tensor_copy(rows_out[:, :, D], gate[1][:, :]).then_inc(s["gate2_done"], 1)
            pool.wait_ge(s["gate2_done"], 1)
            for tile in range(TILES):
                pool.indirect_dma_start(scattered, bass.IndirectOffsetOnAxis(ap=place[1][:, tile:tile + 1], axis=0),
                                        rows_out[:, tile, :], None).then_inc(s["scatter1"], 16)

            def add_rows(r, p):
                pool.wait_ge(s["y_done"], r + SHARED_UNITS + 1)
                pool.wait_ge(s["number_done"], r + 1)
                wait_past(pool, s["y_added"], r * (16 * UT))
                pool.tensor_tensor(turn[:, bass.ds(r + 1, 1)], turn[:, 0:1], turn[:, 0:1], ALU.add)
                for j in range(UT):
                    pool.indirect_dma_start(dst, bass.IndirectOffsetOnAxis(ap=number[p][:, j:j + 1], axis=0),
                                            y[p][:, j, :], None, compute_op=ALU.add).then_inc(s["y_added"], 16)

            pool.wait_ge(y_stored[0], 16 * (SHARED_UNITS // 2))
            pool.wait_ge(y_stored[1], 16 * (SHARED_UNITS // 2))
            pool.memset(turn[:, :], 0.0).then_inc(s["turn_set"], 1)
            pool.wait_ge(s["turn_set"], 1)
            add_rows(0, 0)
            add_rows(1, 1)
            with pool.Fori(1, ROUTED_UNITS // 2) as pair:
                for p in range(2):
                    add_rows(pair * 2 + p, p)
            for r in range(ROUTED_UNITS // 2 * 2, ROUTED_UNITS):
                add_rows(r, r % 2)

        @block.tensor
        def _(pe):
            pe.wait_ge(s["params"], 32)

            def turn_block(b, p):
                pe.wait_ge(s["xn_done"], b + 1)
                wait_past(pe, s["xt_kept"], b - 1)
                for j in range(UT):
                    last = pe.transpose(up_bank[p][:, j * P:(j + 1) * P], xn[p][:, j, :], t["ident"][:, :])
                last.then_inc(s["xn_turned"], 1)

            def route_block(b, p):
                pe.wait_ge(s["xt_out"], b + 1)
                wait_past(pe, s["logit_kept"], b - 1)
                for j in range(UT):
                    last = pe.matmul(up_bank[2 + p][:, j * EXPERTS:(j + 1) * EXPERTS], x_t[p][:, j * P:(j + 1) * P],
                                     router_w[:, :], start=True, stop=True)
                last.then_inc(s["logit_done"], 1)

            turn_block(0, 0)
            turn_block(1, 1)
            route_block(0, 0)
            with pe.Fori(1, SHARED_UNITS // 2) as pair:
                turn_block(pair * 2, 0)
                route_block(pair * 2 - 1, 1)
                turn_block(pair * 2 + 1, 1)
                route_block(pair * 2, 0)
            route_block(SHARED_UNITS - 1, 1)

            pe.wait_ge(s["both_done"], 1)
            flat = both[:, :, :].rearrange("p t e -> p (t e)")
            pe.matmul(down_bank[0][:, 0:TILES * EXPERTS], earlier[:, :], flat, start=True, stop=True)
            pe.matmul(down_bank[1][:, 0:TILES * EXPERTS], ones[:, :], flat, start=True, stop=True
                      ).then_inc(s["prefixed"], 1)

            def step(u, like):
                p, q = like % 2, (like + 1) % 2
                up, down, turn = like < UNITS, 1 <= like <= UNITS, 2 <= like
                hi, lo = (sh_hi, sh_lo) if like < SHARED_UNITS else (w_hi[p], w_lo[p])
                hi1, lo1 = (sh_hi, sh_lo) if like - 1 < SHARED_UNITS else (w_hi[q], w_lo[q])
                for c in range(CHUNKS):
                    cols = slice(c * P, (c + 1) * P)
                    if up:
                        if c == 0:
                            pe.wait_ge(s["x_split"], u + 1)
                            if like < SHARED_UNITS:
                                pe.wait_ge(s["sh_split"], 1)
                            else:
                                pe.wait_ge(s["w1_split"], u - SHARED_UNITS + 1)
                        if like == 0:
                            pe.wait_ge(s["logit_kept"], SHARED_UNITS)
                        wait_past(pe, s["gelu_done"], (u - 1) * CHUNKS + c + 1)
                        three_passes(pe, up_bank[c][:, :], hi[:, 0, cols], lo[:, 0, cols], x_hi[p][:, :], x_lo[p][:, :]
                                     ).then_inc(s["up_done"], 1)
                    if down:
                        if c == 0:
                            if like - 1 >= SHARED_UNITS:
                                pe.wait_ge(s["w2_split"], u - SHARED_UNITS)
                            wait_past(pe, s["yt_done"], u - 2)
                            if like - 1 < 2:
                                pe.wait_ge(s["places_done"], 1)
                        pe.wait_ge(s["h_split"], (u - 1) * CHUNKS + c + 1)
                        last = three_passes(pe, down_bank[q][:, :], hi1[:, 1, cols], lo1[:, 1, cols],
                                            h_hi[:, q, c, :], h_lo[:, q, c, :], start=c == 0, stop=c == CHUNKS - 1)
                        if c == CHUNKS - 1:
                            last.then_inc(s["down_done"], 1)
                    if c == 0 and SHARED_UNITS <= like + 1 < UNITS:
                        r = u + 1 - SHARED_UNITS
                        pe.wait_ge(rows_loaded[q], (r - q) * 8 + 16)
                        pe.wait_ge(s["x_split"], u + 1)
                        for j in range(UT):
                            last = pe.transpose(x_bank[:, j * P:(j + 1) * P], rows[q][:, j, 0:D], t["ident"][:, :])
                        last.then_inc(s["x_turned"], 1)
                    if c == 1 and turn:
                        pe.wait_ge(s["yt_done"], u - 1)
                        wait_past(pe, s["y_done"], u - 2)
                        for j in range(UT):
                            last = pe.transpose(y_bank[:, j * P:(j + 1) * P], y_t[p][:, j * P:(j + 1) * P], t["ident"][:, :])
                        last.then_inc(s["y_turned"], 1)

            run_steps(pe, step)

        @block.scalar
        def _(act):
            act.wait_ge(m["var_done"], 1)
            act.activation(m["root"][:, :], m["var"][:, :], ACT.Sqrt).then_inc(s["rooted"], 1)

            def evacuate(b, p):
                act.wait_ge(s["xn_turned"], b + 1)
                wait_past(act, s["logit_done"], b - 1)
                act.copy(x_t[p][:, :], up_bank[p][:, :]).then_inc(s["xt_out"], 1)
                act.copy(x_t_all[:, bass.ds(b, 1), :].rearrange("p b n -> p (b n)"), up_bank[p][:, :]
                         ).then_inc(s["xt_kept"], 1)

            evacuate(0, 0)
            evacuate(1, 1)
            with act.Fori(1, SHARED_UNITS // 2) as pair:
                for p in range(2):
                    evacuate(pair * 2 + p, p)
            act.wait_ge(s["sh_loaded"], 16)
            for k in range(2):
                act.copy(sh_hi[:, k, :], sh_raw[:, (1 - k) * FF:(2 - k) * FF]).then_inc(s["sh_hi"], 1)
            act.wait_ge(s["shifted"], 1)
            act.activation(prob[:, :, :], logits[:, :, :], ACT.Exp).then_inc(s["exped"], 1)

            def high_x(u, like):
                p = like % 2
                if like < SHARED_UNITS:
                    act.wait_ge(s["xt_kept"], SHARED_UNITS)
                    source = x_t_all[:, bass.ds(u, 1), :].rearrange("p b n -> p (b n)")
                else:
                    act.wait_ge(s["x_turned"], u - SHARED_UNITS + 1)
                    source = x_bank[:, :]
                wait_past(act, s["up_done"], (u - 1) * CHUNKS)
                act.copy(x_hi[p][:, :], source).then_inc(s["x_high"], 1)

            def high_w(which, u, like, done):
                p, r = like % 2, u - SHARED_UNITS
                act.wait_ge((w1_loaded, w2_loaded)[which][p], (r - p) * 8 + 16)
                if which == 0:
                    wait_past(act, s["up_done"], (u - 1) * CHUNKS)
                else:
                    wait_past(act, s["down_done"], u - 1)
                act.copy(w_hi[p][:, which, :], (w1_raw, w2_raw)[which][p][:, 0:FF]).then_inc(done, 1)

            high_x(0, 0)

            def step(u, like):
                p = like % 2
                if like >= 2:
                    act.wait_ge(s["down_done"], u - 1)
                    wait_past(act, s["y_turned"], u - 2)
                    if like - 2 < SHARED_UNITS:
                        bias = sh_raw[:, 2 * FF + CHUNKS:]
                    else:
                        act.wait_ge(s["bias_kept"], u - 2 - SHARED_UNITS + 1)
                        bias = bias_of[:, bass.ds(u - 2 - SHARED_UNITS, 1), CHUNKS:].rearrange("p u c -> p (u c)")
                    act.activation(y_t[p][:, :], down_bank[p][:, :], ACT.Identity, bias=bias).then_inc(s["yt_done"], 1)
                for c in range(CHUNKS):
                    if like < UNITS:
                        act.wait_ge(s["up_done"], u * CHUNKS + c + 1)
                        wait_past(act, s["h_split"], (u - 1) * CHUNKS + c + 1)
                        if like < SHARED_UNITS:
                            bias = sh_raw[:, 2 * FF + c:2 * FF + c + 1]
                        else:
                            if c == 0:
                                act.wait_ge(s["bias_kept"], u - SHARED_UNITS + 1)
                            bias = bias_of[:, bass.ds(u - SHARED_UNITS, 1), c:c + 1].rearrange("p u c -> p (u c)")
                        act.activation(h[:, c, :], up_bank[c][:, :], ACT.Gelu_apprx_tanh, bias=bias
                                       ).then_inc(s["gelu_done"], 1)
                    if c == 0 and SHARED_UNITS <= like + 1 < UNITS:
                        high_w(0, u + 1, like + 1, s["w1_high"])
                    if c == 1 and like + 1 < UNITS:
                        high_x(u + 1, like + 1)
                    if c == 2 and SHARED_UNITS <= like < UNITS:
                        high_w(1, u, like, s["w2_high"])
                    if c == 2 and like >= SHARED_UNITS + 2:
                        r = u - 2 - SHARED_UNITS
                        act.wait_ge(s["y_turned"], u - 1)
                        if like < SHARED_UNITS + 4:
                            act.wait_ge(y_stored[p], 16 * (SHARED_UNITS // 2))
                        else:
                            act.wait_ge(s["y_added"], (r - 1) * (16 * UT))
                        act.wait_ge(s["tail_kept"], r + 1)
                        for j in range(UT):
                            last = act.mul(y[p][:, j, :], y_bank[:, j * P:(j + 1) * P],
                                           tail_of[:, bass.ds(r, 1), j, 0:1].rearrange("p u c -> p (u c)"))
                        last.then_inc(s["y_done"], 1)
                    if c == 3 and 2 <= like < SHARED_UNITS + 2:
                        act.wait_ge(s["y_done"], u - 1)
                        act.dma_start(dst[bass.ds((u - 2) * UNIT, UNIT), :].rearrange("(t p) d -> p t d", p=P),
                                      y[p][:, :, :]).then_inc(y_stored[p], 16)

            run_steps(act, step)

        @block.vector
        def _(dve):
            chain = Chain(dve, s["chain"])
            dve.wait_ge(t["tables_loaded"], 16 * t["n_tables"])
            dve.tensor_copy(earlier[:, :], t["earlier"][:, :])
            dve.tensor_scalar(ones[:, :], t["earlier"][:, :], 0.0, 1.0, ALU.mult, ALU.add).then_inc(s["casts"], 1)
            layernorm_stats(dve, s["rooted"], chain, t["x"], m, () if f else t["x_loaded"])

            def normalise_block(b, p):
                wait_past(dve, s["xn_turned"], b - 1)
                wait_past(dve, s["row_kept"], b - 1)
                for j in range(UT):
                    last = normalise(dve, xn[p][:, j, :], t["x"], b * UT + j, m)
                last.then_inc(s["xn_done"], 1)

            def keep_logits(b, p):
                dve.wait_ge(s["logit_done"], b + 1)
                dve.tensor_tensor(logits[:, bass.ds(b * UT, UT), :],
                                  up_bank[2 + p][:, 0:UT * EXPERTS].rearrange("p (t e) -> p t e", e=EXPERTS),
                                  router_b[:, :].unsqueeze(1).to_broadcast([P, UT, EXPERTS]), ALU.add
                                  ).then_inc(s["logit_kept"], 1)

            dve.wait_ge(s["params"], 32)
            normalise_block(0, 0)
            normalise_block(1, 1)
            with dve.Fori(1, SHARED_UNITS // 2) as pair:
                normalise_block(pair * 2, 0)
                keep_logits(pair * 2 - 2, 0)
                normalise_block(pair * 2 + 1, 1)
                keep_logits(pair * 2 - 1, 1)
            keep_logits(SHARED_UNITS - 2, 0)
            keep_logits(SHARED_UNITS - 1, 1)
            dve.wait_ge(s["logit_kept"], SHARED_UNITS)

            def per_expert(column):
                return column[:, :].unsqueeze(2).to_broadcast([P, TILES, EXPERTS])

            def per_token(row):
                return row.unsqueeze(1).to_broadcast([P, TILES, EXPERTS])

            chain.then(dve.tensor_reduce(best[:, :], logits[:, :, :], AX.X, ALU.max))
            dve.tensor_tensor(logits[:, :, :], logits[:, :, :], per_expert(best), ALU.subtract).then_inc(s["shifted"], 1)
            dve.wait_ge(s["exped"], 1)
            chain.then(dve.tensor_reduce(best[:, :], prob[:, :, :], AX.X, ALU.add))
            chain.then(dve.reciprocal(best[:, :], best[:, :]))
            chain.then(dve.tensor_tensor(prob[:, :, :], prob[:, :, :], per_expert(best), ALU.mult))
            rev = t["const"][:, C_REV:C_REV + EXPERTS]
            left = prob
            for k in range(TOP):
                chain.then(dve.tensor_reduce(top[k][:, :], left[:, :, :], AX.X, ALU.max))
                chain.then(dve.tensor_tensor(score[:, :, :], left[:, :, :], per_expert(top[k]), ALU.is_equal))
                chain.then(dve.tensor_tensor(score[:, :, :], score[:, :, :], per_token(rev), ALU.mult))
                chain.then(dve.tensor_reduce(best[:, :], score[:, :, :], AX.X, ALU.max))
                chain.then(dve.tensor_tensor(chosen[k][:, :, :], score[:, :, :], per_expert(best), ALU.is_equal))
                if k == 0:
                    chain.then(dve.scalar_tensor_tensor(out=rest[:, :, :], in0=chosen[0][:, :, :], scalar=-2.0,
                                                        in1=prob[:, :, :], op0=ALU.mult, op1=ALU.add))
                    left = rest
            dve.wait_ge(s["casts"], 1)
            dve.tensor_tensor(both[:, :, :], chosen[0][:, :, :], chosen[1][:, :, :], ALU.add).then_inc(s["both_done"], 1)
            chain.then(dve.tensor_tensor(best[:, :], top[0][:, :], top[1][:, :], ALU.add))
            chain.then(dve.reciprocal(best[:, :], best[:, :]))
            for k in range(TOP):
                chain.then(dve.scalar_tensor_tensor(out=gate[k][:, :], in0=top[k][:, :], scalar=0.5, in1=best[:, :],
                                                    op0=ALU.mult, op1=ALU.mult))
            dve.tensor_copy(rows_out[:, :, D + 1], t["const"][:, C_ID:C_ID + TILES]).then_inc(s["id_done"], 1)
            dve.tensor_copy(rows_out[:, :, D], gate[0][:, :]).then_inc(s["gates_done"], 1)
            dve.wait_ge(s["prefixed"], 1)
            chain.then(dve.tensor_copy(totals[:, :, :].rearrange("p t e -> p (t e)"), down_bank[1][:, 0:TILES * EXPERTS]))
            for e in range(EXPERTS):
                last = dve.tensor_tensor_scan(running[:, :, e], t["ones"][:, 0:TILES], totals[:, :, e], 0.0,
                                              ALU.mult, ALU.add)
            chain.then(last)
            steps = t["const"][:, C_STEP:C_STEP + EXPERTS]
            chain.then(dve.tensor_tensor(over[:, :, :],
                                         running[:, TILES - 1, :].unsqueeze(2).to_broadcast([P, EXPERTS, EXPERTS]),
                                         steps.unsqueeze(1).to_broadcast([P, EXPERTS, EXPERTS]), ALU.is_gt))
            chain.then(dve.tensor_reduce(units_of[:, :], over[:, :, :], AX.X, ALU.add))
            chain.then(dve.tensor_tensor_scan(end_of[:, :], t["ones"][:, 0:EXPERTS], units_of[:, :], 0.0, ALU.mult, ALU.add))
            chain.then(dve.tensor_tensor(base_of[:, :], end_of[:, :], units_of[:, :], ALU.subtract))
            chain.then(dve.tensor_scalar(base_of[:, :], base_of[:, :], float(UNIT), None, ALU.mult))
            chain.then(dve.tensor_tensor(
                passed[:, :, :], end_of[:, 0:EXPERTS - 1].unsqueeze(1).to_broadcast([P, ROUTED_UNITS, EXPERTS - 1]),
                t["const"][:, C_UNIT:C_UNIT + ROUTED_UNITS].unsqueeze(2).to_broadcast([P, ROUTED_UNITS, EXPERTS - 1]),
                ALU.is_le))
            chain.then(dve.tensor_reduce(expert_f[:, :], passed[:, :, :], AX.X, ALU.add))
            dve.tensor_copy(expert_of[:, :], expert_f[:, :]).then_inc(s["experts_done"], 1)
            chain.then(dve.tensor_tensor(running[:, :, :], running[:, :, :], totals[:, :, :], ALU.subtract))
            chain.then(dve.tensor_tensor(running[:, :, :], running[:, :, :], per_token(base_of[:, :]), ALU.add))
            chain.then(dve.tensor_tensor(running[:, :, :], running[:, :, :],
                                         down_bank[0][:, 0:TILES * EXPERTS].rearrange("p (t e) -> p t e", e=EXPERTS),
                                         ALU.add))
            for k in range(TOP):
                chain.then(dve.tensor_tensor(score[:, :, :], running[:, :, :], chosen[k][:, :, :], ALU.mult))
                chain.then(dve.tensor_reduce(place_f[k][:, :], score[:, :, :], AX.X, ALU.add))
                last = dve.tensor_copy(place[k][:, :], place_f[k][:, :])
            last.then_inc(s["places_done"], 1)

            dve.wait_ge(s["sh_hi"], 2)
            for k in range(2):
                last = dve.tensor_tensor(sh_lo[:, k, :], sh_raw[:, (1 - k) * FF:(2 - k) * FF],
                                         sh_hi[:, k, :].bitcast(F32), ALU.subtract)
            last.then_inc(s["sh_split"], 1)

            def low_x(u, like):
                p = like % 2
                dve.wait_ge(s["x_high"], u + 1)
                source = (x_t_all[:, bass.ds(u, 1), :].rearrange("p b n -> p (b n)") if like < SHARED_UNITS
                          else x_bank[:, :])
                dve.tensor_tensor(x_lo[p][:, :], source, x_hi[p][:, :].bitcast(F32), ALU.subtract).then_inc(s["x_split"], 1)
                if like >= SHARED_UNITS:
                    r = u - SHARED_UNITS
                    dve.wait_ge(rows_loaded[p], (r - p) * 8 + 16)
                    dve.tensor_scalar(tail_of[:, bass.ds(r, 1), :, :].rearrange("p u t c -> p (u t) c"),
                                      rows[p][:, :, D:ROW], 1.0, None, ALU.mult).then_inc(s["tail_kept"], 1)

            def low_w(which, u, like, high, done):
                p, r = like % 2, u - SHARED_UNITS
                dve.wait_ge(high, r + 1)
                if which == 0:
                    dve.tensor_scalar(bias_of[:, bass.ds(r, 1), :].rearrange("p u c -> p (u c)"),
                                      w1_raw[p][:, FF:], 1.0, None, ALU.mult).then_inc(s["bias_kept"], 1)
                dve.tensor_tensor(w_lo[p][:, which, :], (w1_raw, w2_raw)[which][p][:, 0:FF],
                                  w_hi[p][:, which, :].bitcast(F32), ALU.subtract).then_inc(done, 1)

            low_x(0, 0)

            def step(u, like):
                p = like % 2
                for c in range(CHUNKS):
                    if like < UNITS:
                        n = u * CHUNKS + c + 1
                        dve.wait_ge(s["gelu_done"], n)
                        wait_past(dve, s["down_done"], u - 1)
                        dve.tensor_copy(h_hi[:, p, c, :], h[:, c, :]).then_inc(s["h_high"], 1)
                        dve.wait_ge(s["h_high"], n)
                        dve.tensor_tensor(h_lo[:, p, c, :], h[:, c, :], h_hi[:, p, c, :].bitcast(F32), ALU.subtract
                                          ).then_inc(s["h_split"], 1)
                    if c == 0 and SHARED_UNITS <= like + 1 < UNITS:
                        low_w(0, u + 1, like + 1, s["w1_high"], s["w1_split"])
                    if c == 1 and like + 1 < UNITS:
                        low_x(u + 1, like + 1)
                    if c == 2 and SHARED_UNITS <= like < UNITS:
                        low_w(1, u, like, s["w2_high"], s["w2_split"])
                    if c == 2 and 2 <= like < SHARED_UNITS + 2:
                        v = u - 2
                        dve.wait_ge(s["y_turned"], v + 1)
                        wait_past(dve, y_stored[p], (v - p) * 8)
                        dve.scalar_tensor_tensor(
                            out=y[p][:, :, :].rearrange("p t d -> p (t d)"), in0=y_bank[:, :], scalar=0.5,
                            in1=t["x"][:, bass.ds(v * UT, UT), :].rearrange("p t d -> p (t d)"),
                            op0=ALU.mult, op1=ALU.add).then_inc(s["y_done"], 1)
                    if c == 2 and like >= SHARED_UNITS + 2:
                        r = u - 2 - SHARED_UNITS
                        wait_past(dve, s["y_added"], (r - 1) * (16 * UT))
                        dve.wait_ge(s["tail_kept"], r + 1)
                        dve.tensor_scalar(number[p][:, :], tail_of[:, bass.ds(r, 1), :, 1].rearrange("p u t -> p (u t)"),
                                          1.0, None, ALU.mult).then_inc(s["number_done"], 1)

            run_steps(dve, step)


def run_batches(eng, step):
    for b in range(4):
        step(b, b)
    with eng.Fori(2, BATCH // 2 - 1) as pair:
        for j in range(2):
            step(pair * 2 + j, 4 + j)
    for b in range(BATCH - 2, BATCH + 2):
        step(b, b)


def own_columns(values, c):
    return values[:, c, :, :, :].rearrange("p h j v -> p h (j v)").rearrange("p h (k v) -> p h k v", v=VD)[:, :, 0:4:3, :]


def retention(nc, t, src):
    with ExitStack() as ctx:
        sems = []

        def sem(name):
            sems.append(nc.alloc_semaphore(f"r_{name}"))
            return sems[-1]

        def sb(name, shape, dt=F32):
            return ctx.enter_context(nc.sbuf_tensor(f"r_{name}", shape, dt))

        def psum(name, shape):
            return ctx.enter_context(nc.psum_tensor(f"r_{name}", shape, F32))

        CH = SEQ // P
        GROUPS = HEADS // 4
        W = 4 * D
        score_bank = [psum(f"score{i}", [P, 4, P]) for i in range(2)]
        turn_bank = psum("turn", [P, 512])
        qk_bank, heads_bank = psum("qk", [P, 512]), psum("heads", [P, CH, 2 * D])
        v_bank = psum("v", [P, 2, 2 * D])
        out_bank = [psum(f"out{c}", [P, 2, P]) for c in range(CH)]

        m = dict(stats=sb("stats", [P, TILES, 6]), mean=sb("mean", [P, TILES]), var=sb("var", [P, TILES]),
                            diff=sb("diff", [P, TILES]), root=sb("root", [P, TILES]), rstd=sb("rstd", [P, TILES]),
                            var_done=sem("var_done"))
        qk_raw, qk_hi, qk_lo = sb("qk_raw", [P, W]), sb("qk_hi", [P, W], F32R), sb("qk_lo", [P, W], F32R)
        vg_raw, vg_hi, vg_lo = sb("vg_raw", [P, W]), sb("vg_hi", [P, W], F32R), sb("vg_lo", [P, W], F32R)
        o_raw, o_hi, o_lo = sb("o_raw", [P, 2 * D]), sb("o_hi", [P, 2 * D], F32R), sb("o_lo", [P, 2 * D], F32R)
        vg_bias, o_bias, qk_bias = sb("vg_bias", [P, W]), sb("o_bias", [P, D]), sb("qk_bias", [P, 4])
        turns = sb("turns", [P, 4, SEQ])
        mask = sb("mask", [P, HEADS, P])
        q_decay, k_decay, own_head = sb("q_decay", [P, P]), sb("k_decay", [P, P]), sb("own_head", [P, HEADS, VD])
        decays, head_of = sb("decays", [P, SEQ]), sb("head_of", [P, HEADS])

        xn = [sb(f"xn{p}", [P, CH, D]) for p in range(2)]
        x_hi, x_lo = sb("x_hi", [P, SEQ], F32R), sb("x_lo", [P, SEQ], F32R)
        q_part, q_turn = sb("q_part", [P, SEQ]), sb("q_turn", [P, SEQ])
        k_part, k_turn = sb("k_part", [P, SEQ]), sb("k_turn", [P, SEQ])
        q_all = sb("q_all", [P, SEQ])
        keys = [sb(f"keys{p}", [P, SEQ]) for p in range(2)]
        keys_hi, keys_lo = ([sb(f"keys_{k}{p}", [P, SEQ], F32R) for p in range(2)] for k in ("hi", "lo"))
        q_hi, q_lo = sb("q_hi", [P, SEQ], F32R), sb("q_lo", [P, SEQ])
        spread_hi, spread_lo = ([sb(f"spread_{k}{p}", [P, 4, SEQ], F32R) for p in range(2)] for k in ("hi", "lo"))
        q_dec = [sb(f"q_dec{p}", [P, P]) for p in range(2)]
        values = [sb(f"values{p}", [P, CH, HEADS // 2, 2, 2 * VD]) for p in range(2)]
        key_sums, sum_terms = sb("key_sums", [P, SEQ]), sb("sum_terms", [P, SEQ])
        out_turned = sb("out_turned", [P, CH, 2, P])
        g_raw = [sb(f"g_raw{p}", [P, CH, 2 * D]) for p in range(2)]
        g_act = [sb(f"g_act{p}", [P, CH, 2 * D]) for p in range(2)]
        probs = sb("probs", [P, CH, HEADS, P])
        k_dec, state = sb("k_dec", [P, P]), sb("state", [P, HEADS, VD])
        heads = [sb(f"heads{p}", [P, CH * HEADS, VD]) for p in range(2)]
        squares = sb("squares", [P, CH * HEADS, VD])
        bounded, clipped, square_sum, o_var, power, o_rstd, factor = (
            sb(name, [P, CH * HEADS]) for name in ("bounded", "clipped", "square_sum", "o_var", "power", "o_rstd",
                                                   "factor"))
        inverse, inverse2 = ([sb(f"{name}{p}", [P, CH * HEADS]) for p in range(2)] for name in ("inverse", "inverse2"))
        normed = sb("normed", [P, CH * HEADS, VD])
        gated = sb("gated", [P, CH * HEADS, VD])
        y_hi, y_lo = sb("y_hi", [P, CH * 2 * P], F32R), sb("y_lo", [P, CH * 2 * P], F32R)
        x_plus = [sb(f"x_plus{p}", [P, CH, D]) for p in range(2)]
        value_mean = sb("value_mean", [P, 2, HEADS])

        s = {n: sem(n) for n in (
            "weights", "tables", "rooted", "chain", "high", "split", "power_set", "zeros_set", "xn_done", "x_turned", "x_high",
            "x_split", "q_done", "k_done", "parts_done", "q_all_done", "keys_done", "spread_done", "q_high", "q_split", "keys_high", "keys_split", "q_dec_done",
            "v_done", "v_kept", "g_kept", "g_done", "scored", "masked", "k_turned", "k_dec_done", "state_done",
            "state_kept", "out0_done", "out_done", "out_kept", "heads_turned",
            "heads_kept", "key_sums_done", "sum_terms_done", "squared", "sum_bounded", "sum_clipped",
            "sum_inverted", "inverse_squared", "squares_summed", "var_scaled", "o_var_done", "rstd_done",
            "factor_done", "normed_done", "gated_done", "y_turned", "y_high", "y_split", "o_done", "x_plus_done",
            "added")}
        x_in = [sem(f"x_in{q}") for q in range(4)]

        ctx.callback(release, nc, sems)
        block = ctx.enter_context(nc.Block())
        a = t["a"]
        weights = ((qk_raw[:, :], a["w_qk"]), (vg_raw[:, :], a["w_vg"]), (o_raw[:, :], a["w_o"]),
                   (vg_bias[:, :], a["b_vg"]))
        tables = ((qk_bias[:, :], a["b_qk"]), (turns[:, :, :], a["turns"]), (o_bias[:, :], a["b_o"]),
                  (q_decay[:, :], a["q_decay"]), (k_decay[:, :], a["k_decay"]), (own_head[:, :, :], a["own_head"]),
                  (decays[:, :], a["decays"]), (head_of[:, :], a["head_of"]), (mask[:, :, :], a["mask"]))

        @block.sync
        def _(sp):
            for to, what in weights:
                sp.dma_start(to, what).then_inc(s["weights"], 16)
            n = TILES // 4
            for q in range(4):
                sp.dma_start(t["x"][:, q * n:q * n + n, :], src[q * n * P:(q + 1) * n * P, :]
                             .rearrange("(t p) d -> p t d", p=P)).then_inc(x_in[q], 16)
            for to, what in tables:
                sp.dma_start(to, what).then_inc(s["tables"], 16)

        @block.gpsimd
        def _(pool):
            pool.memset(power[:, :], -0.5).then_inc(s["power_set"], 1)
            for p in range(2):
                last = pool.memset(values[p][:, :, :, :, :], 0.0)
            last.then_inc(s["zeros_set"], 1)
            pool.wait_ge(s["tables"], 16 * len(tables))
            pool.wait_ge(s["power_set"], 1)

            def step(b, like):
                p = like % 2
                if 2 <= like:
                    pool.wait_ge(s["o_var_done"], b - 1)
                    pool.tensor_tensor(o_rstd[:, :], o_var[:, :], power[:, :], ALU.pow).then_inc(s["rstd_done"], 1)
                    pool.wait_ge(s["rstd_done"], b - 1)
                    wait_past(pool, s["normed_done"], b - 2)
                    pool.tensor_tensor(factor[:, :], o_rstd[:, :], inverse[p][:, :], ALU.mult).then_inc(s["factor_done"], 1)
                    wait_past(pool, s["added"], b - 3)
                    pool.tensor_tensor(x_plus[p][:, :, :], t["x"][:, bass.ds((b - 2) * CH, CH), :],
                                       o_bias[:, :].unsqueeze(1).to_broadcast([P, CH, D]), ALU.add
                                       ).then_inc(s["x_plus_done"], 1)
                if like < BATCH:
                    pool.wait_ge(s["q_high"], b + 1)
                    wait_past(pool, s["spread_done"], b)
                    pool.tensor_tensor(q_lo[:, :], q_all[:, :], q_hi[:, :].bitcast(F32), ALU.subtract
                                       ).then_inc(s["q_split"], 1)
                    pool.wait_ge(s["keys_high"], b + 1)
                    pool.tensor_tensor(keys_lo[p][:, :], keys[p][:, :], keys_hi[p][:, :].bitcast(F32), ALU.subtract
                                       ).then_inc(s["keys_split"], 1)
                    wait_past(pool, s["out_done"], b - 1)
                    pool.tensor_tensor(q_dec[p][:, :], q_all[:, P:SEQ], q_decay[:, :], ALU.mult
                                       ).then_inc(s["q_dec_done"], 1)
                    pool.wait_ge(s["key_sums_done"], b + 1)
                    wait_past(pool, s["k_turned"], b)
                    pool.tensor_tensor(sum_terms[:, :], q_all[:, :], key_sums[:, :], ALU.mult
                                       ).then_inc(s["sum_terms_done"], 1)

            run_batches(pool, step)

        @block.tensor
        def _(pe):
            pe.wait_ge(s["split"], 3)

            def turn_x(b, p):
                pe.wait_ge(s["xn_done"], b + 1)
                for c in range(CH):
                    last = pe.transpose(turn_bank[:, c * P:c * P + P], xn[p][:, c, :], t["ident"][:, :])
                last.then_inc(s["x_turned"], 1)

            turn_x(0, 0)

            def score(c, g, b, q):
                n = (b - 1) * (CH * GROUPS) + c * GROUPS + g
                wait_past(pe, s["masked"], n - 1)
                rows, cols = slice(32 * g, 32 * g + 32), slice(c * P, c * P + P)
                three_passes(pe, score_bank[g % 2][:, :, :], keys_hi[q][rows, cols], keys_lo[q][rows, cols],
                             spread_hi[q][rows, :, cols], spread_lo[q][rows, :, cols]).then_inc(s["scored"], 1)

            def outputs(c, first, b, q):
                pe.wait_ge(s["masked"], (b - 1) * (CH * GROUPS) + c * GROUPS + first // 4 + 1)
                if c == 1 and first % 8 == 0:
                    pe.matmul(out_bank[1][:, first // 8, :], state[:, first:first + 8, :].rearrange("p h v -> p (h v)"),
                              q_dec[q][:, :], start=True, stop=False, skip_group_check=True)
                for h in range(first, first + 4):
                    quad, half = h // 2 % 4 * 32, h // 8
                    last = pe.matmul(out_bank[c][quad:quad + 32, half, :], values[q][:, c, h // 2, h % 2, :],
                                     probs[:, c, h, :], start=c == 0 and h % 2 == 0, stop=h % 2 == 1,
                                     skip_group_check=True)
                return last

            def turn_heads(c, b):
                pe.wait_ge(s["out_kept"], (b - 1) * CH + c + 1)
                wait_past(pe, s["heads_kept"], (b - 1) * CH + c)
                for half in range(2):
                    last = pe.transpose(heads_bank[:, c, half * P:half * P + P], out_turned[:, c, half, :],
                                        t["ident"][:, :])
                last.then_inc(s["heads_turned"], 1)

            def step(b, like):
                p, q = like % 2, (like + 1) % 2
                new, mid, old, ahead = like < BATCH, 1 <= like <= BATCH, 2 <= like, like + 1 < BATCH

                def values_and_gates(c):
                    wait_past(pe, s["g_kept"], CH * b + c)
                    if c == 0:
                        wait_past(pe, s["added"], b - 2)
                    cols = slice(c * P, c * P + P)
                    three_passes(pe, v_bank[:, :, :].rearrange("p c n -> p (c n)"), x_hi[:, cols], x_lo[:, cols],
                                 vg_hi[:, :], vg_lo[:, :]).then_inc(s["v_done"], 1)

                if mid:
                    pe.wait_ge(s["keys_done"], b)
                    if new:
                        pe.wait_ge(s["x_split"], b + 1)
                    pe.wait_ge(s["sum_terms_done"], b)
                    pe.transpose(turn_bank[:, 0:P], keys[q][:, 0:P], t["ident"][:, :])
                    for c in range(CH):
                        last = pe.matmul(turn_bank[:, P + c * HEADS:P + (c + 1) * HEADS], sum_terms[:, c * P:(c + 1) * P],
                                         head_of[:, :], start=True, stop=True)
                    last.then_inc(s["k_turned"], 1)
                    pe.wait_ge(s["spread_done"], b)
                    pe.wait_ge(s["keys_split"], b)
                    score(0, 0, b, q)
                    score(0, 1, b, q)
                if new:
                    pe.wait_ge(s["x_split"], b + 1)
                    wait_past(pe, s["state_kept"], b - 1)
                    wait_past(pe, s["parts_done"], 2 * b)
                    for k in range(2):
                        cols = slice(k * D, (k + 1) * D)
                        last = three_passes(pe, qk_bank[:, k * SEQ:(k + 1) * SEQ], qk_hi[:, cols], qk_lo[:, cols], x_hi[:, :], x_lo[:, :])
                    last.then_inc(s["q_done"], 1)
                if mid:
                    score(0, 2, b, q)
                if new:
                    values_and_gates(0)
                if mid:
                    score(0, 3, b, q)
                if new:
                    pe.wait_ge(s["parts_done"], 2 * b + 1)
                    for k in range(2):
                        cols = slice((2 + k) * D, (3 + k) * D)
                        last = three_passes(pe, qk_bank[:, k * SEQ:(k + 1) * SEQ], qk_hi[:, cols], qk_lo[:, cols], x_hi[:, :], x_lo[:, :])
                    last.then_inc(s["k_done"], 1)
                if mid:
                    outputs(0, 0, b, q)
                    score(1, 0, b, q)
                    outputs(0, 4, b, q)
                    score(1, 1, b, q)
                    outputs(0, 8, b, q)
                    pe.wait_ge(s["k_dec_done"], b)
                    pe.wait_ge(s["v_kept"], CH * b)
                    if new:
                        pe.wait_ge(s["parts_done"], 2 * b + 2)
                    pe.matmul(qk_bank[:, 0:HEADS * VD], k_dec[:, :], own_columns(values[q], 0),
                              start=True, stop=True).then_inc(s["state_done"], 1)
                    score(1, 2, b, q)
                    outputs(0, 12, b, q).then_inc(s["out0_done"], 1)
                    score(1, 3, b, q)
                if new:
                    values_and_gates(1)
                if mid:
                    turn_heads(0, b)
                if old:
                    pe.wait_ge(s["gated_done"], b - 1)
                    if mid:
                        pe.wait_ge(s["sum_clipped"], b)
                    for k in range(CH * 2):
                        last = pe.transpose(turn_bank[:, k * P:k * P + P],
                                            gated[:, :, :].rearrange("p h v -> p (h v)")[:, k * P:k * P + P],
                                            t["ident"][:, :])
                    last.then_inc(s["y_turned"], 1)
                if mid:
                    pe.wait_ge(s["state_kept"], b)
                    pe.wait_ge(s["q_dec_done"], b)
                    outputs(1, 0, b, q)
                if mid:
                    outputs(1, 4, b, q)
                    outputs(1, 8, b, q)
                if ahead:
                    if old:
                        pe.wait_ge(s["y_split"], b - 1)
                    elif mid:
                        pe.wait_ge(s["sum_clipped"], b)
                    else:
                        pe.wait_ge(s["x_split"], b + 1)
                    turn_x(b + 1, q)
                if mid:
                    outputs(1, 12, b, q).then_inc(s["out_done"], 1)
                if old:
                    pe.wait_ge(s["y_split"], b - 1)
                    if new:
                        pe.wait_ge(s["g_kept"], CH * (b + 1))
                    wait_past(pe, s["added"], b - 2)
                    for c in range(CH):
                        for half in range(2):
                            k = c * 2 + half
                            cols, w = slice(k * P, k * P + P), slice(half * D, half * D + D)
                            last = three_passes(pe, v_bank[:, 0, c * D:(c + 1) * D], y_hi[:, cols], y_lo[:, cols],
                                                o_hi[:, w], o_lo[:, w], start=half == 0, stop=half == 1)
                    last.then_inc(s["o_done"], 1)
                if mid:
                    turn_heads(1, b)

            run_batches(pe, step)

        @block.scalar
        def _(act):
            act.wait_ge(s["weights"], 16 * len(weights))
            act.copy(qk_hi[:, :], qk_raw[:, :]).then_inc(s["high"], 1)
            act.copy(o_hi[:, :], o_raw[:, :]).then_inc(s["high"], 1)
            act.wait_ge(m["var_done"], 1)
            act.activation(m["root"][:, :], m["var"][:, :], ACT.Sqrt).then_inc(s["rooted"], 1)

            def high_x(b):
                act.wait_ge(s["x_turned"], b + 1)
                wait_past(act, s["v_done"], CH * b)
                act.copy(x_hi[:, :], turn_bank[:, 0:SEQ]).then_inc(s["x_high"], 1)

            high_x(0)

            def spread_out(spread, source):
                for j in range(4):
                    last = act.mul(spread[:, j, :], source[:, :], t["const"][:, C_HEAD + j:C_HEAD + j + 1])
                return last

            def keep_out(c, b):
                act.wait_ge(s["out_done" if c else "out0_done"], b)
                wait_past(act, s["heads_turned"], (b - 2) * CH + c + 1)
                act.copy(out_turned[:, c, :, :], out_bank[c][:, :, :]).then_inc(s["out_kept"], 1)

            def keep_heads(c, b, p):
                act.wait_ge(s["heads_turned"], (b - 1) * CH + c + 1)
                if c == 0:
                    wait_past(act, s["normed_done"], b - 2)
                act.copy(heads[p][:, c * HEADS:(c + 1) * HEADS, :].rearrange("p h v -> p (h v)"), heads_bank[:, c, :]
                         ).then_inc(s["heads_kept"], 1)

            def step(b, like):
                p, q = like % 2, (like + 1) % 2
                if 2 <= like:
                    keep_heads(1, b - 1, p)
                    act.wait_ge(s["heads_kept"], CH * (b - 1))
                    wait_past(act, s["squares_summed"], b - 2)
                    act.activation(squares[:, :, :], heads[p][:, :, :], ACT.Square).then_inc(s["squared"], 1)
                if like < BATCH:
                    act.wait_ge(s["q_all_done"], b + 1)
                    wait_past(act, s["scored"], (b - 1) * (CH * GROUPS))
                    act.copy(q_hi[:, :], q_all[:, :]).then_inc(s["q_high"], 1)
                    spread_out(spread_hi[p], q_all)
                    act.wait_ge(s["keys_done"], b + 1)
                    act.copy(keys_hi[p][:, :], keys[p][:, :]).then_inc(s["keys_high"], 1)
                if 1 <= like <= BATCH:
                    keep_out(0, b)
                if like < BATCH:
                    act.wait_ge(s["q_split"], b + 1)
                    spread_out(spread_lo[p], q_lo).then_inc(s["spread_done"], 1)
                if 1 <= like <= BATCH:
                    keep_heads(0, b, q)
                if like >= 2:
                    act.wait_ge(s["y_turned"], b - 1)
                    wait_past(act, s["o_done"], b - 2)
                    act.copy(y_hi[:, :], turn_bank[:, :]).then_inc(s["y_high"], 1)
                if like + 1 < BATCH:
                    high_x(b + 1)
                if like < BATCH:
                    act.wait_ge(s["g_kept"], CH * (b + 1))
                    wait_past(act, s["gated_done"], b - 1)
                    act.activation(g_act[p][:, :, :], g_raw[p][:, :, :], ACT.Silu).then_inc(s["g_done"], 1)
                if 1 <= like <= BATCH:
                    keep_out(1, b)

            run_batches(act, step)

        @block.vector
        def _(dve):
            chain = Chain(dve, s["chain"])
            dve.wait_ge(s["weights"], 16 * len(weights))
            per_head = [v[:, 0:2 * D].rearrange("p (h v) -> p h v", v=VD) for v in (vg_raw, vg_bias)]
            for k, part in enumerate(per_head):
                last = dve.tensor_reduce(value_mean[:, k, :], part, AX.X, ALU.add)
            chain.then(last)
            for k, part in enumerate(per_head):
                last = dve.scalar_tensor_tensor(out=part, in0=value_mean[:, k, :].unsqueeze(2).to_broadcast([P, HEADS, VD]),
                                                scalar=-1.0 / VD, in1=part, op0=ALU.mult, op1=ALU.add)
            chain.then(last)
            chain.then(dve.tensor_copy(vg_hi[:, :], vg_raw[:, :]))
            dve.wait_ge(s["high"], 2)
            for hi, lo, raw in ((qk_hi, qk_lo, qk_raw), (vg_hi, vg_lo, vg_raw), (o_hi, o_lo, o_raw)):
                dve.tensor_tensor(lo[:, :], raw[:, :], hi[:, :].bitcast(F32), ALU.subtract).then_inc(s["split"], 1)

            def normalise_batch(b, p):
                wait_past(dve, s["x_turned"], b - 1)
                for c in range(CH):
                    last = normalise(dve, xn[p][:, c, :], t["x"], b * CH + c, m)
                last.then_inc(s["xn_done"], 1)

            def low_x(b):
                dve.wait_ge(s["x_high"], b + 1)
                dve.tensor_tensor(x_lo[:, :], turn_bank[:, 0:SEQ], x_hi[:, :].bitcast(F32), ALU.subtract
                                  ).then_inc(s["x_split"], 1)

            layernorm_stats(dve, s["rooted"], chain, t["x"], m, x_in)
            dve.wait_ge(s["zeros_set"], 1)
            normalise_batch(0, 0)
            normalise_batch(1, 1)
            low_x(0)
            dve.wait_ge(s["tables"], 16 * len(tables))

            def masks(c, g, b):
                n = (b - 1) * (CH * GROUPS) + c * GROUPS + g
                dve.wait_ge(s["scored"], n + 1)
                if g == 0:
                    wait_past(dve, s["out_done" if c else "out0_done"], b - 1)
                dve.tensor_tensor(probs[:, c, 4 * g:4 * g + 4, :], score_bank[g % 2][:, :, :],
                                  mask[:, 4 * g:4 * g + 4, :], ALU.mult).then_inc(s["masked"], 1)

            def turned(b, first, done, parts):
                dve.wait_ge(done, b + 1)
                for k, to in enumerate(parts):
                    w = first + k
                    last = dve.scalar_tensor_tensor(out=to[:, :], in0=qk_bank[:, k * SEQ:(k + 1) * SEQ],
                                                    scalar=qk_bias[:, w:w + 1], in1=turns[:, w, :],
                                                    op0=ALU.add, op1=ALU.mult)
                last.then_inc(s["parts_done"], 1)

            def keep_values(c, b, p):
                if c == 0:
                    wait_past(dve, s["out_done"], b - 1)
                    wait_past(dve, s["g_done"], b - 1)
                dve.wait_ge(s["v_done"], CH * b + c + 1)
                dve.tensor_tensor(own_columns(values[p], c),
                                  v_bank[:, 0, :].rearrange("p (h j v) -> p h j v", j=2, v=VD),
                                  vg_bias[:, 0:2 * D].rearrange("p (h j v) -> p h j v", j=2, v=VD), ALU.add
                                  ).then_inc(s["v_kept"], 1)
                dve.tensor_tensor(g_raw[p][:, c, :], v_bank[:, 1, :], vg_bias[:, 2 * D:], ALU.add
                                  ).then_inc(s["g_kept"], 1)

            def step(b, like):
                p, q = like % 2, (like + 1) % 2
                new, mid, old = like < BATCH, 1 <= like <= BATCH, 2 <= like
                if mid:
                    sums = turn_bank[:, P:P + CH * HEADS]
                    dve.wait_ge(s["k_turned"], b)
                    dve.tensor_scalar(bounded[:, :], sums, 1.0, None, ALU.max).then_inc(s["sum_bounded"], 1)
                    wait_past(dve, s["state_done"], b - 1)
                    dve.tensor_tensor(k_dec[:, :], turn_bank[:, 0:P], k_decay[:, :], ALU.mult).then_inc(s["k_dec_done"], 1)
                    dve.wait_ge(s["sum_bounded"], b)
                    dve.scalar_tensor_tensor(out=clipped[:, :], in0=sums, scalar=-1.0, in1=bounded[:, :],
                                             op0=ALU.mult, op1=ALU.max).then_inc(s["sum_clipped"], 1)
                    masks(0, 0, b)
                if old:
                    dve.wait_ge(s["squared"], b - 1)
                    dve.tensor_reduce(square_sum[:, :], squares[:, :, :], AX.X, ALU.add).then_inc(s["squares_summed"], 1)
                if mid:
                    masks(0, 1, b)
                if old:
                    dve.wait_ge(s["squares_summed"], b - 1)
                    dve.wait_ge(s["inverse_squared"], b - 1)
                    dve.scalar_tensor_tensor(out=square_sum[:, :], in0=square_sum[:, :], scalar=1.0 / VD,
                                             in1=inverse2[p][:, :], op0=ALU.mult, op1=ALU.mult).then_inc(s["var_scaled"], 1)
                    dve.wait_ge(s["var_scaled"], b - 1)
                    wait_past(dve, s["rstd_done"], b - 2)
                    dve.tensor_scalar(o_var[:, :], square_sum[:, :], EPS, None, ALU.add).then_inc(s["o_var_done"], 1)
                if new:
                    turned(b, 0, s["q_done"], (q_part, q_turn))
                if mid:
                    masks(0, 2, b)
                if new:
                    dve.wait_ge(s["parts_done"], 2 * b + 1)
                    wait_past(dve, s["sum_terms_done"], b)
                    wait_past(dve, s["spread_done"], b)
                    dve.tensor_tensor(q_all[:, :], q_part[:, :], q_turn[:, :], ALU.add).then_inc(s["q_all_done"], 1)
                if new:
                    keep_values(0, b, p)
                if mid:
                    masks(0, 3, b)
                if new:
                    turned(b, 2, s["k_done"], (k_part, k_turn))
                if mid:
                    masks(1, 0, b)
                if new:
                    dve.wait_ge(s["parts_done"], 2 * b + 2)
                    wait_past(dve, s["out_done"], b - 1)
                    dve.tensor_tensor(keys[p][:, :], k_part[:, :], k_turn[:, :], ALU.add).then_inc(s["keys_done"], 1)
                if mid:
                    masks(1, 1, b)
                if old:
                    dve.wait_ge(s["factor_done"], b - 1)
                    wait_past(dve, s["gated_done"], b - 2)
                    dve.tensor_tensor(normed[:, :, :], heads[p][:, :, :],
                                      factor[:, :].unsqueeze(2).to_broadcast([P, CH * HEADS, VD]), ALU.mult
                                      ).then_inc(s["normed_done"], 1)
                if mid:
                    dve.wait_ge(s["state_done"], b)
                    dve.tensor_tensor(state[:, :, :].rearrange("p h v -> p (h v)"),
                                      qk_bank[:, 0:HEADS * VD],
                                      own_head[:, :, :].rearrange("p h v -> p (h v)"), ALU.mult
                                      ).then_inc(s["state_kept"], 1)
                    masks(1, 2, b)
                    dve.wait_ge(s["sum_clipped"], b)
                    wait_past(dve, s["factor_done"], b - 2)
                    dve.reciprocal(inverse[q][:, :], clipped[:, :]).then_inc(s["sum_inverted"], 1)
                if old:
                    dve.wait_ge(s["normed_done"], b - 1)
                    dve.wait_ge(s["g_done"], b - 1)
                    wait_past(dve, s["y_turned"], b - 2)
                    dve.tensor_tensor(gated[:, :, :].rearrange("p h v -> p (h v)"),
                                      normed[:, :, :].rearrange("p h v -> p (h v)"),
                                      g_act[p][:, :, :].rearrange("p c n -> p (c n)"), ALU.mult
                                      ).then_inc(s["gated_done"], 1)
                if mid:
                    dve.wait_ge(s["sum_inverted"], b)
                    dve.tensor_tensor(inverse2[q][:, :], inverse[q][:, :], inverse[q][:, :], ALU.mult
                                      ).then_inc(s["inverse_squared"], 1)
                    masks(1, 3, b)
                if new:
                    keep_values(1, b, p)
                if new:
                    dve.wait_ge(s["keys_done"], b + 1)
                    wait_past(dve, s["sum_terms_done"], b)
                    dve.tensor_tensor_scan(key_sums[:, :], decays[:, :], keys[p][:, :], 0.0, ALU.mult, ALU.add
                                           ).then_inc(s["key_sums_done"], 1)
                if like + 2 < BATCH:
                    normalise_batch(b + 2, p)
                if old:
                    dve.wait_ge(s["y_high"], b - 1)
                    dve.tensor_tensor(y_lo[:, :], turn_bank[:, :], y_hi[:, :].bitcast(F32), ALU.subtract
                                      ).then_inc(s["y_split"], 1)
                if like + 1 < BATCH:
                    low_x(b + 1)
                if old:
                    dve.wait_ge(s["o_done"], b - 1)
                    dve.wait_ge(s["x_plus_done"], b - 1)
                    dve.tensor_tensor(t["x"][:, bass.ds((b - 2) * CH, CH), :], v_bank[:, 0, :].rearrange("p (c d) -> p c d", c=CH),
                                      x_plus[p][:, :, :], ALU.add).then_inc(s["added"], 1)

            run_batches(dve, step)


def program(nc, a, out):
    with ExitStack() as ctx:
        def sb(name, shape, dt=F32):
            return ctx.enter_context(nc.sbuf_tensor(name, shape, dt))

        def sem(name):
            return ctx.enter_context(nc.semaphore(name))

        t = dict(
            x=sb("x", [P, TILES, D]), padding=sb("padding", [P, UT, ROW]), ident=sb("ident", [P, P]), earlier=sb("earlier", [P, P]),
            ones=sb("ones", [P, 2 * HEADS]), const=sb("const", [P, C_COLS]), n_tables=3,
            x_loaded=[sem(f"x_loaded{q}") for q in range(4)], tables_loaded=sem("tables_loaded"),
            scattered=[nc.dram_tensor(f"scattered{f}", (ROUTED_UNITS * UNIT, ROW), F32, kind="Internal").ap()
                       for f in range(2)],
            experts=a["experts"], router_w=a["router_w"], router_b=a["router_b"], a=a)
        middle = nc.dram_tensor("middle", (DST_ROWS, D), F32, kind="Internal").ap()
        padding = t["padding"]
        padding_set, ones_set = sem("padding_set"), sem("ones_set")
        with nc.Block() as block:
            @block.sync
            def _(sp):
                sp.dma_start(t["ident"][:, :], a["ident"]).then_inc(t["tables_loaded"], 16)
                sp.dma_start(t["earlier"][:, :], a["earlier"]).then_inc(t["tables_loaded"], 16)
                sp.dma_start(t["const"][:, :], a["const"]).then_inc(t["tables_loaded"], 16)
                n = TILES // 4
                for q in range(4):
                    sp.dma_start(t["x"][:, q * n:q * n + n, :], a["x"][q * n * P:(q + 1) * n * P, :]
                                 .rearrange("(t p) d -> p t d", p=P)).then_inc(t["x_loaded"][q], 16)

            @block.vector
            def _(dve):
                dve.memset(padding[:, :, 0:D + 1], 0.0).then_inc(padding_set, 1)
                dve.wait_ge(t["tables_loaded"], 16 * t["n_tables"])
                dve.tensor_scalar(padding[:, :, D + 1], t["const"][:, C_ID:C_ID + UT], float(TOKENS), None, ALU.add
                                  ).then_inc(padding_set, 1)
                dve.memset(t["ones"][:, :], 1.0).then_inc(ones_set, 1)

        moe(nc, t, 0, middle)
        retention(nc, t, middle)
        moe(nc, t, 1, out)


def tables():
    import numpy as np

    p = np.arange(P)
    const = np.zeros((P, C_COLS), np.float32)
    const[:, C_ID:C_ID + TILES] = p[:, None] + P * np.arange(TILES)
    const[:, C_REV:C_REV + EXPERTS] = EXPERTS - np.arange(EXPERTS)
    const[:, C_STEP:C_STEP + EXPERTS] = UNIT * np.arange(EXPERTS)
    const[:, C_UNIT:C_UNIT + ROUTED_UNITS] = np.arange(ROUTED_UNITS)
    const[:, C_HEAD:C_HEAD + 4] = (p[:, None] % 32) // KD == np.arange(4)
    head = np.arange(HEADS)
    angle = np.repeat((1.0 / 10000.0 ** np.linspace(0.0, 1.0, KD // 2, dtype=np.float32)).astype(np.float32), 2)
    at = np.arange(SEQ, dtype=np.float32)
    sin, cos = np.sin(at[None, :] * angle[:, None]), np.cos(at[None, :] * angle[:, None])
    sin = sin * np.where(np.arange(KD) % 2 == 0, -1.0, 1.0)[:, None]
    scaling = KD ** -0.5
    decay = np.log(1.0 - 2.0 ** (-5.0 - head))
    apart = np.arange(SEQ)[:, None] - np.arange(SEQ)[None, :]
    full = np.where(apart >= 0, np.exp(decay[:, None, None] * apart), 0.0)
    norm = np.repeat(1.0 / np.sqrt(full.sum(-1)), KD, axis=0)
    turns = np.tile(cos, (HEADS, 1)), np.tile(sin, (HEADS, 1))
    turns = np.stack([turns[0] * norm, turns[1] * norm, turns[0] * scaling, turns[1] * scaling], axis=1)
    mask = full[:, 0:P, 0:P].transpose(2, 0, 1)
    of_row = p // KD
    q_decay = np.exp(decay[of_row][:, None] * p[None, :])
    k_decay = np.exp(decay[of_row][None, :] * (P - p[:, None]))
    head_of = of_row[:, None] == head[None, :]
    out = {"turns": turns, "mask": mask, "q_decay": q_decay, "k_decay": k_decay, "head_of": head_of,
           "own_head": np.repeat(head_of[:, :, None], VD, axis=2),
           "decays": np.broadcast_to(np.exp(decay[of_row])[:, None], (P, SEQ))}
    out = {k: v.astype(np.float32) for k, v in out.items()} | {"ident": np.eye(P, dtype=np.float32), "earlier": (p[:, None] < p[None, :]).astype(np.float32),
           "const": const}
    return out


def kernel(**inputs):
    import numpy as np
    import concourse.bacc as bacc
    from concourse.bass_utils import run_bass_kernel_spmd as run

    i = {k.replace("L0_", ""): np.asarray(v) for k, v in inputs.items()}

    def expert_rows(w1, b1, w2, b2):
        return np.concatenate([w2.T.reshape(CHUNKS, P, D).transpose(1, 0, 2).reshape(P, FF), w1.T,
                               b1.reshape(CHUNKS, P).T, b2[:, None]], axis=1)

    experts = [expert_rows(i["ffn_spec_w1"][e], i["ffn_spec_b1"][e], i["ffn_spec_w2"][e], i["ffn_spec_b2"][e])
               for e in range(EXPERTS)]
    experts.append(expert_rows(i["ffn_shared_w1"], i["ffn_shared_b1"], i["ffn_shared_w2"], i["ffn_shared_b2"]))
    swap = np.arange(D) ^ 1
    arrays = {
        "x": i["attn_x"].reshape(TOKENS, D),
        "experts": np.stack(experts),
        "router_w": i["ffn_router_w"].T,
        "router_b": np.broadcast_to(i["ffn_router_b"], (P, EXPERTS)),
        "w_qk": np.concatenate([i["attn_Wq"], i["attn_Wq"][:, swap], i["attn_Wk"], i["attn_Wk"][:, swap]], axis=1),
        "b_qk": np.stack([i["attn_bq"], i["attn_bq"][swap], i["attn_bk"], i["attn_bk"][swap]], axis=1),
        "w_vg": np.concatenate([i["attn_Wv"], i["attn_Wg"]], axis=1),
        "b_vg": np.broadcast_to(np.concatenate([i["attn_bv"], i["attn_bg"]]), (P, 4 * D)),
        "w_o": i["attn_Wo"].reshape(2, P, D).transpose(1, 0, 2).reshape(P, 2 * D),
        "b_o": np.broadcast_to(i["attn_bo"], (P, D)),
        **tables(),
    }
    nc = bacc.Bacc("TRN2", target_bir_lowering=False, num_devices=1)
    arrays = {f"in_{k}": np.ascontiguousarray(v) for k, v in arrays.items()}
    a = {k[3:]: nc.dram_tensor(k, v.shape, mybir.dt.from_np(v.dtype), kind="ExternalInput").ap()
         for k, v in arrays.items()}
    out = nc.dram_tensor("out", (DST_ROWS, D), F32, kind="ExternalOutput").ap()
    program(nc, a, out)
    result = run(nc, [arrays], core_ids=[0])
    return result.results[0]["out"][:TOKENS].reshape(BATCH, SEQ, D)
```

```python
from contextlib import ExitStack

import concourse.bass as bass
from concourse import mybir

F32, F32R, I32 = mybir.dt.float32, mybir.dt.float32r, mybir.dt.int32
ALU, ACT, AX = mybir.AluOpType, mybir.ActivationFunctionType, mybir.AxisListType

P = 128
BATCH, SEQ, D = 16, 256, 128
TOKENS = BATCH * SEQ
TILES = TOKENS // P
FF, EXPERTS, TOP = 512, 8, 2
CHUNKS = FF // P
UNIT = 512
UT = UNIT // P
SHARED_UNITS = TOKENS // UNIT
ROUTED_UNITS = (TOP * TOKENS + EXPERTS * (UNIT - 1)) // UNIT
UNITS = SHARED_UNITS + ROUTED_UNITS
REGION = TOKENS + UNIT
PAD_UNIT = EXPERTS * REGION
GROUPS = ((0, 3), (3, 8))
ROW = D + 2
DST_ROWS = TOKENS + UNIT
W_COLS = 2 * FF + CHUNKS + 1
HEADS, KD, VD = 16, 8, 16
V1 = VD + 1
EPS = 1e-5
C_ID, C_REV, C_STEP, C_REGION, C_UNIT, C_HEAD = (
    0, TILES, TILES + EXPERTS, TILES + 2 * EXPERTS, TILES + 3 * EXPERTS, TILES + 3 * EXPERTS + 32)
C_COLS = C_HEAD + 4


def group(g):
    first, end = GROUPS[g][0] * UT, GROUPS[g][1] * UT
    return first, end - first, slice(first, end)


def wait_past(eng, sem, value):
    if not isinstance(value, int) or value > 0:
        eng.wait_ge(sem, value)


def release(nc, sems):
    nc.clear_and_free_semaphores(sems)
    nc.all_engine_barrier()


class Chain:

    def __init__(self, eng, sem):
        self.eng, self.sem, self.count = eng, sem, 0

    def then(self, instruction):
        self.count += 1
        instruction.then_inc(self.sem, 1)
        self.eng.wait_ge(self.sem, self.count)


def three_passes(pe, out, w_hi, w_lo, x_hi, x_lo, start=True, stop=True):
    pe.matmul(out, w_hi, x_hi, start=start, stop=False)
    pe.matmul(out, w_hi, x_lo, start=False, stop=False)
    return pe.matmul(out, w_lo, x_hi, start=False, stop=stop)


def quarter(q):
    n = TILES // 4
    return slice(q * n, (q + 1) * n)


def row_stats(dve, chain, x, m, q, arrived=None):
    if arrived:
        dve.wait_ge(arrived, 16)
    k = quarter(q)
    for tile in range(k.start, k.stop):
        last = dve.bn_stats(m["stats"][:, tile, :], x[:, tile, :])
    chain.then(last)
    even_mean, even_cv, odd_mean, odd_cv = (m["stats"][:, k, c] for c in (1, 2, 4, 5))
    mean, var, diff = m["mean"][:, k], m["var"][:, k], m["diff"][:, k]
    dve.tensor_tensor(diff, even_mean, odd_mean, ALU.subtract)
    dve.tensor_tensor(mean, even_mean, odd_mean, ALU.add)
    chain.then(dve.tensor_tensor(var, even_cv, odd_cv, ALU.add))
    chain.then(dve.tensor_tensor(diff, diff, diff, ALU.mult))
    chain.then(dve.scalar_tensor_tensor(out=var, in0=var, scalar=4.0 / D, in1=diff, op0=ALU.mult, op1=ALU.add))
    dve.tensor_scalar(mean, mean, 0.5, None, ALU.mult)
    dve.tensor_scalar(var, var, 0.25, EPS, ALU.mult, ALU.add).then_inc(m["var_done"], 1)


def row_scale(pool, t, m, q):
    pool.wait_ge(m["var_done"], q + 1)
    pool.tensor_tensor(m["rstd"][:, quarter(q)], m["var"][:, quarter(q)], t["power"][:, :], ALU.pow
                       ).then_inc(m["rstd_done"], 1)


def normalise(dve, out, x, tile, m):
    return dve.tensor_scalar(out, x[:, bass.ds(tile, 1), :].rearrange("p t d -> p (t d)"),
                             m["mean"][:, bass.ds(tile, 1)], m["rstd"][:, bass.ds(tile, 1)], ALU.subtract, ALU.mult)


def run_steps(eng, step):
    a, b = 4, SHARED_UNITS - 2
    c = SHARED_UNITS + 4
    d = c + (UNITS - 1 - c) // 2 * 2
    for u in range(a):
        step(u, u)
    with eng.Fori(a // 2, b // 2) as pair:
        for j in range(2):
            step(pair * 2 + j, a + j)
    for u in range(b, c):
        step(u, u)
    with eng.Fori(c // 2, d // 2) as pair:
        for j in range(2):
            step(pair * 2 + j, c + j)
    for u in range(d, UNITS + 2):
        step(u, u)


def moe(nc, t, f, dst):
    scattered = t["scattered"][f]
    with ExitStack() as ctx:
        sems = []

        def sem(name):
            sems.append(nc.alloc_semaphore(f"m{f}_{name}"))
            return sems[-1]

        def sb(name, shape, dt=F32):
            return ctx.enter_context(nc.sbuf_tensor(f"m{f}_{name}", shape, dt))

        bank = [ctx.enter_context(nc.psum_tensor(f"m{f}_bank{i}", [P, UNIT], F32)) for i in range(8)]
        up_bank, down_bank, y_bank, x_bank = bank[0:4], bank[4:6], bank[6], bank[7]

        m = dict(stats=sb("stats", [P, TILES, 6]), mean=sb("mean", [P, TILES]), var=sb("var", [P, TILES]),
                            diff=sb("diff", [P, TILES]), rstd=sb("rstd", [P, TILES]),
                            var_done=sem("var_done"), rstd_done=sem("rows_rstd_done"))
        xn = [sb(f"xn{p}", [P, UT, D]) for p in range(2)]
        x_t = [sb(f"x_t{p}", [P, UNIT]) for p in range(2)]
        x_t_all = sb("x_t_all", [P, SHARED_UNITS, UNIT])
        rows_out = sb("rows_out", [P, TILES, ROW])
        logits = sb("logits", [P, TILES, EXPERTS])
        prob = sb("prob", [P, TILES, EXPERTS])
        rest = sb("rest", [P, TILES, EXPERTS])
        score = sb("score", [P, TILES, EXPERTS])
        chosen = [sb(f"chosen{k}", [P, TILES, EXPERTS]) for k in range(TOP)]
        both = sb("both", [P, TILES, EXPERTS], F32R)
        best = sb("best", [P, TILES])
        top = [sb(f"top{k}", [P, TILES]) for k in range(TOP)]
        gate = [sb(f"gate{k}", [P, TILES]) for k in range(TOP)]
        before = sb("before", [P, TILES, EXPERTS])
        count_of, units_of, end_of, base_of = (sb(f"{name}_of", [P, EXPERTS]) for name in ("count", "units", "end", "base"))
        over = sb("over", [P, EXPERTS, EXPERTS])
        passed = sb("passed", [P, ROUTED_UNITS, EXPERTS])
        moved = sb("moved", [P, ROUTED_UNITS, EXPERTS - 1])
        expert_f, row_f, row_left = (sb(name, [P, ROUTED_UNITS]) for name in ("expert_f", "row_f", "row_left"))
        expert_of, row_of = sb("expert_of", [P, ROUTED_UNITS], I32), sb("row_of", [P, ROUTED_UNITS], I32)
        next_row, fill_row = sb("next_row", [P, EXPERTS]), sb("fill_row", [P, EXPERTS], I32)
        place_f = [sb(f"place_f{k}", [P, TILES]) for k in range(TOP)]
        place = [sb(f"place{k}", [P, TILES], I32) for k in range(TOP)]
        w1_raw = [sb(f"w1_raw{p}", [P, W_COLS - FF]) for p in range(2)]
        w2_raw = [sb(f"w2_raw{p}", [P, FF]) for p in range(2)]
        w_hi = [sb(f"w_hi{p}", [P, 2, FF], F32R) for p in range(2)]
        w_lo = [sb(f"w_lo{p}", [P, 2, FF], F32R) for p in range(2)]
        sh_raw, sh_hi, sh_lo = sb("sh_raw", [P, W_COLS]), sb("sh_hi", [P, 2, FF], F32R), sb("sh_lo", [P, 2, FF], F32R)
        bias_of = sb("bias_of", [P, ROUTED_UNITS, CHUNKS + 1])
        tail_of = sb("tail_of", [P, ROUTED_UNITS, UT, 2])
        rows = [sb(f"rows{p}", [P, UT, ROW]) for p in range(2)]
        x_hi = [sb(f"x_hi{p}", [P, UNIT], F32R) for p in range(2)]
        x_lo = [sb(f"x_lo{p}", [P, UNIT], F32R) for p in range(2)]
        h = sb("h", [P, CHUNKS, UNIT])
        h_hi = sb("h_hi", [P, 2, CHUNKS, UNIT], F32R)
        h_lo = sb("h_lo", [P, 2, CHUNKS, UNIT], F32R)
        y_t = [sb(f"y_t{p}", [P, UNIT]) for p in range(2)]
        y = [sb(f"y{p}", [P, UT, D]) for p in range(2)]
        number = [sb(f"number{p}", [P, UT], I32) for p in range(2)]
        turn = sb("turn", [1, 1 + ROUTED_UNITS])
        router_w = sb("router_w", [P, EXPERTS])
        router_b = sb("router_b", [P, EXPERTS])
        earlier = sb("earlier", [P, P], F32R)
        ones = sb("ones", [P, P], F32R)

        s = {n: sem(n) for n in (
            "params", "casts", "chain", "xn_done", "xn_turned", "xt_out", "xt_kept", "logit_done",
            "logit_kept", "row_kept", "shifted", "exped", "both_done", "prefixed", "gates_done", "places_done",
            "experts_done", "gate2_done", "scatter1", "sh_loaded", "sh_hi", "sh_split",
            "x_turned", "x_high", "x_split", "w1_high", "w1_split", "w2_high", "w2_split", "up_done", "gelu_done",
            "h_high", "h_split", "down_done", "yt_done", "y_turned", "y_done", "tail_kept", "bias_kept", "y_added", "turn_set", "number_done", "filled")}
        scatter0 = [sem(f"scatter0{half}") for half in range(2)]
        w1_loaded = [sem(f"w1_loaded{p}") for p in range(2)]
        w2_loaded = [sem(f"w2_loaded{p}") for p in range(2)]
        rows_loaded = [sem(f"rows_loaded{p}") for p in range(2)]
        y_stored = [sem(f"y_stored{p}") for p in range(2)]

        ctx.callback(release, nc, sems)
        block = ctx.enter_context(nc.Block())

        @block.sync
        def _(sp):
            sp.dma_start(router_w[:, :], t["router_w"]).then_inc(s["params"], 16)
            sp.dma_start(router_b[:, :], t["router_b"]).then_inc(s["params"], 16)
            sp.dma_start(sh_raw[:, :], t["experts"][EXPERTS]).then_inc(s["sh_loaded"], 16)

            sp.dma_start(scattered[PAD_UNIT:PAD_UNIT + UNIT, :].rearrange("(j p) c -> p j c", p=P),
                         t["padding"][:, :, :]).then_inc(s["filled"], 16)
            sp.dma_start(dst[TOKENS:DST_ROWS, :].rearrange("(j p) d -> p j d", p=P), t["padding"][:, :, 0:D]
                         ).then_inc(s["filled"], 16)

            def load_w1(r, p):
                e = expert(r)
                wait_past(sp, s["bias_kept"], r - 1)
                wait_past(sp, s["w1_split"], r - 1)
                sp.dma_start(w1_raw[p][:, :], t["experts"][bass.ds(e, 1), :, FF:].rearrange("e p c -> (e p) c")
                             ).then_inc(w1_loaded[p], 16)

            def load_w2(r, p):
                e = expert(r)
                wait_past(sp, s["w2_split"], r - 1)
                sp.dma_start(w2_raw[p][:, :], t["experts"][bass.ds(e, 1), :, 0:FF].rearrange("e p c -> (e p) c")
                             ).then_inc(w2_loaded[p], 16)

            def load_rows(r, p):
                wait_past(sp, s["tail_kept"], r - 1)
                wait_past(sp, s["x_turned"], r - 1)
                first = sp.value_load(row_of[0:1, bass.ds(r, 1)], min_val=0, max_val=PAD_UNIT)
                sp.dma_start(rows[p][:, :, :], scattered[bass.ds(first, UNIT), :]
                             .rearrange("(t p) c -> p t c", p=P)).then_inc(rows_loaded[p], 16)

            def expert(r):
                return sp.value_load(expert_of[0:1, bass.ds(r, 1)], min_val=0, max_val=EXPERTS - 1)

            sp.wait_ge(s["experts_done"], 1)
            for r in range(2):
                load_w1(r, r)
                load_w2(r, r)

            for e in range(EXPERTS):
                first = sp.value_load(fill_row[0:1, e:e + 1], min_val=0, max_val=PAD_UNIT - UNIT)
                sp.dma_start(scattered[bass.ds(first, UNIT), :].rearrange("(j p) c -> p j c", p=P),
                             t["padding"][:, :, :]).then_inc(s["filled"], 16)
            for half in range(2):
                sp.wait_ge(scatter0[half], 16 * (TILES // 2))
            sp.wait_ge(s["scatter1"], 16 * TILES)
            sp.wait_ge(s["filled"], 16 * (EXPERTS + 2))
            for r in range(2):
                load_rows(r, r)

            def load(r, p):
                load_rows(r, p)
                load_w1(r, p)
                load_w2(r, p)

            with sp.Fori(1, ROUTED_UNITS // 2) as pair:
                for p in range(2):
                    load(pair * 2 + p, p)
            for r in range(ROUTED_UNITS // 2 * 2, ROUTED_UNITS):
                load(r, r % 2)
            sp.wait_ge(s["y_added"], 16 * UT * ROUTED_UNITS)
            sp.wait_ge(y_stored[0], 16 * (SHARED_UNITS // 2))
            sp.wait_ge(y_stored[1], 16 * (SHARED_UNITS // 2))

        @block.gpsimd
        def _(pool):
            for q in range(4):
                row_scale(pool, t, m, q)

            def scatter(k, tile):
                return pool.indirect_dma_start(scattered, bass.IndirectOffsetOnAxis(ap=place[k][:, tile:tile + 1], axis=0),
                                               rows_out[:, tile, :], None)

            for g, (block, end) in enumerate(GROUPS):
                middle = (block + end) * UT // 2
                halves = [range(block * UT, middle), range(middle, end * UT)]
                pool.wait_ge(s["row_kept"], end)
                pool.wait_ge(s["gates_done"], g + 1)
                pool.wait_ge(s["places_done"], g + 1)
                for half in range(2):
                    for tile in halves[half]:
                        scatter(0, tile).then_inc(scatter0[half], 16)
                for half in range(2):
                    n = g * 2 + half + 1
                    pool.wait_ge(scatter0[half], 8 * end * UT)
                    tiles = slice(halves[half][0], halves[half][-1] + 1)
                    pool.tensor_copy(rows_out[:, tiles, D], gate[1][:, tiles]).then_inc(s["gate2_done"], 1)
                    pool.wait_ge(s["gate2_done"], n)
                    for tile in halves[half]:
                        scatter(1, tile).then_inc(s["scatter1"], 16)

            def add_rows(r, p):
                pool.wait_ge(s["y_done"], r + SHARED_UNITS + 1)
                pool.wait_ge(s["number_done"], r + 1)
                wait_past(pool, s["y_added"], r * (16 * UT))
                pool.tensor_tensor(turn[:, bass.ds(r + 1, 1)], turn[:, 0:1], turn[:, 0:1], ALU.add)
                for j in range(UT):
                    pool.indirect_dma_start(dst, bass.IndirectOffsetOnAxis(ap=number[p][:, j:j + 1], axis=0),
                                            y[p][:, j, :], None, compute_op=ALU.add).then_inc(s["y_added"], 16)

            pool.wait_ge(y_stored[0], 16 * (SHARED_UNITS // 2))
            pool.wait_ge(y_stored[1], 16 * (SHARED_UNITS // 2))
            pool.memset(turn[:, :], 0.0).then_inc(s["turn_set"], 1)
            pool.wait_ge(s["turn_set"], 1)
            add_rows(0, 0)
            add_rows(1, 1)
            with pool.Fori(1, ROUTED_UNITS // 2) as pair:
                for p in range(2):
                    add_rows(pair * 2 + p, p)
            for r in range(ROUTED_UNITS // 2 * 2, ROUTED_UNITS):
                add_rows(r, r % 2)

        @block.tensor
        def _(pe):
            pe.wait_ge(s["params"], 32)

            def turn_block(b, p):
                pe.wait_ge(s["xn_done"], b + 1)
                wait_past(pe, s["xt_kept"], b - 1)
                for j in range(UT):
                    last = pe.transpose(up_bank[p][:, j * P:(j + 1) * P], xn[p][:, j, :], t["ident"][:, :])
                last.then_inc(s["xn_turned"], 1)

            def route_block(b, p):
                pe.wait_ge(s["xt_out"], b + 1)
                wait_past(pe, s["logit_kept"], b - 1)
                for j in range(UT):
                    last = pe.matmul(up_bank[2 + p][:, j * EXPERTS:(j + 1) * EXPERTS], x_t[p][:, j * P:(j + 1) * P],
                                     router_w[:, :], start=True, stop=True)
                last.then_inc(s["logit_done"], 1)

            def place_group(g):
                pe.wait_ge(s["both_done"], g + 1)
                first, n, tiles = group(g)
                out = down_bank[g][:, 0:(n + 1) * EXPERTS].rearrange("p (t e) -> p t e", e=EXPERTS)
                pe.matmul(out[:, 1:, :], ones[:, :], both[:, tiles, :], start=True, stop=False,
                          skip_group_check=True)
                pe.matmul(out[:, 0:n, :], earlier[:, :], both[:, tiles, :],
                          start=False, stop=False, skip_group_check=True)
                for j in range(n - 1):
                    last = pe.matmul(out[:, j + 2:, :], ones[:, :],
                                     both[:, first + j, :].unsqueeze(1).to_broadcast([P, n - 1 - j, EXPERTS]),
                                     start=False, stop=j == n - 2, skip_group_check=True)
                last.then_inc(s["prefixed"], 1)

            first_end = GROUPS[0][1]
            turn_block(0, 0)
            for b in range(1, first_end + 2):
                turn_block(b, b % 2)
                route_block(b - 1, (b - 1) % 2)
            place_group(0)
            for b in range(first_end + 2, SHARED_UNITS):
                route_block(b - 1, (b - 1) % 2)
                turn_block(b, b % 2)
            route_block(SHARED_UNITS - 1, (SHARED_UNITS - 1) % 2)

            def step(u, like):
                p, q = like % 2, (like + 1) % 2
                up, down, turn = like < UNITS, 1 <= like <= UNITS, 2 <= like
                hi, lo = (sh_hi, sh_lo) if like < SHARED_UNITS else (w_hi[p], w_lo[p])
                hi1, lo1 = (sh_hi, sh_lo) if like - 1 < SHARED_UNITS else (w_hi[q], w_lo[q])
                for c in range(CHUNKS):
                    cols = slice(c * P, (c + 1) * P)
                    if up:
                        if c == 0:
                            pe.wait_ge(s["x_split"], u + 1)
                            if like < SHARED_UNITS:
                                pe.wait_ge(s["sh_split"], 1)
                            else:
                                pe.wait_ge(s["w1_split"], u - SHARED_UNITS + 1)
                        if like == 0:
                            pe.wait_ge(s["logit_kept"], SHARED_UNITS)
                        wait_past(pe, s["gelu_done"], (u - 1) * CHUNKS + c + 1)
                        three_passes(pe, up_bank[c][:, :], hi[:, 0, cols], lo[:, 0, cols], x_hi[p][:, :], x_lo[p][:, :]
                                     ).then_inc(s["up_done"], 1)
                    if down:
                        if c == 0:
                            if like - 1 >= SHARED_UNITS:
                                pe.wait_ge(s["w2_split"], u - SHARED_UNITS)
                            wait_past(pe, s["yt_done"], u - 2)
                            if like - 1 < 2:
                                pe.wait_ge(s["places_done"], len(GROUPS))
                        pe.wait_ge(s["h_split"], (u - 1) * CHUNKS + c + 1)
                        last = three_passes(pe, down_bank[q][:, :], hi1[:, 1, cols], lo1[:, 1, cols],
                                            h_hi[:, q, c, :], h_lo[:, q, c, :], start=c == 0, stop=c == CHUNKS - 1)
                        if c == CHUNKS - 1:
                            last.then_inc(s["down_done"], 1)
                    if c == (CHUNKS - 1 if like + 1 == SHARED_UNITS else 0) and SHARED_UNITS <= like + 1 < UNITS:
                        r = u + 1 - SHARED_UNITS
                        pe.wait_ge(rows_loaded[q], (r - q) * 8 + 16)
                        pe.wait_ge(s["x_split"], u + 1)
                        for j in range(UT):
                            last = pe.transpose(x_bank[:, j * P:(j + 1) * P], rows[q][:, j, 0:D], t["ident"][:, :])
                        last.then_inc(s["x_turned"], 1)
                    if c == 1 and turn:
                        pe.wait_ge(s["yt_done"], u - 1)
                        wait_past(pe, s["y_done"], u - 2)
                        for j in range(UT):
                            last = pe.transpose(y_bank[:, j * P:(j + 1) * P], y_t[p][:, j * P:(j + 1) * P], t["ident"][:, :])
                        last.then_inc(s["y_turned"], 1)

                if like == 0:
                    place_group(1)

            run_steps(pe, step)

        @block.scalar
        def _(act):

            def evacuate(b, p):
                act.wait_ge(s["xn_turned"], b + 1)
                wait_past(act, s["logit_done"], b - 1)
                act.copy(x_t[p][:, :], up_bank[p][:, :]).then_inc(s["xt_out"], 1)
                act.copy(x_t_all[:, bass.ds(b, 1), :].rearrange("p b n -> p (b n)"), up_bank[p][:, :]
                         ).then_inc(s["xt_kept"], 1)

            def exponentials(g):
                act.wait_ge(s["shifted"], g + 1)
                tiles = group(g)[2]
                act.activation(prob[:, tiles, :], logits[:, tiles, :], ACT.Exp
                               ).then_inc(s["exped"], 1)

            act.wait_ge(s["sh_loaded"], 16)
            for k in range(2):
                act.copy(sh_hi[:, k, :], sh_raw[:, (1 - k) * FF:(2 - k) * FF]).then_inc(s["sh_hi"], 1)
            def keep_rows(b, p):
                act.wait_ge(s["xn_done"], b + 1)
                act.copy(rows_out[:, b * UT:(b + 1) * UT, 0:D], xn[p][:, :, :]).then_inc(s["row_kept"], 1)

            def high_x(u, like):
                p = like % 2
                if like < SHARED_UNITS:
                    act.wait_ge(s["xt_kept"], u + 1)
                    source = x_t_all[:, bass.ds(u, 1), :].rearrange("p b n -> p (b n)")
                else:
                    act.wait_ge(s["x_turned"], u - SHARED_UNITS + 1)
                    source = x_bank[:, :]
                wait_past(act, s["up_done"], (u - 1) * CHUNKS)
                act.copy(x_hi[p][:, :], source).then_inc(s["x_high"], 1)

            for b in range(SHARED_UNITS):
                evacuate(b, b % 2)
                keep_rows(b, b % 2)
                if b == GROUPS[0][1] + 1:
                    exponentials(0)
            high_x(0, 0)
            exponentials(1)

            def high_w(which, u, like, done):
                p, r = like % 2, u - SHARED_UNITS
                act.wait_ge((w1_loaded, w2_loaded)[which][p], (r - p) * 8 + 16)
                if which == 0:
                    wait_past(act, s["up_done"], (u - 1) * CHUNKS)
                else:
                    wait_past(act, s["down_done"], u - 1)
                act.copy(w_hi[p][:, which, :], (w1_raw, w2_raw)[which][p][:, 0:FF]).then_inc(done, 1)

            def step(u, like):
                p = like % 2
                if like >= 2:
                    act.wait_ge(s["down_done"], u - 1)
                    wait_past(act, s["y_turned"], u - 2)
                    if like - 2 < SHARED_UNITS:
                        bias = sh_raw[:, 2 * FF + CHUNKS:]
                    else:
                        act.wait_ge(s["bias_kept"], u - 2 - SHARED_UNITS + 1)
                        bias = bias_of[:, bass.ds(u - 2 - SHARED_UNITS, 1), CHUNKS:].rearrange("p u c -> p (u c)")
                    act.activation(y_t[p][:, :], down_bank[p][:, :], ACT.Identity, bias=bias).then_inc(s["yt_done"], 1)
                for c in range(CHUNKS):
                    if like < UNITS:
                        act.wait_ge(s["up_done"], u * CHUNKS + c + 1)
                        wait_past(act, s["h_split"], (u - 1) * CHUNKS + c + 1)
                        if like < SHARED_UNITS:
                            bias = sh_raw[:, 2 * FF + c:2 * FF + c + 1]
                        else:
                            if c == 0:
                                act.wait_ge(s["bias_kept"], u - SHARED_UNITS + 1)
                            bias = bias_of[:, bass.ds(u - SHARED_UNITS, 1), c:c + 1].rearrange("p u c -> p (u c)")
                        act.activation(h[:, c, :], up_bank[c][:, :], ACT.Gelu_apprx_tanh, bias=bias
                                       ).then_inc(s["gelu_done"], 1)
                    if c == 0 and SHARED_UNITS <= like + 1 < UNITS:
                        high_w(0, u + 1, like + 1, s["w1_high"])
                    if c == (CHUNKS - 1 if like + 1 == SHARED_UNITS else 1) and like + 1 < UNITS:
                        high_x(u + 1, like + 1)
                    if c == 1 and SHARED_UNITS <= like < UNITS:
                        high_w(1, u, like, s["w2_high"])
                    if c == 2 and like >= SHARED_UNITS + 2:
                        r = u - 2 - SHARED_UNITS
                        act.wait_ge(s["y_turned"], u - 1)
                        if like < SHARED_UNITS + 4:
                            act.wait_ge(y_stored[p], 16 * (SHARED_UNITS // 2))
                        else:
                            act.wait_ge(s["y_added"], (r - 1) * (16 * UT))
                        act.wait_ge(s["tail_kept"], r + 1)
                        for j in range(UT):
                            last = act.mul(y[p][:, j, :], y_bank[:, j * P:(j + 1) * P],
                                           tail_of[:, bass.ds(r, 1), j, 0:1].rearrange("p u c -> p (u c)"))
                        last.then_inc(s["y_done"], 1)
                    if c == 3 and 2 <= like < SHARED_UNITS + 2:
                        act.wait_ge(s["y_done"], u - 1)
                        act.dma_start(dst[bass.ds((u - 2) * UNIT, UNIT), :].rearrange("(t p) d -> p t d", p=P),
                                      y[p][:, :, :]).then_inc(y_stored[p], 16)

            run_steps(act, step)

        @block.vector
        def _(dve):
            chain = Chain(dve, s["chain"])
            dve.wait_ge(t["tables_loaded"], 16 * t["n_tables"])
            dve.tensor_copy(earlier[:, :], t["earlier"][:, :])
            dve.tensor_scalar(ones[:, :], t["earlier"][:, :], 0.0, 1.0, ALU.mult, ALU.add).then_inc(s["casts"], 1)

            def stats(q):
                row_stats(dve, chain, t["x"], m, q, None if f else t["x_loaded"][q])

            stats(0)

            def normalise_block(b, p):
                dve.wait_ge(m["rstd_done"], b // 2 + 1)
                wait_past(dve, s["xn_turned"], b - 1)
                wait_past(dve, s["row_kept"], b - 1)
                for j in range(UT):
                    last = normalise(dve, xn[p][:, j, :], t["x"], b * UT + j, m)
                last.then_inc(s["xn_done"], 1)

            def keep_logits(b, p):
                dve.wait_ge(s["logit_done"], b + 1)
                dve.tensor_tensor(logits[:, bass.ds(b * UT, UT), :],
                                  up_bank[2 + p][:, 0:UT * EXPERTS].rearrange("p (t e) -> p t e", e=EXPERTS),
                                  router_b[:, :].unsqueeze(1).to_broadcast([P, UT, EXPERTS]), ALU.add
                                  ).then_inc(s["logit_kept"], 1)

            dve.wait_ge(s["params"], 32)
            def choose(g):
                first, n, tiles = group(g)
                dve.wait_ge(s["logit_kept"], GROUPS[g][1])

                def per_expert(column):
                    return column[:, tiles].unsqueeze(2).to_broadcast([P, n, EXPERTS])

                z, pr, sc = logits[:, tiles, :], prob[:, tiles, :], score[:, tiles, :]
                chain.then(dve.tensor_reduce(best[:, tiles], z, AX.X, ALU.max))
                dve.tensor_tensor(z, z, per_expert(best), ALU.subtract).then_inc(s["shifted"], 1)
                dve.wait_ge(s["exped"], g + 1)
                chain.then(dve.tensor_reduce(best[:, tiles], pr, AX.X, ALU.add))
                chain.then(dve.reciprocal(best[:, tiles], best[:, tiles]))
                chain.then(dve.tensor_tensor(pr, pr, per_expert(best), ALU.mult))
                rev = t["const"][:, C_REV:C_REV + EXPERTS].unsqueeze(1).to_broadcast([P, n, EXPERTS])
                left = pr
                for k in range(TOP):
                    chain.then(dve.tensor_reduce(top[k][:, tiles], left, AX.X, ALU.max))
                    chain.then(dve.tensor_tensor(sc, left, per_expert(top[k]), ALU.is_equal))
                    chain.then(dve.tensor_tensor(sc, sc, rev, ALU.mult))
                    chain.then(dve.tensor_reduce(best[:, tiles], sc, AX.X, ALU.max))
                    chain.then(dve.tensor_tensor(chosen[k][:, tiles, :], sc, per_expert(best), ALU.is_equal))
                    if k == 0:
                        left = rest[:, tiles, :]
                        chain.then(dve.scalar_tensor_tensor(out=left, in0=chosen[0][:, tiles, :], scalar=-2.0, in1=pr,
                                                            op0=ALU.mult, op1=ALU.add))
                dve.wait_ge(s["casts"], 1)
                dve.tensor_tensor(both[:, tiles, :], chosen[0][:, tiles, :], chosen[1][:, tiles, :], ALU.add
                                  ).then_inc(s["both_done"], 1)
                chain.then(dve.tensor_tensor(best[:, tiles], top[0][:, tiles], top[1][:, tiles], ALU.add))
                chain.then(dve.reciprocal(best[:, tiles], best[:, tiles]))
                for k in range(TOP):
                    chain.then(dve.scalar_tensor_tensor(out=gate[k][:, tiles], in0=top[k][:, tiles], scalar=0.5,
                                                        in1=best[:, tiles], op0=ALU.mult, op1=ALU.mult))
                dve.tensor_copy(rows_out[:, tiles, D + 1], t["const"][:, C_ID + first:C_ID + first + n])
                dve.tensor_copy(rows_out[:, tiles, D], gate[0][:, tiles]).then_inc(s["gates_done"], 1)

            def place_rows(g):
                first, n, tiles = group(g)
                dve.wait_ge(s["prefixed"], g + 1)
                counts = down_bank[g][:, 0:(n + 1) * EXPERTS].rearrange("p (t e) -> p t e", e=EXPERTS)
                chain.then(dve.tensor_tensor(before[:, tiles, :], counts[:, 0:n, :],
                                             next_row[:, :].unsqueeze(1).to_broadcast([P, n, EXPERTS]), ALU.add))
                chain.then(dve.tensor_tensor(next_row[:, :], next_row[:, :], counts[:, n, :], ALU.add))
                for k in range(TOP):
                    chain.then(dve.tensor_tensor(score[:, tiles, :], before[:, tiles, :], chosen[k][:, tiles, :], ALU.mult))
                    chain.then(dve.tensor_reduce(place_f[k][:, tiles], score[:, tiles, :], AX.X, ALU.add))
                    last = dve.tensor_copy(place[k][:, tiles], place_f[k][:, tiles])
                last.then_inc(s["places_done"], 1)

            def low_x(u, like):
                p = like % 2
                dve.wait_ge(s["x_high"], u + 1)
                source = (x_t_all[:, bass.ds(u, 1), :].rearrange("p b n -> p (b n)") if like < SHARED_UNITS
                          else x_bank[:, :])
                dve.tensor_tensor(x_lo[p][:, :], source, x_hi[p][:, :].bitcast(F32), ALU.subtract).then_inc(s["x_split"], 1)
                if like >= SHARED_UNITS:
                    r = u - SHARED_UNITS
                    dve.wait_ge(rows_loaded[p], (r - p) * 8 + 16)
                    dve.tensor_scalar(tail_of[:, bass.ds(r, 1), :, :].rearrange("p u t c -> p (u t) c"),
                                      rows[p][:, :, D:ROW], 1.0, None, ALU.mult).then_inc(s["tail_kept"], 1)

            dve.tensor_copy(next_row[:, :], t["const"][:, C_REGION:C_REGION + EXPERTS])
            first_end = GROUPS[0][1]
            stats(1)
            normalise_block(0, 0)
            normalise_block(1, 1)
            for b in range(2, first_end + 2):
                if b % 2 == 0:
                    stats(b // 2 + 1)
                normalise_block(b, b % 2)
                keep_logits(b - 2, b % 2)
            choose(0)
            place_rows(0)
            for b in range(first_end + 2, SHARED_UNITS):
                normalise_block(b, b % 2)
                keep_logits(b - 2, b % 2)
            for b in range(SHARED_UNITS - 2, SHARED_UNITS):
                keep_logits(b, b % 2)
            dve.wait_ge(s["sh_hi"], 2)
            for k in range(2):
                last = dve.tensor_tensor(sh_lo[:, k, :], sh_raw[:, (1 - k) * FF:(2 - k) * FF],
                                         sh_hi[:, k, :].bitcast(F32), ALU.subtract)
            last.then_inc(s["sh_split"], 1)
            low_x(0, 0)
            choose(1)

            def unit_tables():
                chain.then(dve.tensor_tensor(count_of[:, :], next_row[:, :], t["const"][:, C_REGION:C_REGION + EXPERTS],
                                             ALU.subtract))
                steps = t["const"][:, C_STEP:C_STEP + EXPERTS]
                region = t["const"][:, C_REGION:C_REGION + EXPERTS]
                unit = t["const"][:, C_UNIT:C_UNIT + ROUTED_UNITS]
                chain.then(dve.tensor_tensor(over[:, :, :], count_of[:, :].unsqueeze(2).to_broadcast([P, EXPERTS, EXPERTS]),
                                             steps.unsqueeze(1).to_broadcast([P, EXPERTS, EXPERTS]), ALU.is_gt))
                chain.then(dve.tensor_reduce(units_of[:, :], over[:, :, :], AX.X, ALU.add))
                chain.then(dve.tensor_tensor_scan(end_of[:, :], t["ones"][:, 0:EXPERTS], units_of[:, :], 0.0, ALU.mult, ALU.add))
                chain.then(dve.tensor_tensor(base_of[:, :], end_of[:, :], units_of[:, :], ALU.subtract))
                chain.then(dve.scalar_tensor_tensor(out=base_of[:, :], in0=base_of[:, :], scalar=-float(UNIT), in1=region,
                                                    op0=ALU.mult, op1=ALU.add))
                chain.then(dve.tensor_tensor(passed[:, :, :], end_of[:, :].unsqueeze(1).to_broadcast([P, ROUTED_UNITS, EXPERTS]),
                                             unit.unsqueeze(2).to_broadcast([P, ROUTED_UNITS, EXPERTS]), ALU.is_le))
                chain.then(dve.tensor_reduce(expert_f[:, :], passed[:, :, 0:EXPERTS - 1], AX.X, ALU.add))
                dve.tensor_copy(expert_of[:, :], expert_f[:, :])
                chain.then(dve.tensor_tensor(over[:, 0, 0:EXPERTS - 1], base_of[:, 1:], base_of[:, 0:EXPERTS - 1], ALU.subtract))
                chain.then(dve.tensor_tensor(moved[:, :, :], passed[:, :, 0:EXPERTS - 1],
                                             over[:, 0, 0:EXPERTS - 1].unsqueeze(1).to_broadcast([P, ROUTED_UNITS, EXPERTS - 1]),
                                             ALU.mult))
                chain.then(dve.tensor_reduce(row_f[:, :], moved[:, :, :], AX.X, ALU.add))
                chain.then(dve.scalar_tensor_tensor(out=row_f[:, :], in0=unit, scalar=float(UNIT), in1=row_f[:, :],
                                                    op0=ALU.mult, op1=ALU.add))
                chain.then(dve.tensor_scalar(row_left[:, :], row_f[:, :], -1.0, float(PAD_UNIT), ALU.mult, ALU.add))
                chain.then(dve.tensor_tensor(row_left[:, :], row_left[:, :], passed[:, :, EXPERTS - 1], ALU.mult))
                chain.then(dve.tensor_tensor(row_f[:, :], row_f[:, :], row_left[:, :], ALU.add))
                dve.tensor_copy(row_of[:, :], row_f[:, :])
                dve.tensor_copy(fill_row[:, :], next_row[:, :]).then_inc(s["experts_done"], 1)

            def low_w(which, u, like, high, done):
                p, r = like % 2, u - SHARED_UNITS
                dve.wait_ge(high, r + 1)
                if which == 0:
                    dve.tensor_scalar(bias_of[:, bass.ds(r, 1), :].rearrange("p u c -> p (u c)"),
                                      w1_raw[p][:, FF:], 1.0, None, ALU.mult).then_inc(s["bias_kept"], 1)
                dve.tensor_tensor(w_lo[p][:, which, :], (w1_raw, w2_raw)[which][p][:, 0:FF],
                                  w_hi[p][:, which, :].bitcast(F32), ALU.subtract).then_inc(done, 1)

            def step(u, like):
                p = like % 2
                for c in range(CHUNKS):
                    if like == 0 and c == CHUNKS - 2:
                        place_rows(1)
                    if like < UNITS:
                        n = u * CHUNKS + c + 1
                        dve.wait_ge(s["gelu_done"], n)
                        wait_past(dve, s["down_done"], u - 1)
                        dve.tensor_copy(h_hi[:, p, c, :], h[:, c, :]).then_inc(s["h_high"], 1)
                    if c == 0 and SHARED_UNITS <= like + 1 < UNITS:
                        low_w(0, u + 1, like + 1, s["w1_high"], s["w1_split"])
                    if c == 1 and like + 1 < UNITS and like + 1 != SHARED_UNITS:
                        low_x(u + 1, like + 1)
                    if c == 2 and SHARED_UNITS <= like < UNITS:
                        low_w(1, u, like, s["w2_high"], s["w2_split"])
                    if like < UNITS:
                        dve.wait_ge(s["h_high"], n)
                        dve.tensor_tensor(h_lo[:, p, c, :], h[:, c, :], h_hi[:, p, c, :].bitcast(F32), ALU.subtract
                                          ).then_inc(s["h_split"], 1)
                    if c == 2 and 2 <= like < SHARED_UNITS + 2:
                        v = u - 2
                        dve.wait_ge(s["y_turned"], v + 1)
                        wait_past(dve, y_stored[p], (v - p) * 8)
                        dve.scalar_tensor_tensor(
                            out=y[p][:, :, :].rearrange("p t d -> p (t d)"), in0=y_bank[:, :], scalar=0.5,
                            in1=t["x"][:, bass.ds(v * UT, UT), :].rearrange("p t d -> p (t d)"),
                            op0=ALU.mult, op1=ALU.add).then_inc(s["y_done"], 1)
                    if c == 2 and like >= SHARED_UNITS + 2:
                        r = u - 2 - SHARED_UNITS
                        wait_past(dve, s["y_added"], (r - 1) * (16 * UT))
                        dve.wait_ge(s["tail_kept"], r + 1)
                        dve.tensor_scalar(number[p][:, :], tail_of[:, bass.ds(r, 1), :, 1].rearrange("p u t -> p (u t)"),
                                          1.0, None, ALU.mult).then_inc(s["number_done"], 1)
                if like + 1 == SHARED_UNITS:
                    low_x(u + 1, like + 1)
                if like == 1:
                    unit_tables()

            run_steps(dve, step)


def run_batches(eng, step):
    for b in range(4):
        step(b, b)
    with eng.Fori(2, BATCH // 2 - 1) as pair:
        for j in range(2):
            step(pair * 2 + j, 4 + j)
    for b in range(BATCH - 2, BATCH + 2):
        step(b, b)


def own_columns(values, c):
    return values[:, c, :, :, :].rearrange("p h j v -> p h (j v)").rearrange("p h (k v) -> p h k v", v=VD)[:, :, 0:4:3, :]


def retention(nc, t, src):
    with ExitStack() as ctx:
        sems = []

        def sem(name):
            sems.append(nc.alloc_semaphore(f"r_{name}"))
            return sems[-1]

        def sb(name, shape, dt=F32):
            return ctx.enter_context(nc.sbuf_tensor(f"r_{name}", shape, dt))

        def psum(name, shape):
            return ctx.enter_context(nc.psum_tensor(f"r_{name}", shape, F32))

        CH = SEQ // P
        GROUPS = HEADS // 4
        W = 4 * D
        score_bank = [psum(f"score{i}", [P, 4, P]) for i in range(2)]
        turn_bank = psum("turn", [P, 512])
        qk_bank, heads_bank = psum("qk", [P, 512]), psum("heads", [P, CH, 2 * D])
        v_bank = psum("v", [P, 2, 2 * D])
        out_bank = [psum(f"out{c}", [P, 2, P]) for c in range(CH)]

        m = dict(stats=sb("stats", [P, TILES, 6]), mean=sb("mean", [P, TILES]), var=sb("var", [P, TILES]),
                            diff=sb("diff", [P, TILES]), rstd=sb("rstd", [P, TILES]),
                            var_done=sem("var_done"), rstd_done=sem("rows_rstd_done"))
        qk_raw, qk_hi, qk_lo = sb("qk_raw", [P, W]), sb("qk_hi", [P, W], F32R), sb("qk_lo", [P, W], F32R)
        vg_raw, vg_hi, vg_lo = sb("vg_raw", [P, W]), sb("vg_hi", [P, W], F32R), sb("vg_lo", [P, W], F32R)
        o_raw = sb("o_raw", [P, 2 * D])
        vg_bias, o_bias, qk_bias = sb("vg_bias", [P, W]), sb("o_bias", [P, D]), sb("qk_bias", [P, 4])
        turns = sb("turns", [P, 4, SEQ])
        mask = sb("mask", [P, HEADS, P])
        q_decay, k_decay, own_head = sb("q_decay", [P, P]), sb("k_decay", [P, P]), sb("own_head", [P, HEADS, VD])
        decays, head_of = sb("decays", [P, SEQ]), sb("head_of", [P, HEADS])

        xn = [sb(f"xn{p}", [P, CH, D]) for p in range(2)]
        x_hi, x_lo = sb("x_hi", [P, SEQ], F32R), sb("x_lo", [P, SEQ], F32R)
        q_part, q_turn = sb("q_part", [P, SEQ]), sb("q_turn", [P, SEQ])
        k_part, k_turn = sb("k_part", [P, SEQ]), sb("k_turn", [P, SEQ])
        q_all = sb("q_all", [P, SEQ])
        keys = [sb(f"keys{p}", [P, SEQ]) for p in range(2)]
        keys_hi, keys_lo = ([sb(f"keys_{k}{p}", [P, SEQ], F32R) for p in range(2)] for k in ("hi", "lo"))
        q_hi, q_lo = sb("q_hi", [P, SEQ], F32R), sb("q_lo", [P, SEQ])
        spread_hi, spread_lo = ([sb(f"spread_{k}{p}", [P, 4, SEQ], F32R) for p in range(2)] for k in ("hi", "lo"))
        q_dec = [sb(f"q_dec{p}", [P, P]) for p in range(2)]
        values = [sb(f"values{p}", [P, CH, HEADS // 2, 2, 2 * VD]) for p in range(2)]
        key_sums, sum_terms = sb("key_sums", [P, SEQ]), sb("sum_terms", [P, SEQ])
        out_turned = sb("out_turned", [P, CH, 2, P])
        g_raw = [sb(f"g_raw{p}", [P, CH, 2 * D]) for p in range(2)]
        g_act = [sb(f"g_act{p}", [P, CH, 2 * D]) for p in range(2)]
        probs = sb("probs", [P, CH, HEADS, P])
        k_dec, state = sb("k_dec", [P, P]), sb("state", [P, HEADS, VD])
        heads = [sb(f"heads{p}", [P, CH * HEADS, VD]) for p in range(2)]
        squares = sb("squares", [P, CH * HEADS, VD])
        bounded, clipped, square_sum, o_var, power, o_rstd, factor = (
            sb(name, [P, CH * HEADS]) for name in ("bounded", "clipped", "square_sum", "o_var", "power", "o_rstd",
                                                   "factor"))
        inverse, inverse2 = ([sb(f"{name}{p}", [P, CH * HEADS]) for p in range(2)] for name in ("inverse", "inverse2"))
        normed = sb("normed", [P, CH * HEADS, VD])
        gated = sb("gated", [P, CH * HEADS, VD])
        y_turned = sb("y_turned", [P, CH * 2 * P])
        x_plus = [sb(f"x_plus{p}", [P, CH, D]) for p in range(2)]
        value_mean = sb("value_mean", [P, 2, HEADS])

        s = {n: sem(n) for n in (
            "weights", "tables", "chain", "high", "split", "power_set", "zeros_set", "xn_done", "x_turned", "x_high",
            "x_split", "q_done", "k_done", "parts_done", "q_all_done", "keys_done", "spread_done", "q_high", "q_split", "keys_high", "keys_split", "q_dec_done",
            "v_done", "v_kept", "g_kept", "g_done", "scored", "masked", "k_turned", "k_dec_done", "state_done",
            "state_kept", "out0_done", "out_done", "out_kept", "heads_turned",
            "heads_kept", "key_sums_done", "sum_terms_done", "squared", "sum_bounded", "sum_clipped",
            "sum_inverted", "inverse_squared", "squares_summed", "var_scaled", "o_var_done", "rstd_done",
            "factor_done", "normed_done", "gated_done", "y_turned", "y_kept", "o_done", "x_plus_done",
            "added")}
        x_in = [sem(f"x_in{q}") for q in range(4)]

        ctx.callback(release, nc, sems)
        block = ctx.enter_context(nc.Block())
        a = t["a"]
        weights = ((qk_raw[:, :], a["w_qk"]), (vg_raw[:, :], a["w_vg"]), (o_raw[:, :], a["w_o"]),
                   (vg_bias[:, :], a["b_vg"]))
        tables = ((qk_bias[:, :], a["b_qk"]), (turns[:, :, :], a["turns"]), (o_bias[:, :], a["b_o"]),
                  (q_decay[:, :], a["q_decay"]), (k_decay[:, :], a["k_decay"]), (own_head[:, :, :], a["own_head"]),
                  (decays[:, :], a["decays"]), (head_of[:, :], a["head_of"]), (mask[:, :, :], a["mask"]))

        @block.sync
        def _(sp):
            n = TILES // 4
            for q in range(4):
                sp.dma_start(t["x"][:, q * n:q * n + n, :], src[q * n * P:(q + 1) * n * P, :]
                             .rearrange("(t p) d -> p t d", p=P)).then_inc(x_in[q], 16)
                if q == 0:
                    for to, what in weights:
                        sp.dma_start(to, what).then_inc(s["weights"], 16)
                    for to, what in tables:
                        sp.dma_start(to, what).then_inc(s["tables"], 16)

        @block.gpsimd
        def _(pool):
            pool.memset(power[:, :], -0.5).then_inc(s["power_set"], 1)
            for p in range(2):
                last = pool.memset(values[p][:, :, :, :, :], 0.0)
            last.then_inc(s["zeros_set"], 1)
            row_scale(pool, t, m, 0)
            pool.wait_ge(s["tables"], 16 * len(tables))
            pool.wait_ge(s["power_set"], 1)

            def scale(c, n):
                pool.wait_ge(s["o_var_done"], n)
                cols = slice(c * HEADS, (c + 1) * HEADS)
                pool.tensor_tensor(o_rstd[:, cols], o_var[:, cols], power[:, cols], ALU.pow).then_inc(s["rstd_done"], 1)

            def step(b, like):
                p = like % 2
                if 1 <= like <= 3:
                    row_scale(pool, t, m, like)
                if 2 <= like:
                    scale(1, 2 * b - 2)
                    pool.wait_ge(s["rstd_done"], 2 * b - 2)
                    wait_past(pool, s["normed_done"], b - 2)
                    pool.tensor_tensor(factor[:, :], o_rstd[:, :], inverse[p][:, :], ALU.mult).then_inc(s["factor_done"], 1)
                    wait_past(pool, s["added"], b - 3)
                    pool.tensor_tensor(x_plus[p][:, :, :], t["x"][:, bass.ds((b - 2) * CH, CH), :],
                                       o_bias[:, :].unsqueeze(1).to_broadcast([P, CH, D]), ALU.add
                                       ).then_inc(s["x_plus_done"], 1)
                if like < BATCH:
                    pool.wait_ge(s["q_high"], b + 1)
                    wait_past(pool, s["spread_done"], b)
                    pool.tensor_tensor(q_lo[:, :], q_all[:, :], q_hi[:, :].bitcast(F32), ALU.subtract
                                       ).then_inc(s["q_split"], 1)
                    pool.wait_ge(s["keys_high"], b + 1)
                    pool.tensor_tensor(keys_lo[p][:, :], keys[p][:, :], keys_hi[p][:, :].bitcast(F32), ALU.subtract
                                       ).then_inc(s["keys_split"], 1)
                    wait_past(pool, s["out_done"], b - 1)
                    pool.tensor_tensor(q_dec[p][:, :], q_all[:, P:SEQ], q_decay[:, :], ALU.mult
                                       ).then_inc(s["q_dec_done"], 1)
                    pool.wait_ge(s["key_sums_done"], b + 1)
                    wait_past(pool, s["k_turned"], b)
                    pool.tensor_tensor(sum_terms[:, :], q_all[:, :], key_sums[:, :], ALU.mult
                                       ).then_inc(s["sum_terms_done"], 1)
                if 1 <= like <= BATCH:
                    scale(0, 2 * b - 1)

            run_batches(pool, step)

        @block.tensor
        def _(pe):
            pe.wait_ge(s["split"], 2)

            def turn_x(b, p):
                pe.wait_ge(s["xn_done"], b + 1)
                for c in range(CH):
                    last = pe.transpose(turn_bank[:, c * P:c * P + P], xn[p][:, c, :], t["ident"][:, :])
                last.then_inc(s["x_turned"], 1)

            turn_x(0, 0)

            def score(c, g, b, q):
                n = (b - 1) * (CH * GROUPS) + c * GROUPS + g
                wait_past(pe, s["masked"], n - 1)
                rows, cols = slice(32 * g, 32 * g + 32), slice(c * P, c * P + P)
                three_passes(pe, score_bank[g % 2][:, :, :], keys_hi[q][rows, cols], keys_lo[q][rows, cols],
                             spread_hi[q][rows, :, cols], spread_lo[q][rows, :, cols]).then_inc(s["scored"], 1)

            def outputs(c, first, b, q):
                pe.wait_ge(s["masked"], (b - 1) * (CH * GROUPS) + c * GROUPS + first // 4 + 1)
                if c == 1 and first % 8 == 0:
                    pe.matmul(out_bank[1][:, first // 8, :], state[:, first:first + 8, :].rearrange("p h v -> p (h v)"),
                              q_dec[q][:, :], start=True, stop=False, skip_group_check=True)
                for h in range(first, first + 4):
                    quad, half = h // 2 % 4 * 32, h // 8
                    last = pe.matmul(out_bank[c][quad:quad + 32, half, :], values[q][:, c, h // 2, h % 2, :],
                                     probs[:, c, h, :], start=c == 0 and h % 2 == 0, stop=h % 2 == 1,
                                     skip_group_check=True)
                return last

            def turn_heads(c, b):
                pe.wait_ge(s["out_kept"], (b - 1) * CH + c + 1)
                wait_past(pe, s["heads_kept"], (b - 1) * CH + c)
                for half in range(2):
                    last = pe.transpose(heads_bank[:, c, half * P:half * P + P], out_turned[:, c, half, :],
                                        t["ident"][:, :])
                last.then_inc(s["heads_turned"], 1)

            def step(b, like):
                p, q = like % 2, (like + 1) % 2
                new, mid, old, ahead = like < BATCH, 1 <= like <= BATCH, 2 <= like, like + 1 < BATCH

                def values_and_gates(c):
                    wait_past(pe, s["g_kept"], CH * b + c)
                    if c == 0:
                        wait_past(pe, s["added"], b - 2)
                    cols = slice(c * P, c * P + P)
                    three_passes(pe, v_bank[:, :, :].rearrange("p c n -> p (c n)"), x_hi[:, cols], x_lo[:, cols],
                                 vg_hi[:, :], vg_lo[:, :]).then_inc(s["v_done"], 1)

                if mid:
                    pe.wait_ge(s["keys_done"], b)
                    if new:
                        pe.wait_ge(s["x_split"], b + 1)
                    pe.wait_ge(s["sum_terms_done"], b)
                    pe.transpose(turn_bank[:, 0:P], keys[q][:, 0:P], t["ident"][:, :])
                    for c in range(CH):
                        last = pe.matmul(turn_bank[:, P + c * HEADS:P + (c + 1) * HEADS], sum_terms[:, c * P:(c + 1) * P],
                                         head_of[:, :], start=True, stop=True)
                    last.then_inc(s["k_turned"], 1)
                if old:
                    turn_heads(1, b - 1)
                if mid:
                    pe.wait_ge(s["spread_done"], b)
                    pe.wait_ge(s["keys_split"], b)
                    score(0, 0, b, q)
                    score(0, 1, b, q)
                if new:
                    pe.wait_ge(s["x_split"], b + 1)
                    wait_past(pe, s["state_kept"], b - 1)
                    wait_past(pe, s["parts_done"], 2 * b)
                    for k in range(2):
                        cols = slice(k * D, (k + 1) * D)
                        last = three_passes(pe, qk_bank[:, k * SEQ:(k + 1) * SEQ], qk_hi[:, cols], qk_lo[:, cols], x_hi[:, :], x_lo[:, :])
                    last.then_inc(s["q_done"], 1)
                if mid:
                    score(0, 2, b, q)
                if new:
                    values_and_gates(0)
                if mid:
                    score(0, 3, b, q)
                if new:
                    pe.wait_ge(s["parts_done"], 2 * b + 1)
                    for k in range(2):
                        cols = slice((2 + k) * D, (3 + k) * D)
                        last = three_passes(pe, qk_bank[:, k * SEQ:(k + 1) * SEQ], qk_hi[:, cols], qk_lo[:, cols], x_hi[:, :], x_lo[:, :])
                    last.then_inc(s["k_done"], 1)
                if mid:
                    outputs(0, 0, b, q)
                    score(1, 0, b, q)
                    outputs(0, 4, b, q)
                    score(1, 1, b, q)
                    outputs(0, 8, b, q)
                    pe.wait_ge(s["k_dec_done"], b)
                    pe.wait_ge(s["v_kept"], CH * b)
                    if new:
                        pe.wait_ge(s["parts_done"], 2 * b + 2)
                    pe.matmul(qk_bank[:, 0:HEADS * VD], k_dec[:, :], own_columns(values[q], 0),
                              start=True, stop=True).then_inc(s["state_done"], 1)
                    score(1, 2, b, q)
                    outputs(0, 12, b, q).then_inc(s["out0_done"], 1)
                    score(1, 3, b, q)
                if new:
                    values_and_gates(1)
                if mid:
                    turn_heads(0, b)
                if mid:
                    pe.wait_ge(s["state_kept"], b)
                    pe.wait_ge(s["q_dec_done"], b)
                    outputs(1, 0, b, q)
                if old:
                    pe.wait_ge(s["gated_done"], b - 1)
                    if mid:
                        pe.wait_ge(s["sum_clipped"], b)
                    for k in range(CH * 2):
                        last = pe.transpose(turn_bank[:, k * P:k * P + P],
                                            gated[:, :, :].rearrange("p h v -> p (h v)")[:, k * P:k * P + P],
                                            t["ident"][:, :])
                    last.then_inc(s["y_turned"], 1)
                if mid:
                    outputs(1, 4, b, q)
                    outputs(1, 8, b, q)
                if ahead:
                    if old:
                        pe.wait_ge(s["y_kept"], b - 1)
                    elif mid:
                        pe.wait_ge(s["sum_clipped"], b)
                    else:
                        pe.wait_ge(s["x_split"], b + 1)
                    turn_x(b + 1, q)
                if mid:
                    outputs(1, 12, b, q).then_inc(s["out_done"], 1)
                if old:
                    pe.wait_ge(s["y_kept"], b - 1)
                    if new:
                        pe.wait_ge(s["g_kept"], CH * (b + 1))
                    wait_past(pe, s["added"], b - 2)
                    for c in range(CH):
                        for half in range(2):
                            k = c * 2 + half
                            cols, w = slice(k * P, k * P + P), slice(half * D, half * D + D)
                            last = pe.matmul(v_bank[:, 0, c * D:(c + 1) * D], y_turned[:, cols], o_raw[:, w],
                                             start=half == 0, stop=half == 1)
                    last.then_inc(s["o_done"], 1)

            run_batches(pe, step)

        @block.scalar
        def _(act):
            act.wait_ge(s["weights"], 16 * len(weights))
            act.copy(qk_hi[:, :], qk_raw[:, :]).then_inc(s["high"], 1)

            def high_x(b):
                act.wait_ge(s["x_turned"], b + 1)
                wait_past(act, s["v_done"], CH * b)
                act.copy(x_hi[:, :], turn_bank[:, 0:SEQ]).then_inc(s["x_high"], 1)

            high_x(0)

            def spread_out(spread, source):
                for j in range(4):
                    last = act.mul(spread[:, j, :], source[:, :], t["const"][:, C_HEAD + j:C_HEAD + j + 1])
                return last

            def keep_out(c, b):
                act.wait_ge(s["out_done" if c else "out0_done"], b)
                wait_past(act, s["heads_turned"], (b - 2) * CH + c + 1)
                act.copy(out_turned[:, c, :, :], out_bank[c][:, :, :]).then_inc(s["out_kept"], 1)

            def keep_heads(c, b, p):
                act.wait_ge(s["heads_turned"], (b - 1) * CH + c + 1)
                if c == 0:
                    wait_past(act, s["normed_done"], b - 2)
                act.copy(heads[p][:, c * HEADS:(c + 1) * HEADS, :].rearrange("p h v -> p (h v)"), heads_bank[:, c, :]
                         ).then_inc(s["heads_kept"], 1)

            def square(c, b, p):
                cols = slice(c * HEADS, (c + 1) * HEADS)
                act.wait_ge(s["heads_kept"], CH * (b - 1) + c + 1)
                wait_past(act, s["squares_summed"], CH * (b - 2) + c + 1)
                act.activation(squares[:, cols, :], heads[p][:, cols, :], ACT.Square).then_inc(s["squared"], 1)

            def step(b, like):
                p, q = like % 2, (like + 1) % 2
                if 2 <= like:
                    keep_heads(1, b - 1, p)
                    square(1, b - 1, p)
                if like < BATCH:
                    act.wait_ge(s["q_all_done"], b + 1)
                    wait_past(act, s["scored"], (b - 1) * (CH * GROUPS))
                    act.copy(q_hi[:, :], q_all[:, :]).then_inc(s["q_high"], 1)
                    spread_out(spread_hi[p], q_all)
                    act.wait_ge(s["keys_done"], b + 1)
                    act.copy(keys_hi[p][:, :], keys[p][:, :]).then_inc(s["keys_high"], 1)
                if 1 <= like <= BATCH:
                    keep_out(0, b)
                if like < BATCH:
                    act.wait_ge(s["q_split"], b + 1)
                    spread_out(spread_lo[p], q_lo).then_inc(s["spread_done"], 1)
                if 1 <= like <= BATCH:
                    keep_heads(0, b, q)
                if like >= 2:
                    act.wait_ge(s["y_turned"], b - 1)
                    wait_past(act, s["o_done"], b - 2)
                    act.copy(y_turned[:, :], turn_bank[:, :]).then_inc(s["y_kept"], 1)
                if 1 <= like <= BATCH:
                    square(0, b, q)
                if like + 1 < BATCH:
                    high_x(b + 1)
                if like < BATCH:
                    act.wait_ge(s["g_kept"], CH * (b + 1))
                    wait_past(act, s["gated_done"], b - 1)
                    act.activation(g_act[p][:, :, :], g_raw[p][:, :, :], ACT.Silu).then_inc(s["g_done"], 1)
                if 1 <= like <= BATCH:
                    keep_out(1, b)

            run_batches(act, step)

        @block.vector
        def _(dve):
            chain = Chain(dve, s["chain"])
            row_stats(dve, chain, t["x"], m, 0, x_in[0])
            dve.wait_ge(s["weights"], 16 * len(weights))
            per_head = [v[:, 0:2 * D].rearrange("p (h v) -> p h v", v=VD) for v in (vg_raw, vg_bias)]
            for k, part in enumerate(per_head):
                last = dve.tensor_reduce(value_mean[:, k, :], part, AX.X, ALU.add)
            chain.then(last)
            for k, part in enumerate(per_head):
                last = dve.scalar_tensor_tensor(out=part, in0=value_mean[:, k, :].unsqueeze(2).to_broadcast([P, HEADS, VD]),
                                                scalar=-1.0 / VD, in1=part, op0=ALU.mult, op1=ALU.add)
            chain.then(last)
            chain.then(dve.tensor_copy(vg_hi[:, :], vg_raw[:, :]))
            dve.wait_ge(s["high"], 1)
            for hi, lo, raw in ((qk_hi, qk_lo, qk_raw), (vg_hi, vg_lo, vg_raw)):
                dve.tensor_tensor(lo[:, :], raw[:, :], hi[:, :].bitcast(F32), ALU.subtract).then_inc(s["split"], 1)

            def normalise_batch(b, p):
                wait_past(dve, s["x_turned"], b - 1)
                for c in range(CH):
                    last = normalise(dve, xn[p][:, c, :], t["x"], b * CH + c, m)
                last.then_inc(s["xn_done"], 1)

            def low_x(b):
                dve.wait_ge(s["x_high"], b + 1)
                dve.tensor_tensor(x_lo[:, :], turn_bank[:, 0:SEQ], x_hi[:, :].bitcast(F32), ALU.subtract
                                  ).then_inc(s["x_split"], 1)

            dve.wait_ge(s["zeros_set"], 1)
            dve.wait_ge(m["rstd_done"], 1)
            normalise_batch(0, 0)
            normalise_batch(1, 1)
            low_x(0)
            dve.wait_ge(s["tables"], 16 * len(tables))

            def masks(c, g, b):
                n = (b - 1) * (CH * GROUPS) + c * GROUPS + g
                dve.wait_ge(s["scored"], n + 1)
                if g == 0:
                    wait_past(dve, s["out_done" if c else "out0_done"], b - 1)
                dve.tensor_tensor(probs[:, c, 4 * g:4 * g + 4, :], score_bank[g % 2][:, :, :],
                                  mask[:, 4 * g:4 * g + 4, :], ALU.mult).then_inc(s["masked"], 1)

            def turned(b, first, done, parts):
                dve.wait_ge(done, b + 1)
                for k, to in enumerate(parts):
                    w = first + k
                    last = dve.scalar_tensor_tensor(out=to[:, :], in0=qk_bank[:, k * SEQ:(k + 1) * SEQ],
                                                    scalar=qk_bias[:, w:w + 1], in1=turns[:, w, :],
                                                    op0=ALU.add, op1=ALU.mult)
                last.then_inc(s["parts_done"], 1)

            def keep_values(c, b, p):
                if c == 0:
                    wait_past(dve, s["out_done"], b - 1)
                    wait_past(dve, s["g_done"], b - 1)
                dve.wait_ge(s["v_done"], CH * b + c + 1)
                dve.tensor_tensor(own_columns(values[p], c),
                                  v_bank[:, 0, :].rearrange("p (h j v) -> p h j v", j=2, v=VD),
                                  vg_bias[:, 0:2 * D].rearrange("p (h j v) -> p h j v", j=2, v=VD), ALU.add
                                  ).then_inc(s["v_kept"], 1)
                dve.tensor_tensor(g_raw[p][:, c, :], v_bank[:, 1, :], vg_bias[:, 2 * D:], ALU.add
                                  ).then_inc(s["g_kept"], 1)

            def sum_squares(c, n):
                cols = slice(c * HEADS, (c + 1) * HEADS)
                dve.wait_ge(s["squared"], n)
                dve.tensor_reduce(square_sum[:, cols], squares[:, cols, :], AX.X, ALU.add).then_inc(s["squares_summed"], 1)

            def variance(c, n, p, inverses):
                cols = slice(c * HEADS, (c + 1) * HEADS)
                dve.wait_ge(s["squares_summed"], n)
                dve.wait_ge(s["inverse_squared"], inverses)
                dve.scalar_tensor_tensor(out=square_sum[:, cols], in0=square_sum[:, cols], scalar=1.0 / VD,
                                         in1=inverse2[p][:, cols], op0=ALU.mult, op1=ALU.mult).then_inc(s["var_scaled"], 1)
                dve.wait_ge(s["var_scaled"], n)
                wait_past(dve, s["rstd_done"], n - 2)
                dve.tensor_scalar(o_var[:, cols], square_sum[:, cols], EPS, None, ALU.add).then_inc(s["o_var_done"], 1)

            def step(b, like):
                p, q = like % 2, (like + 1) % 2
                new, mid, old = like < BATCH, 1 <= like <= BATCH, 2 <= like
                if mid:
                    sums = turn_bank[:, P:P + CH * HEADS]
                    dve.wait_ge(s["k_turned"], b)
                    dve.tensor_scalar(bounded[:, :], sums, 1.0, None, ALU.max).then_inc(s["sum_bounded"], 1)
                    wait_past(dve, s["state_done"], b - 1)
                    dve.tensor_tensor(k_dec[:, :], turn_bank[:, 0:P], k_decay[:, :], ALU.mult).then_inc(s["k_dec_done"], 1)
                    dve.wait_ge(s["sum_bounded"], b)
                    dve.scalar_tensor_tensor(out=clipped[:, :], in0=sums, scalar=-1.0, in1=bounded[:, :],
                                             op0=ALU.mult, op1=ALU.max).then_inc(s["sum_clipped"], 1)
                    masks(0, 0, b)
                if old:
                    sum_squares(1, 2 * b - 2)
                if mid:
                    masks(0, 1, b)
                if old:
                    variance(1, 2 * b - 2, p, b - 1)
                if new:
                    turned(b, 0, s["q_done"], (q_part, q_turn))
                if mid:
                    masks(0, 2, b)
                if new:
                    dve.wait_ge(s["parts_done"], 2 * b + 1)
                    wait_past(dve, s["sum_terms_done"], b)
                    wait_past(dve, s["spread_done"], b)
                    dve.tensor_tensor(q_all[:, :], q_part[:, :], q_turn[:, :], ALU.add).then_inc(s["q_all_done"], 1)
                if new:
                    keep_values(0, b, p)
                if mid:
                    masks(0, 3, b)
                if new:
                    turned(b, 2, s["k_done"], (k_part, k_turn))
                if mid:
                    masks(1, 0, b)
                if new:
                    dve.wait_ge(s["parts_done"], 2 * b + 2)
                    wait_past(dve, s["out_done"], b - 1)
                    dve.tensor_tensor(keys[p][:, :], k_part[:, :], k_turn[:, :], ALU.add).then_inc(s["keys_done"], 1)
                if mid:
                    masks(1, 1, b)
                if old:
                    dve.wait_ge(s["factor_done"], b - 1)
                    wait_past(dve, s["gated_done"], b - 2)
                    dve.tensor_tensor(normed[:, :, :], heads[p][:, :, :],
                                      factor[:, :].unsqueeze(2).to_broadcast([P, CH * HEADS, VD]), ALU.mult
                                      ).then_inc(s["normed_done"], 1)
                if mid:
                    dve.wait_ge(s["state_done"], b)
                    dve.tensor_tensor(state[:, :, :].rearrange("p h v -> p (h v)"),
                                      qk_bank[:, 0:HEADS * VD],
                                      own_head[:, :, :].rearrange("p h v -> p (h v)"), ALU.mult
                                      ).then_inc(s["state_kept"], 1)
                    masks(1, 2, b)
                    dve.wait_ge(s["sum_clipped"], b)
                    wait_past(dve, s["factor_done"], b - 2)
                    dve.reciprocal(inverse[q][:, :], clipped[:, :]).then_inc(s["sum_inverted"], 1)
                if old:
                    dve.wait_ge(s["normed_done"], b - 1)
                    dve.wait_ge(s["g_done"], b - 1)
                    wait_past(dve, s["y_turned"], b - 2)
                    dve.tensor_tensor(gated[:, :, :].rearrange("p h v -> p (h v)"),
                                      normed[:, :, :].rearrange("p h v -> p (h v)"),
                                      g_act[p][:, :, :].rearrange("p c n -> p (c n)"), ALU.mult
                                      ).then_inc(s["gated_done"], 1)
                if mid:
                    dve.wait_ge(s["sum_inverted"], b)
                    dve.tensor_tensor(inverse2[q][:, :], inverse[q][:, :], inverse[q][:, :], ALU.mult
                                      ).then_inc(s["inverse_squared"], 1)
                    masks(1, 3, b)
                if new:
                    keep_values(1, b, p)
                if new:
                    dve.wait_ge(s["keys_done"], b + 1)
                    wait_past(dve, s["sum_terms_done"], b)
                    dve.tensor_tensor_scan(key_sums[:, :], decays[:, :], keys[p][:, :], 0.0, ALU.mult, ALU.add
                                           ).then_inc(s["key_sums_done"], 1)
                if like + 2 < BATCH:
                    if like in (2, 3):
                        dve.wait_ge(m["rstd_done"], 2 * like - 2)
                    normalise_batch(b + 2, p)
                if like < 3:
                    row_stats(dve, chain, t["x"], m, like + 1, x_in[like + 1])
                if like + 1 < BATCH:
                    low_x(b + 1)
                if mid:
                    sum_squares(0, 2 * b - 1)
                    variance(0, 2 * b - 1, q, b)
                if old:
                    dve.wait_ge(s["o_done"], b - 1)
                    dve.wait_ge(s["x_plus_done"], b - 1)
                    dve.tensor_tensor(t["x"][:, bass.ds((b - 2) * CH, CH), :], v_bank[:, 0, :].rearrange("p (c d) -> p c d", c=CH),
                                      x_plus[p][:, :, :], ALU.add).then_inc(s["added"], 1)

            run_batches(dve, step)


def program(nc, a, out):
    with ExitStack() as ctx:
        def sb(name, shape, dt=F32):
            return ctx.enter_context(nc.sbuf_tensor(name, shape, dt))

        def sem(name):
            return ctx.enter_context(nc.semaphore(name))

        t = dict(
            x=sb("x", [P, TILES, D]), padding=sb("padding", [P, UT, ROW]), ident=sb("ident", [P, P]), earlier=sb("earlier", [P, P]),
            ones=sb("ones", [P, 2 * HEADS]), const=sb("const", [P, C_COLS]), n_tables=3,
            power=sb("power", [P, TILES // 4]),
            x_loaded=[sem(f"x_loaded{q}") for q in range(4)], tables_loaded=sem("tables_loaded"),
            scattered=[nc.dram_tensor(f"scattered{f}", (PAD_UNIT + UNIT, ROW), F32, kind="Internal").ap()
                       for f in range(2)],
            experts=a["experts"], router_w=a["router_w"], router_b=a["router_b"], a=a)
        middle = nc.dram_tensor("middle", (DST_ROWS, D), F32, kind="Internal").ap()
        padding = t["padding"]
        with nc.Block() as block:
            @block.sync
            def _(sp):
                sp.dma_start(t["ident"][:, :], a["ident"]).then_inc(t["tables_loaded"], 16)
                sp.dma_start(t["earlier"][:, :], a["earlier"]).then_inc(t["tables_loaded"], 16)
                sp.dma_start(t["const"][:, :], a["const"]).then_inc(t["tables_loaded"], 16)
                n = TILES // 4
                for q in range(4):
                    sp.dma_start(t["x"][:, q * n:q * n + n, :], a["x"][q * n * P:(q + 1) * n * P, :]
                                 .rearrange("(t p) d -> p t d", p=P)).then_inc(t["x_loaded"][q], 16)

            @block.vector
            def _(dve):
                dve.memset(padding[:, :, 0:D + 1], 0.0)
                dve.wait_ge(t["tables_loaded"], 16 * t["n_tables"])
                dve.tensor_scalar(padding[:, :, D + 1], t["const"][:, C_ID:C_ID + UT], float(TOKENS), None, ALU.add)
                dve.memset(t["ones"][:, :], 1.0)
                dve.memset(t["power"][:, :], -0.5)

        moe(nc, t, 0, middle)
        retention(nc, t, middle)
        moe(nc, t, 1, out)


def tables():
    import numpy as np

    p = np.arange(P)
    const = np.zeros((P, C_COLS), np.float32)
    const[:, C_ID:C_ID + TILES] = p[:, None] + P * np.arange(TILES)
    const[:, C_REV:C_REV + EXPERTS] = EXPERTS - np.arange(EXPERTS)
    const[:, C_STEP:C_STEP + EXPERTS] = UNIT * np.arange(EXPERTS)
    const[:, C_REGION:C_REGION + EXPERTS] = REGION * np.arange(EXPERTS)
    const[:, C_UNIT:C_UNIT + ROUTED_UNITS] = np.arange(ROUTED_UNITS)
    const[:, C_HEAD:C_HEAD + 4] = (p[:, None] % 32) // KD == np.arange(4)
    head = np.arange(HEADS)
    angle = np.repeat((1.0 / 10000.0 ** np.linspace(0.0, 1.0, KD // 2, dtype=np.float32)).astype(np.float32), 2)
    at = np.arange(SEQ, dtype=np.float32)
    sin, cos = np.sin(at[None, :] * angle[:, None]), np.cos(at[None, :] * angle[:, None])
    sin = sin * np.where(np.arange(KD) % 2 == 0, -1.0, 1.0)[:, None]
    scaling = KD ** -0.5
    decay = np.log(1.0 - 2.0 ** (-5.0 - head))
    apart = np.arange(SEQ)[:, None] - np.arange(SEQ)[None, :]
    full = np.where(apart >= 0, np.exp(decay[:, None, None] * apart), 0.0)
    norm = np.repeat(1.0 / np.sqrt(full.sum(-1)), KD, axis=0)
    turns = np.tile(cos, (HEADS, 1)), np.tile(sin, (HEADS, 1))
    turns = np.stack([turns[0] * norm, turns[1] * norm, turns[0] * scaling, turns[1] * scaling], axis=1)
    mask = full[:, 0:P, 0:P].transpose(2, 0, 1)
    of_row = p // KD
    q_decay = np.exp(decay[of_row][:, None] * p[None, :])
    k_decay = np.exp(decay[of_row][None, :] * (P - p[:, None]))
    head_of = of_row[:, None] == head[None, :]
    out = {"turns": turns, "mask": mask, "q_decay": q_decay, "k_decay": k_decay, "head_of": head_of,
           "own_head": np.repeat(head_of[:, :, None], VD, axis=2),
           "decays": np.broadcast_to(np.exp(decay[of_row])[:, None], (P, SEQ))}
    out = {k: v.astype(np.float32) for k, v in out.items()} | {"ident": np.eye(P, dtype=np.float32), "earlier": (p[:, None] < p[None, :]).astype(np.float32),
           "const": const}
    return out


def kernel(**inputs):
    import numpy as np
    import concourse.bacc as bacc
    from concourse.bass_utils import run_bass_kernel_spmd as run

    i = {k.replace("L0_", ""): np.asarray(v) for k, v in inputs.items()}

    def expert_rows(w1, b1, w2, b2):
        return np.concatenate([w2.T.reshape(CHUNKS, P, D).transpose(1, 0, 2).reshape(P, FF), w1.T,
                               b1.reshape(CHUNKS, P).T, b2[:, None]], axis=1)

    experts = [expert_rows(i["ffn_spec_w1"][e], i["ffn_spec_b1"][e], i["ffn_spec_w2"][e], i["ffn_spec_b2"][e])
               for e in range(EXPERTS)]
    experts.append(expert_rows(i["ffn_shared_w1"], i["ffn_shared_b1"], i["ffn_shared_w2"], i["ffn_shared_b2"]))
    swap = np.arange(D) ^ 1
    arrays = {
        "x": i["attn_x"].reshape(TOKENS, D),
        "experts": np.stack(experts),
        "router_w": i["ffn_router_w"].T,
        "router_b": np.broadcast_to(i["ffn_router_b"], (P, EXPERTS)),
        "w_qk": np.concatenate([i["attn_Wq"], i["attn_Wq"][:, swap], i["attn_Wk"], i["attn_Wk"][:, swap]], axis=1),
        "b_qk": np.stack([i["attn_bq"], i["attn_bq"][swap], i["attn_bk"], i["attn_bk"][swap]], axis=1),
        "w_vg": np.concatenate([i["attn_Wv"], i["attn_Wg"]], axis=1),
        "b_vg": np.broadcast_to(np.concatenate([i["attn_bv"], i["attn_bg"]]), (P, 4 * D)),
        "w_o": i["attn_Wo"].reshape(2, P, D).transpose(1, 0, 2).reshape(P, 2 * D),
        "b_o": np.broadcast_to(i["attn_bo"], (P, D)),
        **tables(),
    }
    nc = bacc.Bacc("TRN2", target_bir_lowering=False, num_devices=1)
    arrays = {f"in_{k}": np.ascontiguousarray(v) for k, v in arrays.items()}
    a = {k[3:]: nc.dram_tensor(k, v.shape, mybir.dt.from_np(v.dtype), kind="ExternalInput").ap()
         for k, v in arrays.items()}
    out = nc.dram_tensor("out", (DST_ROWS, D), F32, kind="ExternalOutput").ap()
    program(nc, a, out)
    result = run(nc, [arrays], core_ids=[0])
    return result.results[0]["out"][:TOKENS].reshape(BATCH, SEQ, D)
```
